# Optimizing a Trainium2 kernel written in Bass

```python
import numpy as np
import jax
import jax.numpy as jnp

def _softmax(x, axis=-1):
    return jax.nn.softmax(x, axis=axis)

def _gelu(x):
    return jax.nn.gelu(x, approximate=True)

def _silu(x):
    return jax.nn.silu(x)

def _sigmoid(x):
    return jax.nn.sigmoid(x)

def _layernorm(x, axis=-1, eps=1e-05):
    m = jnp.mean(x, axis=axis, keepdims=True)
    v = jnp.var(x, axis=axis, keepdims=True)
    return (x - m) / jnp.sqrt(v + eps)

def _scatter_add(tgt, idx, src, axis=0):
    return tgt.at[idx].add(src)

def _segment_sum(src, seg, n):
    return jax.ops.segment_sum(src, seg, n)
kernel_name = 'mk_seq_postln_d4_jaxref_r8_fc1d3a'

def setup_inputs(seed: int=0):
    np.random.seed(seed)
    _w = jnp.asarray

    def _L0_attn_setup():
        import jax, jax.numpy as jnp
        import numpy as np
        B, T, C = (4, 512, 128)
        H = 16
        LS = 32
        EPS = 1e-06

        def rmsnorm(x, w):
            xf = x.astype(jnp.float32)
            y = xf * jax.lax.rsqrt(jnp.mean(xf * xf, axis=-1, keepdims=True) + EPS)
            return y.astype(x.dtype) * w
        key = jax.random.key(seed)
        k1, k2, k3 = jax.random.split(key, 3)
        x = jax.random.normal(k1, (B, T, C), dtype=jnp.float32)
        w_qkv = jax.random.normal(k2, (C, 3 * C), dtype=jnp.float32) * (1.0 / np.sqrt(C))
        ln_w = jnp.ones((C,), dtype=jnp.float32)
        w_proj = jax.random.normal(k3, (C, C), dtype=jnp.float32) * (1.0 / np.sqrt(C))
        return {'x': x, 'w_qkv': w_qkv, 'ln_w': ln_w, 'w_proj': w_proj}
    _L0_attn_in = _L0_attn_setup()

    def _L0_ffn_setup():
        import jax, jax.numpy as jnp
        import numpy as np
        B, S, H = (1, 256, 128)
        E, K = (16, 4)
        G, TG = (4, 2)
        I_MOE = 64
        N_SH = 2
        SCALE = 2.5

        def _mlp(x, gw, uw, dw):
            return jax.nn.silu(x @ gw.T) * (x @ uw.T) @ dw.T

        def _route(x2d, router_weight, e_bias):
            T = x2d.shape[0]
            scores = jax.nn.sigmoid(x2d @ router_weight.T)
            sc = scores + e_bias[None, :]
            group_scores = jnp.sum(jax.lax.top_k(sc.reshape(T, G, E // G), 2)[0], axis=-1)
            _, gidx = jax.lax.top_k(group_scores, TG)
            gmask = jnp.zeros((T, G), sc.dtype).at[jnp.arange(T)[:, None], gidx].set(1.0)
            smask = jnp.repeat(gmask, E // G, axis=1)
            masked = jnp.where(smask > 0, sc, 0.0)
            _, tidx = jax.lax.top_k(masked, K)
            tw = jnp.take_along_axis(scores, tidx, axis=1)
            tw = tw / (jnp.sum(tw, axis=-1, keepdims=True) + 1e-20)
            tw = tw * SCALE
            return (tidx, tw)

        def _moe_forward(hidden_states, router_weight, e_bias, gate_w, up_w, down_w, sh_gate_w, sh_up_w, sh_down_w):
            orig_shape = hidden_states.shape
            x = hidden_states.reshape(-1, H)
            T = x.shape[0]
            tidx, tw = _route(x, router_weight, e_bias)
            g = jnp.einsum('th,eih->tei', x, gate_w)
            u = jnp.einsum('th,eih->tei', x, up_w)
            h = jax.nn.silu(g) * u
            yo = jnp.einsum('tei,ehi->teh', h, down_w)
            combine = jnp.zeros((T, E), tw.dtype).at[jnp.arange(T)[:, None], tidx].add(tw)
            routed = jnp.einsum('te,teh->th', combine, yo)
            shared = _mlp(hidden_states.reshape(-1, H), sh_gate_w, sh_up_w, sh_down_w)
            return (routed + shared).reshape(orig_shape)
        key = jax.random.key(seed)
        ks = jax.random.split(key, 9)
        s = 0.02
        return {'hidden_states': jax.random.normal(ks[0], (B, S, H), jnp.float32), 'router_weight': jax.random.normal(ks[1], (E, H), jnp.float32) * s, 'e_bias': jnp.zeros((E,), jnp.float32), 'gate_w': jax.random.normal(ks[2], (E, I_MOE, H), jnp.float32) * s, 'up_w': jax.random.normal(ks[3], (E, I_MOE, H), jnp.float32) * s, 'down_w': jax.random.normal(ks[4], (E, H, I_MOE), jnp.float32) * s, 'sh_gate_w': jax.random.normal(ks[5], (N_SH * I_MOE, H), jnp.float32) * s, 'sh_up_w': jax.random.normal(ks[6], (N_SH * I_MOE, H), jnp.float32) * s, 'sh_down_w': jax.random.normal(ks[7], (H, N_SH * I_MOE), jnp.float32) * s}
    _L0_ffn_in = _L0_ffn_setup()

    def _L1_attn_setup():
        import jax, jax.numpy as jnp
        import numpy as np
        import itertools
        B, T, C, H = (2, 256, 128, 8)
        HD = C // H

        def _head_dirs():
            signs = [-1.0, 1.0]
            tri = np.array(list(itertools.product(signs, repeat=3)), dtype=np.float32)
            tri = tri / np.linalg.norm(tri, axis=1, keepdims=True)
            return jnp.asarray(tri[:H])
        key = jax.random.key(seed)
        ks = jax.random.split(key, 5)
        w = lambda k, sh: jax.random.normal(k, sh, dtype=jnp.float32) * 0.02
        return {'x': jax.random.normal(ks[0], (B, T, C), dtype=jnp.float32), 'Wq': w(ks[1], (H * 3, C)), 'Wk': w(ks[2], (H * 3, C)), 'Wv': w(ks[3], (C, C)), 'Wo': w(ks[4], (C, C)), 'scale': jnp.asarray(1.0 / np.sqrt(3.0), dtype=jnp.float32)}
    _L1_attn_in = _L1_attn_setup()

    def _L1_ffn_setup():
        import jax, jax.numpy as jnp
        import numpy as np
        N_EXP = 8
        TOP_K = 2
        CAP_FACTOR = 1.25
        NEG_INF = -1000000000.0

        def _moe_forward(x, w_g, c_fc, c_proj):
            B, T, D = x.shape
            N = B * T
            xf = x.reshape(N, D)
            logits = xf @ w_g
            topv, topi = jax.lax.top_k(logits, TOP_K)
            full = jnp.full_like(logits, NEG_INF)
            full = full.at[jnp.arange(N)[:, None], topi].set(topv)
            probs = jax.nn.softmax(full, axis=-1)
            capacity = int(TOP_K * CAP_FACTOR * N / N_EXP)
            capacity += capacity % 2
            mask = jax.nn.one_hot(jnp.swapaxes(topi, 0, 1), N_EXP, dtype=jnp.int32)
            rank = jnp.cumsum(mask.reshape(TOP_K * N, N_EXP), axis=0).reshape(TOP_K, N, N_EXP) - 1
            mask = mask * (rank < capacity)
            rank_sel = jnp.sum(mask * rank, axis=-1)
            wts = jnp.sum(mask * probs[None], axis=-1)
            cb = jnp.zeros((N, N_EXP, capacity), x.dtype)
            tok = jnp.arange(N)
            for k in range(TOP_K):
                cb = cb.at[tok, topi[:, k], rank_sel[k]].add(wts[k])
            sec_mask = (cb != 0).astype(x.dtype)
            exp_batches = jnp.einsum('nec,nd->ecd', sec_mask, xf)
            h = jax.nn.gelu(jnp.einsum('ecd,edh->ech', exp_batches, c_fc), approximate=False)
            exp_out = jnp.einsum('ech,ehd->ecd', h, c_proj)
            out = jnp.einsum('nec,ecd->nd', cb, exp_out)
            return out.reshape(B, T, D)
        key = jax.random.key(seed)
        k1, k2, k3, k4 = jax.random.split(key, 4)
        B, T, D = (4, 64, 128)
        H = 4 * D
        x = jax.random.normal(k1, (B, T, D), jnp.float32)
        w_g = jax.random.normal(k2, (D, N_EXP), jnp.float32) * 0.02
        c_fc = jax.random.normal(k3, (N_EXP, D, H), jnp.float32) * 0.02
        c_proj = jax.random.normal(k4, (N_EXP, H, D), jnp.float32) * 0.02
        return {'x': x, 'w_g': w_g, 'c_fc': c_fc, 'c_proj': c_proj}
    _L1_ffn_in = _L1_ffn_setup()

    def _L2_attn_setup():
        import jax, jax.numpy as jnp
        import numpy as np
        INF_APPROX = 1e+30
        ROTARY_BASE = 10000.0
        D_HEAD = 128

        def _rope(x, base=ROTARY_BASE):
            _, length, _, width = x.shape
            half = width // 2
            positions = jnp.arange(length, dtype=x.dtype)
            dims = jnp.arange(half, dtype=x.dtype)
            ang_freqs = jnp.power(base, -dims / half)
            radians = positions[:, None] * ang_freqs[None, :]
            cos = jnp.cos(radians)[None, :, None, :]
            sin = jnp.sin(radians)[None, :, None, :]
            even, odd = jnp.split(x, 2, axis=-1)
            return jnp.concatenate([even * cos - odd * sin, even * sin + odd * cos], axis=-1)
        key = jax.random.key(seed)
        k1, k2, k3, k4, k5 = jax.random.split(key, 5)
        B, T, M, H, D = (2, 512, 128, 8, 128)
        n_layer = 24
        x = jax.random.normal(k1, (B, T, M), dtype=jnp.float32)
        std_qkv = M ** (-0.5)
        std_o = (M * 2 * n_layer) ** (-0.5)
        w_aq = jnp.zeros((M, H, D), dtype=jnp.float32)
        w_ak = std_qkv * jax.random.normal(k3, (M, H, D), dtype=jnp.float32)
        w_av = std_qkv * jax.random.normal(k4, (M, H, D), dtype=jnp.float32)
        w_ao = std_o * jax.random.normal(k5, (H, D, M), dtype=jnp.float32)
        return {'x': x, 'w_aq': w_aq, 'w_ak': w_ak, 'w_av': w_av, 'w_ao': w_ao}
    _L2_attn_in = _L2_attn_setup()

    def _L2_ffn_setup():
        import jax, jax.numpy as jnp
        import numpy as np
        B, S, D = (2, 128, 128)
        H, HD = (16, 64)
        E_R = 31
        K_ACT = 3
        INTER = 128
        EPS = 1e-05
        BASE = 10000.0

        def _rmsnorm(x, gamma):
            rms = jnp.sqrt(jnp.mean(x * x, axis=-1, keepdims=True) + EPS)
            return x / rms * gamma

        def _rope(x, theta):
            seq = x.shape[2]
            angles = jnp.arange(seq, dtype=theta.dtype)[:, None] * theta
            cos = jnp.cos(angles)[None, None]
            sin = jnp.sin(angles)[None, None]
            x1, x2 = (x[..., 0::2], x[..., 1::2])
            return jnp.concatenate([x1 * cos - x2 * sin, x1 * sin + x2 * cos], axis=-1)

        def _forward(x, theta, gamma1, gamma2, q_w, q_b, k_w, k_b, v_w, v_b, o_w, o_b, router_w, router_b, sh_w1, sh_b1, sh_w2, sh_b2, re_w1, re_b1, re_w2, re_b2):
            b, s, d = x.shape
            xn = _rmsnorm(x, gamma1)
            q = (xn @ q_w + q_b).reshape(b, s, H, HD).transpose(0, 2, 1, 3)
            k = (xn @ k_w + k_b).reshape(b, s, H, HD).transpose(0, 2, 1, 3)
            v = (xn @ v_w + v_b).reshape(b, s, H, HD).transpose(0, 2, 1, 3)
            q = _rope(q, theta)
            k = _rope(k, theta)
            scale = 1.0 / np.sqrt(HD)
            scores = jnp.einsum('bhqd,bhkd->bhqk', q, k) * scale
            causal = jnp.tril(jnp.ones((s, s), dtype=bool))
            scores = jnp.where(causal, scores, -jnp.inf)
            attn = jax.nn.softmax(scores, axis=-1)
            ctx = jnp.einsum('bhqk,bhkd->bhqd', attn, v)
            ctx = ctx.transpose(0, 2, 1, 3).reshape(b, s, H * HD)
            attn_out = ctx @ o_w + o_b + xn
            an = _rmsnorm(attn_out, gamma2)
            shared = jax.nn.gelu(an @ sh_w1 + sh_b1, approximate=False) @ sh_w2 + sh_b2
            logits = an @ router_w + router_b
            aff = jax.nn.softmax(logits, axis=-1)
            topv, topi = jax.lax.top_k(aff, K_ACT)
            gates = jnp.sum(jax.nn.one_hot(topi, E_R, dtype=aff.dtype) * topv[..., None], axis=-2)
            h = jax.nn.gelu(jnp.einsum('bsd,edh->besh', an, re_w1) + re_b1[None, :, None, :], approximate=False)
            routed = jnp.einsum('bse,besh,ehd->bsd', gates, h, re_w2) + jnp.einsum('bse,ed->bsd', gates, re_b2)
            return shared + routed + an + attn_out
        key = jax.random.key(seed)
        ks = jax.random.split(key, 24)
        s = 0.02
        theta = BASE ** (-jnp.arange(HD // 2, dtype=jnp.float32) * 2.0 / HD)
        inp = {'x': jax.random.normal(ks[0], (B, S, D), jnp.float32), 'positions': jnp.arange(S, dtype=jnp.int32), 'theta': theta, 'gamma1': jnp.ones((D,), jnp.float32), 'gamma2': jnp.ones((D,), jnp.float32), 'q_w': jax.random.normal(ks[1], (D, H * HD), jnp.float32) * s, 'q_b': jnp.zeros((H * HD,), jnp.float32), 'k_w': jax.random.normal(ks[2], (D, H * HD), jnp.float32) * s, 'k_b': jnp.zeros((H * HD,), jnp.float32), 'v_w': jax.random.normal(ks[3], (D, H * HD), jnp.float32) * s, 'v_b': jnp.zeros((H * HD,), jnp.float32), 'o_w': jax.random.normal(ks[4], (H * HD, D), jnp.float32) * s, 'o_b': jnp.zeros((D,), jnp.float32), 'router_w': jax.random.normal(ks[5], (D, E_R), jnp.float32) * s, 'router_b': jnp.zeros((E_R,), jnp.float32), 'sh_w1': jax.random.normal(ks[6], (D, INTER), jnp.float32) * s, 'sh_b1': jnp.zeros((INTER,), jnp.float32), 'sh_w2': jax.random.normal(ks[7], (INTER, D), jnp.float32) * s, 'sh_b2': jnp.zeros((D,), jnp.float32), 're_w1': jax.random.normal(ks[8], (E_R, D, INTER), jnp.float32) * s, 're_b1': jnp.zeros((E_R, INTER), jnp.float32), 're_w2': jax.random.normal(ks[9], (E_R, INTER, D), jnp.float32) * s, 're_b2': jnp.zeros((E_R, D), jnp.float32)}
        return inp
    _L2_ffn_in = _L2_ffn_setup()

    def _L3_attn_setup():
        import jax, jax.numpy as jnp
        import numpy as np
        from jax import lax
        DIM = 128
        EXP = 2
        GMLP_EXP = 2
        K = 4
        HID = DIM * EXP
        GHID = DIM * GMLP_EXP
        ALPHA_LOG_SCALE = -8.0

        def init_forget_gate(size, a=0.001, b=0.1, lo=-9.0, hi=-4.323):
            x = np.log(np.expm1(np.linspace(a, b, size, dtype=np.float64)))
            x = (x - x.min()) / (x.max() - x.min())
            x = x * abs(hi - lo) + lo
            return jnp.asarray(x, dtype=jnp.float32)

        def _rmsnorm(x, gamma):
            n = jnp.sqrt(jnp.sum(x * x, axis=-1, keepdims=True))
            return gamma * jnp.sqrt(jnp.float32(x.shape[-1])) * (x / n)

        def _linear_recurrence(alpha, x):

            def combine(e1, e2):
                a1, b1 = e1
                a2, b2 = e2
                return (a1 * a2, a2 * b1 + b2)
            _, h = lax.associative_scan(combine, (alpha, x), axis=1)
            return h

        def _hawk_block(x, W_in, conv_w, conv_b, W_gates, b_gates, forget_base, W_out, gamma1, gamma2, W_grow, W_shrink):
            B, T, _ = x.shape
            xn = _rmsnorm(x, gamma1)
            z = xn @ W_in.T
            gate, xc = (z[..., :HID], z[..., HID:])
            xc_t = jnp.pad(xc.transpose(0, 2, 1), ((0, 0), (0, 0), (K - 1, 0)))
            xc = lax.conv_general_dilated(xc_t, conv_w, window_strides=(1,), padding='VALID', dimension_numbers=('NCH', 'OIH', 'NCH'), feature_group_count=HID)
            xc = (xc + conv_b[None, :, None]).transpose(0, 2, 1)
            g = xc @ W_gates.T + b_gates
            forget, inp = (g[..., :HID], g[..., HID:])
            alpha = jnp.exp(ALPHA_LOG_SCALE * jax.nn.softplus(forget_base) * jax.nn.sigmoid(forget))
            beta = jnp.sqrt(1.0 - alpha ** 2 + 1e-06)
            xs = beta * jax.nn.sigmoid(inp) * xc
            h = _linear_recurrence(alpha, xs)
            rglru_out = jax.nn.gelu(gate, approximate=False) * h @ W_out.T
            x = x + rglru_out
            xn2 = _rmsnorm(x, gamma2)
            gz = xn2 @ W_grow.T
            mgate, mx = (gz[..., :GHID], gz[..., GHID:])
            mlp_out = jax.nn.gelu(mgate, approximate=False) * mx @ W_shrink.T
            return x + mlp_out
        key = jax.random.key(seed)
        ks = jax.random.split(key, 10)
        B, T = (4, 256)
        x = jax.random.normal(ks[0], (B, T, DIM), dtype=jnp.float32)
        W_in = jax.random.normal(ks[1], (2 * HID, DIM), dtype=jnp.float32) * DIM ** (-0.5)
        conv_w = jax.random.normal(ks[2], (HID, 1, K), dtype=jnp.float32) * (1.0 / K) ** 0.5
        conv_b = jnp.zeros((HID,), dtype=jnp.float32)
        W_gates = jax.random.normal(ks[3], (2 * HID, HID), dtype=jnp.float32) * HID ** (-0.5)
        b_gates = jnp.zeros((2 * HID,), dtype=jnp.float32)
        forget_base = init_forget_gate(HID)
        W_out = jax.random.normal(ks[4], (DIM, HID), dtype=jnp.float32) * HID ** (-0.5)
        gamma1 = jnp.ones((DIM,), dtype=jnp.float32)
        gamma2 = jnp.ones((DIM,), dtype=jnp.float32)
        W_grow = jax.random.normal(ks[5], (2 * GHID, DIM), dtype=jnp.float32) * DIM ** (-0.5)
        W_shrink = jax.random.normal(ks[6], (DIM, GHID), dtype=jnp.float32) * GHID ** (-0.5)
        return {'x': x, 'W_in': W_in, 'conv_w': conv_w, 'conv_b': conv_b, 'W_gates': W_gates, 'b_gates': b_gates, 'forget_base': forget_base, 'W_out': W_out, 'gamma1': gamma1, 'gamma2': gamma2, 'W_grow': W_grow, 'W_shrink': W_shrink}
    _L3_attn_in = _L3_attn_setup()

    def _L3_ffn_setup():
        import jax, jax.numpy as jnp
        import numpy as np
        B, L, D, H, E, K = (4, 256, 128, 256, 8, 2)

        def _mlp(x, w1, b1, w2, b2):
            h = jax.nn.gelu(x @ w1 + b1, approximate=True)
            return h @ w2 + b2
        key = jax.random.key(seed)
        ks = jax.random.split(key, 16)
        s = 0.02
        inp = {'x': jax.random.normal(ks[0], (B, L, D), dtype=jnp.float32), 'task_ids': jax.random.randint(ks[1], (B,), 0, 9), 'gw1': jax.random.normal(ks[2], (D, H), dtype=jnp.float32) * s, 'gb1': jnp.zeros((H,), dtype=jnp.float32), 'gw2': jax.random.normal(ks[3], (H, E), dtype=jnp.float32) * s, 'gb2': jnp.zeros((E,), dtype=jnp.float32), 'We1': jax.random.normal(ks[4], (E, D, H), dtype=jnp.float32) * s, 'be1': jnp.zeros((E, H), dtype=jnp.float32), 'We2': jax.random.normal(ks[5], (E, H, D), dtype=jnp.float32) * s, 'be2': jnp.zeros((E, D), dtype=jnp.float32), 'Ws1': jax.random.normal(ks[6], (D, H), dtype=jnp.float32) * s, 'bs1': jnp.zeros((H,), dtype=jnp.float32), 'Ws2': jax.random.normal(ks[7], (H, D), dtype=jnp.float32) * s, 'bs2': jnp.zeros((D,), dtype=jnp.float32)}
        return inp
    _L3_ffn_in = _L3_ffn_setup()
    _d = {'L0_attn_x': _L0_attn_in['x'], 'L0_attn_w_qkv': _L0_attn_in['w_qkv'], 'L0_attn_ln_w': _L0_attn_in['ln_w'], 'L0_attn_w_proj': _L0_attn_in['w_proj'], 'L0_ffn_router_weight': _L0_ffn_in['router_weight'], 'L0_ffn_e_bias': _L0_ffn_in['e_bias'], 'L0_ffn_gate_w': _L0_ffn_in['gate_w'], 'L0_ffn_up_w': _L0_ffn_in['up_w'], 'L0_ffn_down_w': _L0_ffn_in['down_w'], 'L0_ffn_sh_gate_w': _L0_ffn_in['sh_gate_w'], 'L0_ffn_sh_up_w': _L0_ffn_in['sh_up_w'], 'L0_ffn_sh_down_w': _L0_ffn_in['sh_down_w'], 'L1_attn_Wq': _L1_attn_in['Wq'], 'L1_attn_Wk': _L1_attn_in['Wk'], 'L1_attn_Wv': _L1_attn_in['Wv'], 'L1_attn_Wo': _L1_attn_in['Wo'], 'L1_attn_scale': _L1_attn_in['scale'], 'L1_ffn_w_g': _L1_ffn_in['w_g'], 'L1_ffn_c_fc': _L1_ffn_in['c_fc'], 'L1_ffn_c_proj': _L1_ffn_in['c_proj'], 'L2_attn_w_aq': _L2_attn_in['w_aq'], 'L2_attn_w_ak': _L2_attn_in['w_ak'], 'L2_attn_w_av': _L2_attn_in['w_av'], 'L2_attn_w_ao': _L2_attn_in['w_ao'], 'L2_ffn_positions': _L2_ffn_in['positions'], 'L2_ffn_theta': _L2_ffn_in['theta'], 'L2_ffn_gamma1': _L2_ffn_in['gamma1'], 'L2_ffn_gamma2': _L2_ffn_in['gamma2'], 'L2_ffn_q_w': _L2_ffn_in['q_w'], 'L2_ffn_q_b': _L2_ffn_in['q_b'], 'L2_ffn_k_w': _L2_ffn_in['k_w'], 'L2_ffn_k_b': _L2_ffn_in['k_b'], 'L2_ffn_v_w': _L2_ffn_in['v_w'], 'L2_ffn_v_b': _L2_ffn_in['v_b'], 'L2_ffn_o_w': _L2_ffn_in['o_w'], 'L2_ffn_o_b': _L2_ffn_in['o_b'], 'L2_ffn_router_w': _L2_ffn_in['router_w'], 'L2_ffn_router_b': _L2_ffn_in['router_b'], 'L2_ffn_sh_w1': _L2_ffn_in['sh_w1'], 'L2_ffn_sh_b1': _L2_ffn_in['sh_b1'], 'L2_ffn_sh_w2': _L2_ffn_in['sh_w2'], 'L2_ffn_sh_b2': _L2_ffn_in['sh_b2'], 'L2_ffn_re_w1': _L2_ffn_in['re_w1'], 'L2_ffn_re_b1': _L2_ffn_in['re_b1'], 'L2_ffn_re_w2': _L2_ffn_in['re_w2'], 'L2_ffn_re_b2': _L2_ffn_in['re_b2'], 'L3_attn_W_in': _L3_attn_in['W_in'], 'L3_attn_conv_w': _L3_attn_in['conv_w'], 'L3_attn_conv_b': _L3_attn_in['conv_b'], 'L3_attn_W_gates': _L3_attn_in['W_gates'], 'L3_attn_b_gates': _L3_attn_in['b_gates'], 'L3_attn_forget_base': _L3_attn_in['forget_base'], 'L3_attn_W_out': _L3_attn_in['W_out'], 'L3_attn_gamma1': _L3_attn_in['gamma1'], 'L3_attn_gamma2': _L3_attn_in['gamma2'], 'L3_attn_W_grow': _L3_attn_in['W_grow'], 'L3_attn_W_shrink': _L3_attn_in['W_shrink'], 'L3_ffn_task_ids': _L3_ffn_in['task_ids'], 'L3_ffn_gw1': _L3_ffn_in['gw1'], 'L3_ffn_gb1': _L3_ffn_in['gb1'], 'L3_ffn_gw2': _L3_ffn_in['gw2'], 'L3_ffn_gb2': _L3_ffn_in['gb2'], 'L3_ffn_We1': _L3_ffn_in['We1'], 'L3_ffn_be1': _L3_ffn_in['be1'], 'L3_ffn_We2': _L3_ffn_in['We2'], 'L3_ffn_be2': _L3_ffn_in['be2'], 'L3_ffn_Ws1': _L3_ffn_in['Ws1'], 'L3_ffn_bs1': _L3_ffn_in['bs1'], 'L3_ffn_Ws2': _L3_ffn_in['Ws2'], 'L3_ffn_bs2': _L3_ffn_in['bs2']}
    _x0 = _d['L0_attn_x']
    _d['L0_attn_x'] = jax.random.normal(jax.random.fold_in(jax.random.key(seed), 1), (4, 512, 128), dtype=_x0.dtype)
    del _x0
    return _d

def reference(L0_attn_x, L0_attn_w_qkv, L0_attn_ln_w, L0_attn_w_proj, L0_ffn_router_weight, L0_ffn_e_bias, L0_ffn_gate_w, L0_ffn_up_w, L0_ffn_down_w, L0_ffn_sh_gate_w, L0_ffn_sh_up_w, L0_ffn_sh_down_w, L1_attn_Wq, L1_attn_Wk, L1_attn_Wv, L1_attn_Wo, L1_attn_scale, L1_ffn_w_g, L1_ffn_c_fc, L1_ffn_c_proj, L2_attn_w_aq, L2_attn_w_ak, L2_attn_w_av, L2_attn_w_ao, L2_ffn_positions, L2_ffn_theta, L2_ffn_gamma1, L2_ffn_gamma2, L2_ffn_q_w, L2_ffn_q_b, L2_ffn_k_w, L2_ffn_k_b, L2_ffn_v_w, L2_ffn_v_b, L2_ffn_o_w, L2_ffn_o_b, L2_ffn_router_w, L2_ffn_router_b, L2_ffn_sh_w1, L2_ffn_sh_b1, L2_ffn_sh_w2, L2_ffn_sh_b2, L2_ffn_re_w1, L2_ffn_re_b1, L2_ffn_re_w2, L2_ffn_re_b2, L3_attn_W_in, L3_attn_conv_w, L3_attn_conv_b, L3_attn_W_gates, L3_attn_b_gates, L3_attn_forget_base, L3_attn_W_out, L3_attn_gamma1, L3_attn_gamma2, L3_attn_W_grow, L3_attn_W_shrink, L3_ffn_task_ids, L3_ffn_gw1, L3_ffn_gb1, L3_ffn_gw2, L3_ffn_gb2, L3_ffn_We1, L3_ffn_be1, L3_ffn_We2, L3_ffn_be2, L3_ffn_Ws1, L3_ffn_bs1, L3_ffn_Ws2, L3_ffn_bs2):

    def _L0_attn_ref(x, w_qkv, ln_w, w_proj):
        import jax, jax.numpy as jnp
        import numpy as np
        B, T, C = (4, 512, 128)
        H = 16
        LS = 32
        EPS = 1e-06

        def rmsnorm(x, w):
            xf = x.astype(jnp.float32)
            y = xf * jax.lax.rsqrt(jnp.mean(xf * xf, axis=-1, keepdims=True) + EPS)
            return y.astype(x.dtype) * w
        Bx, Tx, Cx = x.shape
        ng = Tx // LS
        hd = Cx // H
        xg = x.reshape(Bx, ng, LS, Cx)
        qkv = jnp.einsum('bglc,cd->bgld', xg, w_qkv)
        q, k, v = jnp.split(qkv, 3, axis=-1)
        q = rmsnorm(q, ln_w)
        k = rmsnorm(k, ln_w)
        q = q.reshape(Bx, ng, LS, H, hd).transpose(0, 1, 3, 2, 4)
        k = k.reshape(Bx, ng, LS, H, hd).transpose(0, 1, 3, 2, 4)
        v = v.reshape(Bx, ng, LS, H, hd).transpose(0, 1, 3, 2, 4)
        scale = 1.0 / np.sqrt(hd)
        att = jnp.einsum('bghqd,bghkd->bghqk', q, k) * scale
        causal = jnp.tril(jnp.ones((LS, LS), dtype=bool))
        att = jnp.where(causal, att, -jnp.finfo(att.dtype).max)
        att = jax.nn.softmax(att, axis=-1)
        y = jnp.einsum('bghqk,bghkd->bghqd', att, v)
        y = y.transpose(0, 1, 3, 2, 4).reshape(Bx, Tx, Cx)
        return jnp.einsum('btc,cd->btd', y, w_proj)

    def _L0_ffn_ref(hidden_states, router_weight, e_bias, gate_w, up_w, down_w, sh_gate_w, sh_up_w, sh_down_w):
        import jax, jax.numpy as jnp
        import numpy as np
        B, S, H = (1, 256, 128)
        E, K = (16, 4)
        G, TG = (4, 2)
        I_MOE = 64
        N_SH = 2
        SCALE = 2.5

        def _mlp(x, gw, uw, dw):
            return jax.nn.silu(x @ gw.T) * (x @ uw.T) @ dw.T

        def _route(x2d, router_weight, e_bias):
            T = x2d.shape[0]
            scores = jax.nn.sigmoid(x2d @ router_weight.T)
            sc = scores + e_bias[None, :]
            group_scores = jnp.sum(jax.lax.top_k(sc.reshape(T, G, E // G), 2)[0], axis=-1)
            _, gidx = jax.lax.top_k(group_scores, TG)
            gmask = jnp.zeros((T, G), sc.dtype).at[jnp.arange(T)[:, None], gidx].set(1.0)
            smask = jnp.repeat(gmask, E // G, axis=1)
            masked = jnp.where(smask > 0, sc, 0.0)
            _, tidx = jax.lax.top_k(masked, K)
            tw = jnp.take_along_axis(scores, tidx, axis=1)
            tw = tw / (jnp.sum(tw, axis=-1, keepdims=True) + 1e-20)
            tw = tw * SCALE
            return (tidx, tw)

        def _moe_forward(hidden_states, router_weight, e_bias, gate_w, up_w, down_w, sh_gate_w, sh_up_w, sh_down_w):
            orig_shape = hidden_states.shape
            x = hidden_states.reshape(-1, H)
            T = x.shape[0]
            tidx, tw = _route(x, router_weight, e_bias)
            g = jnp.einsum('th,eih->tei', x, gate_w)
            u = jnp.einsum('th,eih->tei', x, up_w)
            h = jax.nn.silu(g) * u
            yo = jnp.einsum('tei,ehi->teh', h, down_w)
            combine = jnp.zeros((T, E), tw.dtype).at[jnp.arange(T)[:, None], tidx].add(tw)
            routed = jnp.einsum('te,teh->th', combine, yo)
            shared = _mlp(hidden_states.reshape(-1, H), sh_gate_w, sh_up_w, sh_down_w)
            return (routed + shared).reshape(orig_shape)
        return _moe_forward(hidden_states, router_weight, e_bias, gate_w, up_w, down_w, sh_gate_w, sh_up_w, sh_down_w)

    def _L1_attn_ref(x, Wq, Wk, Wv, Wo, scale):
        import jax, jax.numpy as jnp
        import numpy as np
        import itertools
        B, T, C, H = (2, 256, 128, 8)
        HD = C // H

        def _head_dirs():
            signs = [-1.0, 1.0]
            tri = np.array(list(itertools.product(signs, repeat=3)), dtype=np.float32)
            tri = tri / np.linalg.norm(tri, axis=1, keepdims=True)
            return jnp.asarray(tri[:H])
        Bb, Tt, Cc = x.shape
        dirs = _head_dirs()
        q3 = (x @ Wq.T).reshape(Bb, Tt, H, 3).transpose(0, 2, 1, 3)
        k3 = (x @ Wk.T).reshape(Bb, Tt, H, 3).transpose(0, 2, 1, 3)
        v = (x @ Wv.T).reshape(Bb, Tt, H, HD).transpose(0, 2, 1, 3)
        q_on_dir = jnp.einsum('bhtd,hd->bht', q3, dirs)
        k_on_dir = jnp.einsum('bhtd,hd->bht', k3, dirs)
        scores = jnp.einsum('bhtd,bhsd->bhts', q3, k3) * scale + q_on_dir[..., :, None] * k_on_dir[..., None, :]
        causal = jnp.tril(jnp.ones((Tt, Tt), dtype=bool))
        scores = jnp.where(causal, scores, -jnp.inf)
        attn = jax.nn.softmax(scores, axis=-1)
        out = jnp.einsum('bhts,bhsd->bhtd', attn, v)
        out = out.transpose(0, 2, 1, 3).reshape(Bb, Tt, Cc)
        return out @ Wo.T

    def _L1_ffn_ref(x, w_g, c_fc, c_proj):
        import jax, jax.numpy as jnp
        import numpy as np
        N_EXP = 8
        TOP_K = 2
        CAP_FACTOR = 1.25
        NEG_INF = -1000000000.0

        def _moe_forward(x, w_g, c_fc, c_proj):
            B, T, D = x.shape
            N = B * T
            xf = x.reshape(N, D)
            logits = xf @ w_g
            topv, topi = jax.lax.top_k(logits, TOP_K)
            full = jnp.full_like(logits, NEG_INF)
            full = full.at[jnp.arange(N)[:, None], topi].set(topv)
            probs = jax.nn.softmax(full, axis=-1)
            capacity = int(TOP_K * CAP_FACTOR * N / N_EXP)
            capacity += capacity % 2
            mask = jax.nn.one_hot(jnp.swapaxes(topi, 0, 1), N_EXP, dtype=jnp.int32)
            rank = jnp.cumsum(mask.reshape(TOP_K * N, N_EXP), axis=0).reshape(TOP_K, N, N_EXP) - 1
            mask = mask * (rank < capacity)
            rank_sel = jnp.sum(mask * rank, axis=-1)
            wts = jnp.sum(mask * probs[None], axis=-1)
            cb = jnp.zeros((N, N_EXP, capacity), x.dtype)
            tok = jnp.arange(N)
            for k in range(TOP_K):
                cb = cb.at[tok, topi[:, k], rank_sel[k]].add(wts[k])
            sec_mask = (cb != 0).astype(x.dtype)
            exp_batches = jnp.einsum('nec,nd->ecd', sec_mask, xf)
            h = jax.nn.gelu(jnp.einsum('ecd,edh->ech', exp_batches, c_fc), approximate=False)
            exp_out = jnp.einsum('ech,ehd->ecd', h, c_proj)
            out = jnp.einsum('nec,ecd->nd', cb, exp_out)
            return out.reshape(B, T, D)
        return _moe_forward(x, w_g, c_fc, c_proj)

    def _L2_attn_ref(x, w_aq, w_ak, w_av, w_ao):
        import jax, jax.numpy as jnp
        import numpy as np
        INF_APPROX = 1e+30
        ROTARY_BASE = 10000.0
        D_HEAD = 128

        def _rope(x, base=ROTARY_BASE):
            _, length, _, width = x.shape
            half = width // 2
            positions = jnp.arange(length, dtype=x.dtype)
            dims = jnp.arange(half, dtype=x.dtype)
            ang_freqs = jnp.power(base, -dims / half)
            radians = positions[:, None] * ang_freqs[None, :]
            cos = jnp.cos(radians)[None, :, None, :]
            sin = jnp.sin(radians)[None, :, None, :]
            even, odd = jnp.split(x, 2, axis=-1)
            return jnp.concatenate([even * cos - odd * sin, even * sin + odd * cos], axis=-1)
        B, T, M = x.shape
        q = jnp.einsum('btm,mhd->bthd', x, w_aq)
        k = jnp.einsum('btm,mhd->bthd', x, w_ak)
        v = jnp.einsum('btm,mhd->bthd', x, w_av)
        q = _rope(q)
        k = _rope(k)
        s = jnp.einsum('bihd,bjhd->bhij', q, k) / D_HEAD
        i = jnp.arange(T)[:, None]
        j = jnp.arange(T)[None, :]
        mask = (i < j).astype(x.dtype)[None, None, :, :]
        s = s - jnp.asarray(INF_APPROX, x.dtype) * mask
        p = jax.nn.softmax(s, axis=-1)
        o = jnp.einsum('bhij,bjhd->bihd', p, v)
        r = jnp.einsum('bihd,hdm->bim', o, w_ao)
        return r

    def _L2_ffn_ref(x, positions, theta, gamma1, gamma2, q_w, q_b, k_w, k_b, v_w, v_b, o_w, o_b, router_w, router_b, sh_w1, sh_b1, sh_w2, sh_b2, re_w1, re_b1, re_w2, re_b2):
        import jax, jax.numpy as jnp
        import numpy as np
        B, S, D = (2, 128, 128)
        H, HD = (16, 64)
        E_R = 31
        K_ACT = 3
        INTER = 128
        EPS = 1e-05
        BASE = 10000.0

        def _rmsnorm(x, gamma):
            rms = jnp.sqrt(jnp.mean(x * x, axis=-1, keepdims=True) + EPS)
            return x / rms * gamma

        def _rope(x, theta):
            seq = x.shape[2]
            angles = jnp.arange(seq, dtype=theta.dtype)[:, None] * theta
            cos = jnp.cos(angles)[None, None]
            sin = jnp.sin(angles)[None, None]
            x1, x2 = (x[..., 0::2], x[..., 1::2])
            return jnp.concatenate([x1 * cos - x2 * sin, x1 * sin + x2 * cos], axis=-1)

        def _forward(x, theta, gamma1, gamma2, q_w, q_b, k_w, k_b, v_w, v_b, o_w, o_b, router_w, router_b, sh_w1, sh_b1, sh_w2, sh_b2, re_w1, re_b1, re_w2, re_b2):
            b, s, d = x.shape
            xn = _rmsnorm(x, gamma1)
            q = (xn @ q_w + q_b).reshape(b, s, H, HD).transpose(0, 2, 1, 3)
            k = (xn @ k_w + k_b).reshape(b, s, H, HD).transpose(0, 2, 1, 3)
            v = (xn @ v_w + v_b).reshape(b, s, H, HD).transpose(0, 2, 1, 3)
            q = _rope(q, theta)
            k = _rope(k, theta)
            scale = 1.0 / np.sqrt(HD)
            scores = jnp.einsum('bhqd,bhkd->bhqk', q, k) * scale
            causal = jnp.tril(jnp.ones((s, s), dtype=bool))
            scores = jnp.where(causal, scores, -jnp.inf)
            attn = jax.nn.softmax(scores, axis=-1)
            ctx = jnp.einsum('bhqk,bhkd->bhqd', attn, v)
            ctx = ctx.transpose(0, 2, 1, 3).reshape(b, s, H * HD)
            attn_out = ctx @ o_w + o_b + xn
            an = _rmsnorm(attn_out, gamma2)
            shared = jax.nn.gelu(an @ sh_w1 + sh_b1, approximate=False) @ sh_w2 + sh_b2
            logits = an @ router_w + router_b
            aff = jax.nn.softmax(logits, axis=-1)
            topv, topi = jax.lax.top_k(aff, K_ACT)
            gates = jnp.sum(jax.nn.one_hot(topi, E_R, dtype=aff.dtype) * topv[..., None], axis=-2)
            h = jax.nn.gelu(jnp.einsum('bsd,edh->besh', an, re_w1) + re_b1[None, :, None, :], approximate=False)
            routed = jnp.einsum('bse,besh,ehd->bsd', gates, h, re_w2) + jnp.einsum('bse,ed->bsd', gates, re_b2)
            return shared + routed + an + attn_out
        del positions
        return _forward(x, theta, gamma1, gamma2, q_w, q_b, k_w, k_b, v_w, v_b, o_w, o_b, router_w, router_b, sh_w1, sh_b1, sh_w2, sh_b2, re_w1, re_b1, re_w2, re_b2)

    def _L3_attn_ref(x, W_in, conv_w, conv_b, W_gates, b_gates, forget_base, W_out, gamma1, gamma2, W_grow, W_shrink):
        import jax, jax.numpy as jnp
        import numpy as np
        from jax import lax
        DIM = 128
        EXP = 2
        GMLP_EXP = 2
        K = 4
        HID = DIM * EXP
        GHID = DIM * GMLP_EXP
        ALPHA_LOG_SCALE = -8.0

        def init_forget_gate(size, a=0.001, b=0.1, lo=-9.0, hi=-4.323):
            x = np.log(np.expm1(np.linspace(a, b, size, dtype=np.float64)))
            x = (x - x.min()) / (x.max() - x.min())
            x = x * abs(hi - lo) + lo
            return jnp.asarray(x, dtype=jnp.float32)

        def _rmsnorm(x, gamma):
            n = jnp.sqrt(jnp.sum(x * x, axis=-1, keepdims=True))
            return gamma * jnp.sqrt(jnp.float32(x.shape[-1])) * (x / n)

        def _linear_recurrence(alpha, x):

            def combine(e1, e2):
                a1, b1 = e1
                a2, b2 = e2
                return (a1 * a2, a2 * b1 + b2)
            _, h = lax.associative_scan(combine, (alpha, x), axis=1)
            return h

        def _hawk_block(x, W_in, conv_w, conv_b, W_gates, b_gates, forget_base, W_out, gamma1, gamma2, W_grow, W_shrink):
            B, T, _ = x.shape
            xn = _rmsnorm(x, gamma1)
            z = xn @ W_in.T
            gate, xc = (z[..., :HID], z[..., HID:])
            xc_t = jnp.pad(xc.transpose(0, 2, 1), ((0, 0), (0, 0), (K - 1, 0)))
            xc = lax.conv_general_dilated(xc_t, conv_w, window_strides=(1,), padding='VALID', dimension_numbers=('NCH', 'OIH', 'NCH'), feature_group_count=HID)
            xc = (xc + conv_b[None, :, None]).transpose(0, 2, 1)
            g = xc @ W_gates.T + b_gates
            forget, inp = (g[..., :HID], g[..., HID:])
            alpha = jnp.exp(ALPHA_LOG_SCALE * jax.nn.softplus(forget_base) * jax.nn.sigmoid(forget))
            beta = jnp.sqrt(1.0 - alpha ** 2 + 1e-06)
            xs = beta * jax.nn.sigmoid(inp) * xc
            h = _linear_recurrence(alpha, xs)
            rglru_out = jax.nn.gelu(gate, approximate=False) * h @ W_out.T
            x = x + rglru_out
            xn2 = _rmsnorm(x, gamma2)
            gz = xn2 @ W_grow.T
            mgate, mx = (gz[..., :GHID], gz[..., GHID:])
            mlp_out = jax.nn.gelu(mgate, approximate=False) * mx @ W_shrink.T
            return x + mlp_out
        return _hawk_block(x, W_in, conv_w, conv_b, W_gates, b_gates, forget_base, W_out, gamma1, gamma2, W_grow, W_shrink)

    def _L3_ffn_ref(x, task_ids, gw1, gb1, gw2, gb2, We1, be1, We2, be2, Ws1, bs1, Ws2, bs2):
        import jax, jax.numpy as jnp
        import numpy as np
        B, L, D, H, E, K = (4, 256, 128, 256, 8, 2)

        def _mlp(x, w1, b1, w2, b2):
            h = jax.nn.gelu(x @ w1 + b1, approximate=True)
            return h @ w2 + b2
        bsz, length, d = x.shape
        T = bsz * length
        xf = x.reshape(T, d)
        logits = jax.nn.gelu(xf @ gw1 + gb1, approximate=False) @ gw2 + gb2
        scores = jax.nn.softmax(logits, axis=-1)
        topk_w, topk_idx = jax.lax.top_k(scores, K)
        rows = jnp.arange(T)[:, None]
        gates = jnp.zeros_like(scores).at[rows, topk_idx].set(topk_w)
        out = _mlp(xf, Ws1, bs1, Ws2, bs2)
        for e in range(E):
            out = out + gates[:, e:e + 1] * _mlp(xf, We1[e], be1[e], We2[e], be2[e])
        return out.reshape(bsz, length, d)
    x = L0_attn_x
    x = _layernorm(x + _L0_attn_ref(x, L0_attn_w_qkv, L0_attn_ln_w, L0_attn_w_proj), axis=-1)
    x = _layernorm(x + _L0_ffn_ref(x, L0_ffn_router_weight, L0_ffn_e_bias, L0_ffn_gate_w, L0_ffn_up_w, L0_ffn_down_w, L0_ffn_sh_gate_w, L0_ffn_sh_up_w, L0_ffn_sh_down_w), axis=-1)
    x = _layernorm(x + _L1_attn_ref(x, L1_attn_Wq, L1_attn_Wk, L1_attn_Wv, L1_attn_Wo, L1_attn_scale), axis=-1)
    x = _layernorm(x + _L1_ffn_ref(x, L1_ffn_w_g, L1_ffn_c_fc, L1_ffn_c_proj), axis=-1)
    x = _layernorm(x + _L2_attn_ref(x, L2_attn_w_aq, L2_attn_w_ak, L2_attn_w_av, L2_attn_w_ao), axis=-1)
    x = _layernorm(x + _L2_ffn_ref(x, L2_ffn_positions, L2_ffn_theta, L2_ffn_gamma1, L2_ffn_gamma2, L2_ffn_q_w, L2_ffn_q_b, L2_ffn_k_w, L2_ffn_k_b, L2_ffn_v_w, L2_ffn_v_b, L2_ffn_o_w, L2_ffn_o_b, L2_ffn_router_w, L2_ffn_router_b, L2_ffn_sh_w1, L2_ffn_sh_b1, L2_ffn_sh_w2, L2_ffn_sh_b2, L2_ffn_re_w1, L2_ffn_re_b1, L2_ffn_re_w2, L2_ffn_re_b2), axis=-1)
    x = _layernorm(x + _L3_attn_ref(x, L3_attn_W_in, L3_attn_conv_w, L3_attn_conv_b, L3_attn_W_gates, L3_attn_b_gates, L3_attn_forget_base, L3_attn_W_out, L3_attn_gamma1, L3_attn_gamma2, L3_attn_W_grow, L3_attn_W_shrink), axis=-1)
    x = _layernorm(x + _L3_ffn_ref(x, L3_ffn_task_ids, L3_ffn_gw1, L3_ffn_gb1, L3_ffn_gw2, L3_ffn_gb2, L3_ffn_We1, L3_ffn_be1, L3_ffn_We2, L3_ffn_be2, L3_ffn_Ws1, L3_ffn_bs1, L3_ffn_Ws2, L3_ffn_bs2), axis=-1)
    return x

_drawn_inputs = setup_inputs


def setup_inputs(seed=0):
    import zlib

    import numpy as np

    out = dict(_drawn_inputs(seed))
    spreads = {'L0_attn_ln_w': (1.0, 0.2),
     'L0_ffn_e_bias': (0.0, 0.8),
     'L2_attn_w_aq': (0.0, 0.8),
     'L2_ffn_gamma1': (1.0, 0.2),
     'L2_ffn_gamma2': (1.0, 0.2),
     'L2_ffn_q_b': (0.0, 0.8),
     'L2_ffn_k_b': (0.0, 0.8),
     'L2_ffn_v_b': (0.0, 0.1),
     'L2_ffn_o_b': (0.0, 0.1),
     'L2_ffn_router_b': (0.0, 0.8),
     'L2_ffn_sh_b1': (0.0, 0.8),
     'L2_ffn_sh_b2': (0.0, 0.1),
     'L2_ffn_re_b1': (0.0, 0.8),
     'L2_ffn_re_b2': (0.0, 0.8),
     'L3_attn_conv_b': (0.0, 0.1),
     'L3_attn_b_gates': (0.0, 0.524),
     'L3_attn_gamma1': (1.0, 0.2),
     'L3_attn_gamma2': (1.0, 0.2),
     'L3_ffn_gb1': (0.0, 0.8),
     'L3_ffn_gb2': (0.0, 0.402),
     'L3_ffn_be1': (0.0, 0.8),
     'L3_ffn_be2': (0.0, 0.424),
     'L3_ffn_bs1': (0.0, 0.515),
     'L3_ffn_bs2': (0.0, 0.1)}
    factors = {'L0_ffn_router_weight': 8.0,
     'L0_ffn_gate_w': 8.0,
     'L0_ffn_up_w': 8.0,
     'L0_ffn_down_w': 8.0,
     'L0_ffn_sh_gate_w': 8.0,
     'L0_ffn_sh_up_w': 8.0,
     'L0_ffn_sh_down_w': 8.0,
     'L1_attn_Wq': 8.0,
     'L1_attn_Wk': 8.0,
     'L1_attn_Wv': 3.215,
     'L1_attn_Wo': 3.293,
     'L2_attn_w_ak': 8.0,
     'L2_ffn_theta': 8.0,
     'L2_ffn_q_w': 8.0,
     'L2_ffn_k_w': 8.0,
     'L2_ffn_router_w': 8.0,
     'L2_ffn_sh_w1': 5.645,
     'L2_ffn_sh_w2': 4.4,
     'L2_ffn_re_w1': 8.0,
     'L2_ffn_re_w2': 8.0,
     'L3_ffn_gw1': 4.856,
     'L3_ffn_gw2': 4.727,
     'L3_ffn_We1': 7.906,
     'L3_ffn_We2': 7.144}
    for name, (base, spread) in spreads.items():
        noise = np.random.default_rng([zlib.crc32(name.encode()), seed]).standard_normal(out[name].shape)
        drawn = base * np.exp(spread * noise) if base else spread * noise
        out[name] = jnp.asarray(drawn.astype(out[name].dtype))
    for name, factor in factors.items():
        out[name] = (out[name] * factor).astype(out[name].dtype)
    return out
```

```python
from contextlib import ExitStack

import numpy as np
import concourse.bass as bass
from concourse import mybir

F32 = mybir.dt.float32
BF16 = mybir.dt.bfloat16
ACT = mybir.ActivationFunctionType
ALU = mybir.AluOpType
AX = mybir.AxisListType

P = 128
B = 4
T = 512
N = B * T
NT = N // P
QT = T // P
NEG = -1.0e30


def cols(c, n=T):
    return bass.ds(c * n, n)


class Stage:

    def __init__(self, core, name):
        self.core, self.nc, self.name = core, core.nc, name
        self.ctx = ExitStack()
        self.sems = []

    def __enter__(self):
        self.ctx.__enter__()
        return self

    def __exit__(self, *e):
        self.core.spent += self.sems
        return self.ctx.__exit__(*e)

    def sb(self, name, shape, dtype=F32):
        return self.ctx.enter_context(self.nc.sbuf_tensor(f"{self.name}_{name}", shape, dtype))

    def sem(self, name):
        self.sems.append(self.nc.alloc_semaphore(f"{self.name}_{name}"))
        return self.sems[-1]


class Steps:

    def __init__(self, engine, sem, base=0):
        self.engine, self.sem, self.base, self.n = engine, sem, base, 0

    def __call__(self, instruction):
        self.n += 1
        instruction.then_inc(self.sem, 1)
        self.engine.wait_ge(self.sem, self.base + self.n)


class Core:

    def __init__(self, nc, ctx, dram):
        self.nc, self.dram = nc, dram
        self.spent = []

        def sb(name, shape, dtype=F32):
            return ctx.enter_context(nc.sbuf_tensor(name, shape, dtype))

        self.x = sb("x_fm", [P, N])
        self.sum = sb("sum_fm", [P, N])
        self.psum = ctx.enter_context(nc.psum_tensor("psum", [P, 8, T], F32))
        self.ident = sb("ident", [P, P])
        self.mean_w = sb("mean_w", [P, P])
        self.center_w = sb("center_w", [P, P])
        self.eps = sb("eps", [P, 4])
        self.identb = sb("identb", [P, P], BF16)
        self.maskb = sb("maskb", [P, P], BF16)


def recycle(core):
    core.nc.clear_and_free_semaphores(core.spent)
    core.nc.all_engine_barrier()
    core.spent = []


def load_start(core):
    nc, dram = core.nc, core.dram
    with Stage(core, "load") as st:
        xt = st.sb("x_tm", [P, NT, P])
        idf = st.sb("maskf", [P, P])
        x_loaded, consts_loaded, tiles_ready = (st.sem(n) for n in ("x_loaded", "consts_loaded", "tiles_ready"))
        with nc.Block() as block:
            @block.sync
            def _(sp):
                sp.dma_start(xt[:], dram["x"].rearrange("(t p) c -> p t c", p=P)).then_inc(x_loaded, 16)
                for to, name in ((core.ident, "c_ident"), (core.mean_w, "c_mean_w"), (core.center_w, "c_center_w"), (core.eps, "c_eps")):
                    sp.dma_start(to[:], dram[name]).then_inc(consts_loaded, 16)
                sp.dma_start(idf[:], dram["c_mask"]).then_inc(consts_loaded, 16)

            @block.tensor
            def _(pe):
                pe.wait_ge(consts_loaded, 5 * 16)
                pe.wait_ge(x_loaded, 16)
                for b in range(B):
                    for q in range(QT):
                        last = nc.tensor.transpose(core.psum[:, b, q * P:(q + 1) * P], xt[:, b * QT + q, :], core.ident[:])
                    last.then_inc(tiles_ready, 1)

            @block.vector
            def _(dve):
                dve.wait_ge(consts_loaded, 5 * 16)
                nc.vector.tensor_copy(core.identb[:], core.ident[:])
                nc.vector.tensor_copy(core.maskb[:], idf[:])
                for b in range(B):
                    dve.wait_ge(tiles_ready, b + 1)
                    nc.vector.tensor_copy(core.x[:, cols(b)], core.psum[:, b, :])


def norm(core, name, src, dst, center, eps_col, gamma=None):
    nc = core.nc
    with Stage(core, name) as st:
        sq = st.sb("sq", [P, 2, T])
        lnv = st.sb("lnv", [P, 2, T])
        rs = st.sb("rs", [P, 2, T])
        centered, squared, var_ready, ln_ready, rs_ready, out_ready = (
            st.sem(n) for n in ("centered", "squared", "var_ready", "ln_ready", "rs_ready", "out_ready"))
        xc = [core.psum[:, b, :] for b in range(4)]
        var = [core.psum[:, 4 + b, :] for b in range(4)]
        with nc.Block() as block:
            @block.tensor
            def _(pe):
                if center:
                    for b in range(B):
                        nc.tensor.matmul(xc[b], core.center_w[:], src[:, cols(b)], start=True, stop=True).then_inc(centered, 1)
                for b in range(B):
                    pe.wait_ge(squared, b + 1)
                    nc.tensor.matmul(var[b], core.mean_w[:], sq[:, b % 2, :], start=True, stop=True).then_inc(var_ready, 1)

            @block.scalar
            def _(act):
                def square(b):
                    if center:
                        act.wait_ge(centered, b + 1)
                    if b >= 2:
                        act.wait_ge(var_ready, b - 1)
                    nc.scalar.activation(sq[:, b % 2, :], xc[b] if center else src[:, cols(b)], ACT.Square).then_inc(squared, 1)

                nc.scalar.preload_act_table_set("natural_log_exp_and_others")
                square(0)
                for b in range(B):
                    if b + 1 < B:
                        square(b + 1)
                    act.wait_ge(var_ready, b + 1)
                    nc.scalar.activation(lnv[:, b % 2, :], var[b], ACT.Ln, bias=core.eps[:, eps_col:eps_col + 1]).then_inc(ln_ready, 1)
                    act.wait_ge(ln_ready, b + 1)
                    if b >= 2:
                        act.wait_ge(out_ready, b - 1)
                    nc.scalar.activation(rs[:, b % 2, :], lnv[:, b % 2, :], ACT.Exp, scale=-0.5).then_inc(rs_ready, 1)

            @block.vector
            def _(dve):
                for b in range(B):
                    dve.wait_ge(rs_ready, b + 1)
                    x_in = xc[b] if center else src[:, cols(b)]
                    if gamma is None:
                        nc.vector.tensor_tensor(dst[:, cols(b)], x_in, rs[:, b % 2, :], ALU.mult).then_inc(out_ready, 1)
                    else:
                        nc.vector.scalar_tensor_tensor(dst[:, cols(b)], x_in, gamma, rs[:, b % 2, :], ALU.mult, ALU.mult).then_inc(out_ready, 1)


def store_end(core):
    nc, dram = core.nc, core.dram
    with Stage(core, "store") as st:
        xt = st.sb("x_tm", [P, NT, P])
        tiles_ready, tiles_out, stored = (st.sem(n) for n in ("tiles_ready", "tiles_out", "stored"))
        out = dram["out"].rearrange("(t p) c -> p t c", p=P)
        with nc.Block() as block:
            @block.tensor
            def _(pe):
                for b in range(B):
                    for q in range(QT):
                        last = nc.tensor.transpose(core.psum[:, b, q * P:(q + 1) * P], core.x[:, (b * QT + q) * P:(b * QT + q + 1) * P], core.ident[:])
                    last.then_inc(tiles_ready, 1)

            @block.vector
            def _(dve):
                for b in range(B):
                    dve.wait_ge(tiles_ready, b + 1)
                    nc.vector.tensor_copy(xt[:, b * QT:(b + 1) * QT, :].rearrange("p t c -> p (t c)"), core.psum[:, b, :]).then_inc(tiles_out, 1)

            @block.sync
            def _(sp):
                for b in range(B):
                    sp.wait_ge(tiles_out, b + 1)
                    sp.dma_start(out[:, b * QT:(b + 1) * QT, :], xt[:, b * QT:(b + 1) * QT, :]).then_inc(stored, 16)
                sp.wait_ge(stored, 16 * B)


def window_attention(core):
    nc, dram = core.nc, core.dram
    G, HG, W = 4, 4, 4
    L = 32
    with Stage(core, "l0a") as st:
        wqkv = st.sb("wqkv", [P, 3 * P])
        wproj = st.sb("wproj", [P, P])
        vecs = st.sb("vecs", [P, 8])
        wmask = st.sb("wmask", [P, L])
        xs = st.sb("xs", [P, T])
        q_raw, k_raw, qn, kn = (st.sb(n, [P, T]) for n in ("q_raw", "k_raw", "qn", "kn"))
        sq = st.sb("sq", [P, 2, T])
        lnm = st.sb("lnm", [P, 2, T])
        rs = st.sb("rs", [P, 2, T])
        v_tm = st.sb("v_tm", [P, QT, P])
        kx = st.sb("kx", [P, QT, W, HG, L])
        s_sb = st.sb("s_sb", [P, G, QT * HG * L])
        p_sb = st.sb("p_sb", [P, G, QT * HG * L])
        smax = st.sb("smax", [P, G, QT * HG])
        ssum = st.sb("ssum", [P, G, QT * HG])
        y_fm = st.sb("y_fm", [P, QT, W, L])
        (loaded, x_ready, qkv_ready, raw_ready, squared, ms_ready, ln_ready, rs_ready, qk_ready, s_ready, shifted,
         exp_ready, pt_ready, av_ready, y_ready, out_ready, chunk_done, dve_step, passed) = (st.sem(n) for n in (
            "loaded", "x_ready", "qkv_ready", "raw_ready", "squared", "ms_ready", "ln_ready", "rs_ready", "qk_ready", "s_ready",
            "shifted", "exp_ready", "pt_ready", "av_ready", "y_ready", "out_ready", "chunk_done", "dve_step", "passed"))
        ps_s = [core.psum[:, g, :] for g in range(G)]
        ps_o = [core.psum[:, 4 + w, :] for w in range(W)]
        DVE_STEPS = 19

        with nc.Block() as block:
            @block.sync
            def _(sp):
                sp.dma_start(wqkv[:], dram["l0_wqkv"]).then_inc(loaded, 16)
                sp.dma_start(wproj[:], dram["l0_wproj"]).then_inc(loaded, 16)
                sp.dma_start(vecs[:, 0:1], dram["l0_lnw"]).then_inc(loaded, 16)
                sp.dma_start(vecs[:, 1:5], dram["c_headmask"]).then_inc(loaded, 16)
                sp.dma_start(wmask[:], dram["c_wmask"]).then_inc(loaded, 16)

            @block.gpsimd
            def _(pool):
                with pool.Fori(0, B) as c:
                    pool.wait_ge(chunk_done, c + 1)
                    pool.sem_inc(passed, 1)
                    nc.gpsimd.tensor_copy(xs[:], core.x[:, cols(c)]).then_inc(x_ready, 1)

            @block.tensor
            def _(pe):
                pe.wait_ge(loaded, 5 * 16)
                with pe.Fori(0, B) as c:
                    pe.wait_ge(x_ready, c + 1)
                    nc.tensor.matmul(ps_s[0], wqkv[:, 0:P], xs[:], start=True, stop=True).then_inc(qkv_ready, 1)
                    nc.tensor.matmul(ps_s[1], wqkv[:, P:2 * P], xs[:], start=True, stop=True).then_inc(qkv_ready, 1)
                    for t in range(QT):
                        last = nc.tensor.matmul(ps_s[2][:, t * P:(t + 1) * P], xs[:, t * P:(t + 1) * P], wqkv[:, 2 * P:], start=True, stop=True)
                    last.then_inc(qkv_ready, 1)
                    for j in range(2):
                        pe.wait_ge(squared, 2 * c + j + 1)
                        nc.tensor.matmul(ps_o[j], core.mean_w[:], sq[:, j, :], start=True, stop=True).then_inc(ms_ready, 1)
                    pe.wait_ge(qk_ready, c + 1)
                    pe.sem_inc(passed, 1)
                    for t in range(QT):
                        for w in range(W):
                            for g in range(G):
                                rows, q_at = slice(32 * g, 32 * g + 32), t * P + w * L
                                last = nc.tensor.matmul(ps_s[g][32 * w:32 * w + 32, t * P:(t + 1) * P], qn[rows, q_at:q_at + L],
                                                        kx[rows, t, w, :, :].rearrange("p h k -> p (h k)"), start=True, stop=True)
                    last.then_inc(s_ready, 1)
                    pe.wait_ge(pt_ready, c + 1)
                    pe.sem_inc(passed, 1)
                    for t in range(QT):
                        for g in range(G):
                            for w in range(W):
                                rows = slice(32 * w, 32 * w + 32)
                                last = nc.tensor.matmul(ps_o[w][32 * g:32 * g + 32, t * P:(t + 1) * P], v_tm[rows, t, 32 * g:32 * g + 32],
                                                        s_sb[rows, g, t * P:(t + 1) * P], start=True, stop=True)
                    last.then_inc(av_ready, 1)
                    pe.wait_ge(y_ready, c + 1)
                    nc.tensor.matmul(ps_s[0], wproj[:], y_fm[:].rearrange("p t w q -> p (t w q)"), start=True, stop=True).then_inc(out_ready, 1)

            @block.scalar
            def _(act):
                nc.scalar.preload_act_table_set("natural_log_exp_and_others")
                act.wait_ge(loaded, 5 * 16)
                with act.Fori(0, B) as c:
                    for j, raw in enumerate((q_raw, k_raw)):
                        act.wait_ge(qkv_ready, 3 * c + j + 1)
                        nc.scalar.activation(raw[:], ps_s[j], ACT.Copy).then_inc(raw_ready, 1)
                        nc.scalar.activation(sq[:, j, :], ps_s[j], ACT.Square).then_inc(squared, 1)
                    for j in range(2):
                        act.wait_ge(ms_ready, 2 * c + j + 1)
                        nc.scalar.activation(lnm[:, j, :], ps_o[j], ACT.Ln, bias=core.eps[:, 1:2]).then_inc(ln_ready, 1)
                        act.wait_ge(ln_ready, 2 * c + j + 1)
                        nc.scalar.activation(rs[:, j, :], lnm[:, j, :], ACT.Exp, scale=-0.5).then_inc(rs_ready, 1)
                    for g in range(G):
                        act.wait_ge(shifted, G * c + g + 1)
                        nc.scalar.activation(p_sb[:, g, :], s_sb[:, g, :], ACT.Exp, scale=8 ** -0.5).then_inc(exp_ready, 1)

            @block.vector
            def _(dve):
                dve.wait_ge(loaded, 5 * 16)
                dve.sem_inc(chunk_done, 1)
                with dve.Fori(0, B) as c:
                    step = Steps(dve, dve_step, c * DVE_STEPS)
                    dve.wait_ge(qkv_ready, 3 * c + 3)
                    step(nc.vector.tensor_copy(v_tm[:].rearrange("p t d -> p (t d)"), ps_s[2]))
                    dve.wait_ge(rs_ready, 2 * c + 2)
                    dve.wait_ge(raw_ready, 2 * c + 2)
                    nc.vector.scalar_tensor_tensor(qn[:], q_raw[:], vecs[:, 0:1], rs[:, 0, :], ALU.mult, ALU.mult)
                    step(nc.vector.scalar_tensor_tensor(kn[:], k_raw[:], vecs[:, 0:1], rs[:, 1, :], ALU.mult, ALU.mult))
                    for h in range(HG):
                        last = nc.vector.tensor_scalar(kx[:, :, :, h, :], kn[:].rearrange("p (t w k) -> p t w k", w=W, k=L),
                                                       vecs[:, 1 + h:2 + h], None, ALU.mult)
                    last.then_inc(qk_ready, 1)
                    dve.wait_ge(s_ready, c + 1)
                    blocks = [s_sb[:, g, :].rearrange("p (b k) -> p b k", k=L) for g in range(G)]
                    for g in range(G):
                        step(nc.vector.tensor_tensor(blocks[g], ps_s[g].rearrange("p (b k) -> p b k", k=L),
                                                     wmask[:].unsqueeze(1).to_broadcast([P, QT * HG, L]), ALU.add))
                        step(nc.vector.tensor_reduce(smax[:, g, :], blocks[g], AX.X, ALU.max))
                        nc.vector.tensor_tensor(blocks[g], blocks[g], smax[:, g, :].unsqueeze(2).to_broadcast([P, QT * HG, L]),
                                                ALU.subtract).then_inc(shifted, 1)
                    for g in range(G):
                        pb = p_sb[:, g, :].rearrange("p (b k) -> p b k", k=L)
                        dve.wait_ge(exp_ready, G * c + g + 1)
                        step(nc.vector.tensor_reduce(ssum[:, g, :], pb, AX.X, ALU.add))
                        if g == G - 1:
                            step(nc.vector.reciprocal(ssum[:], ssum[:]))
                    for g in range(G):
                        pb = p_sb[:, g, :].rearrange("p (b k) -> p b k", k=L)
                        last = nc.vector.tensor_tensor(pb, pb, ssum[:, g, :].unsqueeze(2).to_broadcast([P, QT * HG, L]), ALU.mult)
                    step(last)
                    last = nc.vector.transpose(s_sb[:].rearrange("p g n -> p (g n)"), p_sb[:].rearrange("p g n -> p (g n)"))
                    last.then_inc(pt_ready, 1)
                    dve.wait_ge(av_ready, c + 1)
                    for h in range(HG):
                        for w in range(W):
                            o = ps_o[w].rearrange("p (t h q) -> p t h q", h=HG, q=L)[:, :, h, :]
                            if h == 0:
                                last = nc.vector.tensor_scalar(y_fm[:, :, w, :], o, vecs[:, 1:2], None, ALU.mult)
                            else:
                                last = nc.vector.scalar_tensor_tensor(y_fm[:, :, w, :], o, vecs[:, 1 + h:2 + h], y_fm[:, :, w, :], ALU.mult, ALU.add)
                        if h < HG - 1:
                            step(last)
                    last.then_inc(y_ready, 1)
                    dve.wait_ge(out_ready, c + 1)
                    nc.vector.tensor_tensor(core.sum[:, cols(c)], ps_s[0], core.x[:, cols(c)], ALU.add).then_inc(chunk_done, 1)
                    assert step.n == DVE_STEPS, step.n


GR = 96
SENT = -3.0e38
HIT = 3.0e38


def experts(core, name, *, act_func, x, resid, gates_t, gates3, n_slots, unroll, tiles, w_dram, with_b1=False,
            b2=None, b2_rows=0, glu=False):
    nc = core.nc
    up = 2 if glu else 1
    w1_cols = up * tiles * P
    biases = tiles if with_b1 else 0
    w_cols = w1_cols + tiles * P + biases
    iters = n_slots // unroll
    assert iters * unroll == n_slots
    items = [(s, b, t) for s in range(unroll) for b in range(B) for t in range(tiles)]
    n_items = len(items)
    gated_credit = tiles + 1
    out_credit = n_items
    with Stage(core, name) as st:
        w = st.sb("w", [P, unroll, w_cols])
        act_sb = st.sb("act", [P, 2, T])
        glu_sb = st.sb("glu", [P, 2, T]) if glu else None
        gated = st.sb("gated", [P, 2, T])
        sel_cols = n_slots * P if glu else 32
        selb = st.sb("selb", [GR, sel_cols], BF16)
        self32 = st.sb("self32", [GR, sel_cols])
        w_loaded = [st.sem(f"w{s}_loaded") for s in range(unroll)]
        (consts_loaded, sel_ready, hid_ready, gate_ready, act_ready, glu_ready, gated_ready, out_done) = (
            st.sem(n) for n in ("consts_loaded", "sel_ready", "hid_ready", "gate_ready", "act_ready", "glu_ready",
                                "gated_ready", "out_done"))
        acc = [core.psum[:, b, :] for b in range(B)]
        hid = [core.psum[:, 4 + k, :] for k in range(2)]
        gate = [core.psum[:, 6 + k, :] for k in range(2)]

        with nc.Block() as block:
            @block.sync
            def _(sp):
                sp.dma_start(self32[:], core.dram["c_selpair" if glu else "c_sel"]).then_inc(consts_loaded, 16)
                with sp.Fori(0, iters) as i:
                    for s in range(unroll):
                        sp.wait_ge(out_done, i * n_items + (s + 1) * B * tiles)
                        sp.dma_start(w[:, s, :], w_dram[bass.ds(i * unroll + s, 1)].rearrange("o p n -> p (o n)")).then_inc(w_loaded[s], 16)

            @block.tensor
            def _(pe):
                pe.sem_inc(out_done, out_credit)
                for b in range(B):
                    nc.tensor.matmul(acc[b], core.ident[:], resid[:, cols(b)], start=True, stop=b2 is None)
                    if b2 is not None:
                        nc.tensor.matmul(acc[b], b2[0:b2_rows, :], gates_t[0:b2_rows, cols(b)], start=False, stop=True)
                pe.wait_ge(sel_ready, 1)
                with pe.Fori(0, iters) as i:
                    def hidden(n):
                        s, b, t = items[n]
                        g = i * n_items + n
                        if b == 0 and t == 0:
                            pe.wait_ge(w_loaded[s], 16 * i + 16)
                        if t == 0:
                            pair, e = i * (unroll * B) + s * B + b, i * unroll + s
                            pe.wait_ge(gated_ready, pair * tiles - tiles + gated_credit)
                            sel = (selb[:, bass.ds(e * P, P)] if glu
                                   else selb[:, bass.ds(e, 1)].to_broadcast([GR, P]))
                            nc.tensor.matmul(gate[b % 2], sel, gates3[:, cols(b)], start=True, stop=True).then_inc(gate_ready, 1)
                        if glu:
                            pe.wait_ge(glu_ready, g + 1)
                            for k in range(2):
                                nc.tensor.matmul(hid[k], w[:, s, (k * tiles + t) * P:(k * tiles + t + 1) * P], x[:, cols(b)],
                                                 start=True, stop=True).then_inc(hid_ready, 1)
                        else:
                            pe.wait_ge(act_ready, g + 1)
                            nc.tensor.matmul(hid[n % 2], w[:, s, t * P:(t + 1) * P], x[:, cols(b)],
                                             start=True, stop=True).then_inc(hid_ready, 1)

                    def output(n):
                        s, b, t = items[n]
                        pe.wait_ge(gated_ready, i * n_items + n + 1 + gated_credit)
                        nc.tensor.matmul(acc[b], w[:, s, w1_cols + t * P:w1_cols + (t + 1) * P], gated[:, n % 2, :],
                                         start=False, stop=True, skip_group_check=True).then_inc(out_done, 1)

                    hidden(0)
                    for n in range(n_items):
                        if n + 1 < n_items:
                            hidden(n + 1)
                        output(n)

            @block.scalar
            def _(act):
                act.wait_ge(consts_loaded, 16)
                nc.scalar.activation(selb[:], self32[:], ACT.Copy).then_inc(sel_ready, 1)
                nc.scalar.preload_act_table(act_func)
                act.sem_inc(act_ready, 2)
                with act.Fori(0, iters) as i:
                    for n, (s, b, t) in enumerate(items):
                        g = i * n_items + n
                        act.wait_ge(hid_ready, g * up + 1)
                        act.wait_ge(gated_ready, g - 1 + gated_credit)
                        bias = {"bias": w[:, s, w_cols - tiles + t:w_cols - tiles + t + 1]} if with_b1 else {}
                        nc.scalar.activation(act_sb[:, n % 2, :], hid[0] if glu else hid[n % 2], act_func, **bias).then_inc(act_ready, 1)

            @block.vector
            def _(dve):
                dve.sem_inc(gated_ready, gated_credit)
                if glu:
                    dve.sem_inc(glu_ready, 1)
                with dve.Fori(0, iters) as i:
                    for n, (s, b, t) in enumerate(items):
                        g = i * n_items + n
                        dve.wait_ge(act_ready, g + 3)
                        src = act_sb[:, n % 2, :]
                        if glu:
                            dve.wait_ge(hid_ready, g * 2 + 2)
                            nc.vector.tensor_tensor(glu_sb[:, n % 2, :], src, hid[1], ALU.mult).then_inc(glu_ready, 1)
                            dve.wait_ge(glu_ready, g + 2)
                            src = glu_sb[:, n % 2, :]
                        dve.wait_ge(gate_ready, i * (unroll * B) + s * B + b + 1)
                        dve.wait_ge(out_done, g - 1 + out_credit)
                        nc.vector.tensor_tensor(gated[:, n % 2, :], src, gate[b % 2], ALU.mult).then_inc(gated_ready, 1)
                dve.wait_ge(out_done, iters * n_items + out_credit)
                for b in range(B):
                    nc.vector.tensor_copy(core.sum[:, cols(b)], acc[b])


def router(core, name, kind, *, x, w_dram, n_experts, top, gates_t, gates3, bias_dram=None, hid_dram=None,
           hid_bias_dram=None, tri_dram=None, capacity=None):
    nc = core.nc
    E, KT = n_experts, 2 if hid_dram is not None else 1
    W = P if kind == "top_capacity" else 32
    with Stage(core, name) as st:
        rw = st.sb("rw", [P, KT, E])
        bias = st.sb("bias", [P, E])
        scores = st.sb("scores", [P, NT, E])
        ranked = st.sb("ranked", [P, NT, E + 8])
        marked = st.sb("marked", [P, NT, E + 8])
        top8 = st.sb("top8", [P, NT, 8])
        mask = st.sb("mask", [P, NT, E])
        g_tm = st.sb("g_tm", [P, NT, W])
        small = st.sb("small", [P, NT, 8])
        rest = st.sb("rest", [32, N])
        part = st.sb("part", [32, N], BF16)
        if kind == "sigmoid_groups":
            tri = st.sb("tri", [P, 2, 16])
            gsum = st.sb("gsum", [P, NT, 4])
            work = st.sb("work", [P, NT, 16])
            work2 = st.sb("work2", [P, NT, 16])
        if hid_dram is not None:
            hw = st.sb("hw", [P, KT * P])
            hb = st.sb("hb", [P, KT])
            hid = st.sb("hid", [P, KT, N])
        if kind == "top_capacity":
            masks_t = st.sb("masks_t", [8, 2, N])
            probs_t = st.sb("probs_t", [8, 2, N])
            count = st.sb("count", [8, 2, N])
            ones = st.sb("ones", [8, N])
        (loaded, hid_psum, hid_ready, logits_ready, scores_ready, shifted, exp_ready, gates_ready, gates_t_psum,
         dve_step) = (st.sem(n) for n in ("loaded", "hid_psum", "hid_ready", "logits_ready", "scores_ready", "shifted",
                                          "exp_ready", "gates_ready", "gates_t_psum", "dve_step"))
        logits = core.psum[:, 0, 0:NT * E].rearrange("p (t e) -> p t e", e=E)
        loads = [(rw[:], w_dram)]
        if bias_dram is not None:
            loads.append((bias[:], bias_dram.partition_broadcast(P)))
        if tri_dram is not None:
            loads.append((tri[:], tri_dram))
        if hid_dram is not None:
            loads += [(hw[:], hid_dram), (hb[:], hid_bias_dram)]

        with nc.Block() as block:
            @block.sync
            def _(sp):
                for to, of in loads:
                    sp.dma_start(to, of).then_inc(loaded, 16)

            @block.tensor
            def _(pe):
                pe.wait_ge(loaded, 16 * len(loads))
                if hid_dram is not None:
                    for b in range(B):
                        for k in range(KT):
                            n = b * KT + k
                            if n >= 2:
                                pe.wait_ge(hid_ready, n - 1)
                            nc.tensor.matmul(core.psum[:, 4 + n % 2, :], hw[:, k * P:(k + 1) * P], x[:, cols(b)],
                                             start=True, stop=True).then_inc(hid_psum, 1)
                    pe.wait_ge(hid_ready, B * KT)
                for t in range(NT):
                    for k in range(KT):
                        src = x[:, t * P:(t + 1) * P] if hid_dram is None else hid[:, k, t * P:(t + 1) * P]
                        last = nc.tensor.matmul(logits[:, t, :], src, rw[:, k, :], start=k == 0, stop=k == KT - 1)
                last.then_inc(logits_ready, 1)
                pe.wait_ge(gates_ready, 1)
                for t in range(NT):
                    last = nc.tensor.transpose(core.psum[0:W, t // QT, (t % QT) * P:(t % QT + 1) * P], g_tm[:, t, :], core.ident[:])
                    if t % QT == QT - 1:
                        last.then_inc(gates_t_psum, 1)

            @block.scalar
            def _(act):
                act.wait_ge(loaded, 16 * len(loads))
                if hid_dram is not None:
                    for b in range(B):
                        for k in range(KT):
                            act.wait_ge(hid_psum, b * KT + k + 1)
                            nc.scalar.activation(hid[:, k, cols(b)], core.psum[:, 4 + (b * KT + k) % 2, :], ACT.Gelu,
                                                 bias=hb[:, k:k + 1]).then_inc(hid_ready, 1)
                if kind == "sigmoid_groups":
                    act.wait_ge(logits_ready, 1)
                    nc.scalar.activation(scores[:], logits, ACT.Sigmoid).then_inc(scores_ready, 1)
                else:
                    act.wait_ge(shifted, 1)
                    to, of = (small[:, :, 1:2], small[:, :, 0:1]) if kind == "top_capacity" else (scores[:], scores[:])
                    nc.scalar.activation(to, of, ACT.Exp).then_inc(exp_ready, 1)

            @block.vector
            def _(dve):
                step = Steps(dve, dve_step)

                def wide(ap, n):
                    return ap.to_broadcast([P, NT, n])

                def find_top(k, out):
                    if k < 8:
                        step(nc.vector.memset(top8[:, :, k:8], SENT))
                    for t in range(NT):
                        last = nc.vector.match_replace(marked[:, t, :], top8[:, t, :], ranked[:, t, :], HIT)
                    step(last)
                    step(nc.vector.tensor_scalar(out, marked[:, :, 0:E], HIT, None, ALU.is_equal))

                def rank():
                    for t in range(NT):
                        last = nc.vector.max(top8[:, t, :], ranked[:, t, 0:E])
                    step(last)

                dve.wait_ge(loaded, 16 * len(loads))
                step(nc.vector.memset(ranked[:], SENT))
                step(nc.vector.memset(g_tm[:], 0.0))
                if kind == "sigmoid_groups":
                    dve.wait_ge(scores_ready, 1)
                    step(nc.vector.tensor_tensor(ranked[:, :, 0:E], scores[:], bias[:].unsqueeze(1).to_broadcast([P, NT, E]), ALU.add))
                    four = ranked[:, :, 0:E].rearrange("p t (g k) -> p t g k", k=4)
                    hi1, lo1, hi2, lo2 = (work[:, :, 4 * k:4 * k + 4] for k in range(4))
                    nc.vector.tensor_tensor(hi1, four[:, :, :, 0], four[:, :, :, 1], ALU.max)
                    nc.vector.tensor_tensor(lo1, four[:, :, :, 0], four[:, :, :, 1], ALU.min)
                    nc.vector.tensor_tensor(hi2, four[:, :, :, 2], four[:, :, :, 3], ALU.max)
                    step(nc.vector.tensor_tensor(lo2, four[:, :, :, 2], four[:, :, :, 3], ALU.min))
                    m1, m2, m3 = (work2[:, :, 4 * k:4 * k + 4] for k in range(3))
                    nc.vector.tensor_tensor(m1, hi1, hi2, ALU.max)
                    nc.vector.tensor_tensor(m2, hi1, hi2, ALU.min)
                    step(nc.vector.tensor_tensor(m3, lo1, lo2, ALU.max))
                    step(nc.vector.tensor_tensor(m2, m2, m3, ALU.max))
                    step(nc.vector.tensor_tensor(gsum[:], m1, m2, ALU.add))
                    of_j = gsum[:].unsqueeze(2).to_broadcast([P, NT, 4, 4])
                    of_i = gsum[:].unsqueeze(3).to_broadcast([P, NT, 4, 4])
                    nc.vector.tensor_tensor(work[:].rearrange("p t (i j) -> p t i j", j=4), of_j, of_i, ALU.is_ge)
                    step(nc.vector.tensor_tensor(work2[:].rearrange("p t (i j) -> p t i j", j=4), of_j, of_i, ALU.is_gt))
                    nc.vector.tensor_tensor(work[:], work[:], tri[:, 0:1, :].to_broadcast([P, NT, 16]), ALU.mult)
                    step(nc.vector.tensor_tensor(work2[:], work2[:], tri[:, 1:2, :].to_broadcast([P, NT, 16]), ALU.mult))
                    step(nc.vector.tensor_tensor(work[:], work[:], work2[:], ALU.add))
                    step(nc.vector.tensor_reduce(gsum[:], work[:].rearrange("p t (i j) -> p t i j", j=4), AX.X, ALU.add))
                    step(nc.vector.tensor_scalar(gsum[:], gsum[:], 2.0, None, ALU.is_lt))
                    step(nc.vector.tensor_tensor(four, four, gsum[:].unsqueeze(3).to_broadcast([P, NT, 4, 4]), ALU.mult))
                    step(nc.vector.tensor_scalar(ranked[:, :, 0:E], ranked[:, :, 0:E], 0.0, None, ALU.add))
                    rank()
                    find_top(top, mask[:])
                    step(nc.vector.tensor_tensor(mask[:], mask[:], scores[:], ALU.mult))
                    step(nc.vector.tensor_reduce(small[:, :, 0:1], mask[:], AX.X, ALU.add))
                    step(nc.vector.tensor_scalar(small[:, :, 0:1], small[:, :, 0:1], 1e-20, None, ALU.add))
                    step(nc.vector.reciprocal(small[:, :, 0:1], small[:, :, 0:1]))
                    step(nc.vector.tensor_tensor(mask[:], mask[:], wide(small[:, :, 0:1], E), ALU.mult))
                    nc.vector.tensor_scalar(g_tm[:, :, 0:E], mask[:], 2.5, None, ALU.mult)
                    nc.vector.memset(g_tm[:, :, E:E + 2], 1.0).then_inc(gates_ready, 1)
                elif kind == "softmax_top":
                    dve.wait_ge(logits_ready, 1)
                    step(nc.vector.tensor_tensor(scores[:], logits, bias[:].unsqueeze(1).to_broadcast([P, NT, E]), ALU.add))
                    step(nc.vector.tensor_reduce(small[:, :, 0:1], scores[:], AX.X, ALU.max))
                    nc.vector.tensor_tensor(scores[:], scores[:], wide(small[:, :, 0:1], E), ALU.subtract).then_inc(shifted, 1)
                    dve.wait_ge(exp_ready, 1)
                    step(nc.vector.tensor_reduce(small[:, :, 1:2], scores[:], AX.X, ALU.add))
                    step(nc.vector.reciprocal(small[:, :, 1:2], small[:, :, 1:2]))
                    step(nc.vector.tensor_tensor(ranked[:, :, 0:E], scores[:], wide(small[:, :, 1:2], E), ALU.mult))
                    rank()
                    find_top(top, mask[:])
                    nc.vector.tensor_tensor(g_tm[:, :, 0:E], mask[:], ranked[:, :, 0:E], ALU.mult)
                    nc.vector.memset(g_tm[:, :, E:E + 1], 1.0).then_inc(gates_ready, 1)
                else:
                    dve.wait_ge(logits_ready, 1)
                    step(nc.vector.tensor_copy(ranked[:, :, 0:E], logits))
                    rank()
                    nc.vector.tensor_tensor(small[:, :, 0:1], top8[:, :, 1:2], top8[:, :, 0:1], ALU.subtract).then_inc(shifted, 1)
                    dve.wait_ge(exp_ready, 1)
                    find_top(2, g_tm[:, :, 32:32 + E])
                    find_top(1, g_tm[:, :, 0:E])
                    step(nc.vector.tensor_tensor(g_tm[:, :, 32:32 + E], g_tm[:, :, 32:32 + E], g_tm[:, :, 0:E], ALU.subtract))
                    step(nc.vector.tensor_scalar(small[:, :, 2:3], small[:, :, 1:2], 1.0, None, ALU.add))
                    step(nc.vector.reciprocal(small[:, :, 2:3], small[:, :, 2:3]))
                    step(nc.vector.tensor_tensor(small[:, :, 3:4], small[:, :, 1:2], small[:, :, 2:3], ALU.mult))
                    nc.vector.tensor_tensor(g_tm[:, :, 64:64 + E], g_tm[:, :, 0:E], wide(small[:, :, 2:3], E), ALU.mult)
                    nc.vector.tensor_tensor(g_tm[:, :, 96:96 + E], g_tm[:, :, 32:32 + E], wide(small[:, :, 3:4], E), ALU.mult).then_inc(gates_ready, 1)

                dve.wait_ge(gates_t_psum, B)
                flat = core.psum[:, 0:4, :].rearrange("p b n -> p (b n)")
                if kind == "top_capacity":
                    step(nc.vector.memset(gates_t[:], 0.0))
                    for k in range(2):
                        nc.vector.tensor_copy(masks_t[:, k, :], flat[32 * k:32 * k + E, :])
                        nc.vector.tensor_copy(probs_t[:, k, :], flat[64 + 32 * k:64 + 32 * k + E, :])
                    step(nc.vector.memset(ones[:], 1.0))
                    step(nc.vector.tensor_tensor_scan(count[:, 0, :], ones[:], masks_t[:, 0, :], 0.0, ALU.mult, ALU.add))
                    step(nc.vector.tensor_tensor_scan(count[:, 1, :], ones[:], masks_t[:, 1, :], count[:, 0, N - 1:N], ALU.mult, ALU.add))
                    for k in range(2):
                        step(nc.vector.scalar_tensor_tensor(probs_t[:, k, :], count[:, k, :], float(capacity), probs_t[:, k, :], ALU.is_le, ALU.mult))
                    step(nc.vector.tensor_tensor(gates_t[0:E, :], probs_t[:, 0, :], probs_t[:, 1, :], ALU.add))
                else:
                    step(nc.vector.tensor_copy(gates_t[:], flat[0:32, :]))
                nc.vector.tensor_copy(gates3[0:32, :], gates_t[:])
                step(nc.vector.tensor_copy(part[:], gates_t[:]))
                step(nc.vector.tensor_tensor(rest[:], gates_t[:], part[:], ALU.subtract))
                nc.vector.tensor_copy(gates3[32:64, :], rest[:])
                step(nc.vector.tensor_copy(part[:], rest[:]))
                nc.vector.tensor_tensor(gates3[64:96, :], rest[:], part[:], ALU.subtract)


def ffn0(core):
    d = core.dram
    with Stage(core, "f0") as st:
        gt, g3 = st.sb("gates_t", [32, N]), st.sb("gates3", [GR, N], BF16)
        router(core, "r0", "sigmoid_groups", x=core.x, w_dram=d["l0_router"], n_experts=16, top=4, gates_t=gt, gates3=g3,
               bias_dram=d["l0_ebias"], tri_dram=d["c_tri"])
        experts(core, "e0", act_func=ACT.Silu, x=core.x, resid=core.x, gates_t=gt, gates3=g3, n_slots=9, unroll=3, tiles=1,
                w_dram=d["l0_experts"], glu=True)


def ffn1(core):
    d = core.dram
    with Stage(core, "f1") as st:
        gt, g3 = st.sb("gates_t", [32, N]), st.sb("gates3", [GR, N], BF16)
        capacity = int(2 * 1.25 * N / 8)
        capacity += capacity % 2
        router(core, "r1", "top_capacity", x=core.x, w_dram=d["l1_router"], n_experts=8, top=2, gates_t=gt, gates3=g3,
               capacity=capacity)
        experts(core, "e1", act_func=ACT.Gelu, x=core.x, resid=core.x, gates_t=gt, gates3=g3, n_slots=8, unroll=2, tiles=4,
                w_dram=d["l1_experts"])


def ffn3(core):
    d = core.dram
    with Stage(core, "f3") as st:
        gt, g3 = st.sb("gates_t", [32, N]), st.sb("gates3", [GR, N], BF16)
        b2 = st.sb("b2", [9, P])
        b2_loaded = st.sem("b2_loaded")
        with core.nc.Block() as block:
            @block.sync
            def _(sp):
                sp.dma_start(b2[:], d["l3_b2"]).then_inc(b2_loaded, 16)
                sp.wait_ge(b2_loaded, 16)
        router(core, "r3", "softmax_top", x=core.x, w_dram=d["l3_router"], n_experts=8, top=2, gates_t=gt, gates3=g3,
               bias_dram=d["l3_rbias"], hid_dram=d["l3_gw1"], hid_bias_dram=d["l3_gb1"])
        experts(core, "e3", act_func=ACT.Gelu_apprx_tanh, x=core.x, resid=core.x, gates_t=gt, gates3=g3, n_slots=9, unroll=3, tiles=2,
                w_dram=d["l3_experts"], with_b1=True, b2=b2, b2_rows=9)


def init_sum(core, name, src, bias_dram=None):
    nc = core.nc
    with Stage(core, name) as st:
        bias = st.sb("bias", [P, 1])
        loaded = st.sem("loaded")
        with nc.Block() as block:
            @block.sync
            def _(sp):
                if bias_dram is not None:
                    sp.dma_start(bias[:], bias_dram).then_inc(loaded, 16)

            @block.vector
            def _(dve):
                if bias_dram is None:
                    nc.vector.tensor_copy(core.sum[:], src[:])
                else:
                    dve.wait_ge(loaded, 16)
                    nc.vector.tensor_scalar(core.sum[:], src[:], bias[:], None, ALU.add)


def attention(core, name, *, x, iters, units, heads, q_rows, w_dram=None, tables=None, qk_bias=False, v_bias=None,
              w_static=None):
    nc = core.nc
    rope = w_dram is not None
    sets = 1 if rope else 2
    dv = P // heads
    slots = min(units, B)
    half = q_rows // 2
    groups = units // slots
    w_cols = 4 * P + (2 if qk_bias else 0) if rope else 6 * P
    ahead = 2 if rope else 1
    n_proj = 3 if rope else 5
    items = [(u, q, h) for u in range(units) for q in range(QT) for h in range(heads)]
    n_items, n_tiles = len(items), units * QT
    per_unit = QT * heads
    with Stage(core, name) as st:
        w_all = w_static if w_static is not None else st.sb("w", [P, groups, w_cols])
        xs = st.sb("xs", [P, T]) if not rope else None
        swapped = st.sb("swapped", [P, 2, T]) if rope else None
        rot = st.sb("rot", [P, 2, T]) if rope else None
        qs = st.sb("q", [P, slots, sets, T])
        ks = st.sb("k", [P, slots, sets, T])
        vs = st.sb("v", [P, slots, QT, P])
        probs = st.sb("probs", [P, 2, T])
        probs_t = st.sb("probs_t", [P, 2, QT, P])
        nmax = st.sb("nmax", [P, 4])
        rsum = st.sb("rsum", [P, QT, heads])
        rinv = st.sb("rinv", [P, QT, heads])
        y = st.sb("y", [P, 2, P])
        y_t = st.sb("y_t", [P, T])
        w_loaded = [st.sem(f"w{k}_loaded") for k in range(groups)]
        (swap_ready, sin_ready, x_ready, proj_ready, proj_out, qk_ready, s_ready, max_ready, probs_ready, pt_psum, pt_ready,
         y_psum, rinv_ready, y_ready, yt_psum, yt_ready, unit_done, sum_done, passed) = (st.sem(n) for n in (
             "swap_ready", "sin_ready", "x_ready", "proj_ready", "proj_out", "qk_ready", "s_ready", "max_ready", "probs_ready",
             "pt_psum", "pt_ready", "y_psum", "rinv_ready", "y_ready", "yt_psum", "yt_ready", "unit_done", "sum_done", "passed"))
        ps_s = [core.psum[:, k, :] for k in range(2)]
        ps_t = [core.psum[:, 2 + k, :] for k in range(2)]
        ps_y = core.psum[:, 4, 0:P]
        ps_o = core.psum[:, 5, :]
        ps_p = [core.psum[:, 6 + k, :] for k in range(2)]

        def rows(h):
            base = h * P // heads if rope else 32 * (h % 4)
            return slice(base, base + q_rows)

        def head_set(h):
            return 0 if rope else h // 4

        with nc.Block() as block:
            @block.sync
            def _(sp):
                if rope:
                    with sp.Fori(0, iters) as i:
                        for k in range(groups):
                            sp.wait_ge(unit_done, i * units + (k + 1) * slots)
                            sp.dma_start(w_all[:, k, :], w_dram[bass.ds(i * groups + k, 1)].rearrange("o p n -> p (o n)")).then_inc(w_loaded[k], 16)

            @block.gpsimd
            def _(pool):
                if rope:
                    pool.sem_inc(qk_ready, 2)
                with pool.Fori(0, iters) as i:
                    if not rope:
                        pool.wait_ge(unit_done, i * units + units)
                        pool.sem_inc(passed, 1)
                        nc.gpsimd.tensor_copy(xs[:], x[:, cols(i)]).then_inc(x_ready, 1)
                    else:
                        for u in range(units):
                            U = i * units + u
                            pool.wait_ge(unit_done, U + 1 + units - slots)
                            for j, to in enumerate((qs, ks)):
                                pool.wait_ge(swap_ready, 2 * U + j + 1)
                                nc.gpsimd.tensor_tensor(swapped[:, j, :], swapped[:, j, :], tables[:, 2 * j + 1, :], ALU.mult).then_inc(sin_ready, 1)
                                pool.wait_ge(sin_ready, 2 * U + j + 1)
                                pool.wait_ge(proj_out, n_proj * U + j + 1 + 1)
                                nc.gpsimd.tensor_tensor(to[:, u % slots, 0, :], rot[:, j, :], swapped[:, j, :], ALU.add).then_inc(qk_ready, 1)

            @block.tensor
            def _(pe):
                pe.sem_inc(unit_done, units)
                pe.sem_inc(pt_psum, 2)
                pe.sem_inc(y_psum, 2)
                pe.sem_inc(yt_psum, 2)
                with pe.Fori(0, iters) as i:
                    def x_of(u):
                        return x[:, (u % slots) * T:(u % slots + 1) * T] if rope else xs[:]

                    def w_of(u, k):
                        return w_all[:, u // slots, k * P:(k + 1) * P] if rope else w_all[:, k * P:(k + 1) * P]

                    def project(u, part):
                        U = i * units + u
                        if rope and part == 0 and u % slots == 0:
                            pe.wait_ge(w_loaded[u // slots], 16 * i + 16)
                        if part == 2:
                            pe.wait_ge(proj_out, n_proj * U + n_proj - 2 + 1)
                            for t in range(QT):
                                last = nc.tensor.matmul(ps_p[0][:, t * P:(t + 1) * P], x_of(u)[:, t * P:(t + 1) * P],
                                                        w_of(u, 2 if rope else 4), start=True, stop=True)
                            last.then_inc(proj_ready, 1)
                        elif rope:
                            pe.wait_ge(proj_out, n_proj * U + 1)
                            nc.tensor.matmul(ps_p[part], w_of(u, part), x_of(u), start=True, stop=True).then_inc(proj_ready, 1)
                        else:
                            for k in range(2):
                                n = 2 * part + k
                                pe.wait_ge(proj_out, n_proj * U + (0 if part == 0 else n - 1) + 1)
                                nc.tensor.matmul(ps_p[k], w_of(u, n), x_of(u), start=True, stop=True).then_inc(proj_ready, 1)

                    def scores(j):
                        u, q, h = items[j]
                        U, g = i * units + u, i * n_items + j
                        if q == 0 and h == 0:
                            if rope:
                                pe.wait_ge(qk_ready, 2 * U + 2 + 2)
                            else:
                                pe.wait_ge(proj_out, n_proj * U + 4 + 1)
                        pe.wait_ge(probs_ready, g + 1)
                        s = head_set(h)
                        nc.tensor.matmul(ps_s[j % 2][:, 0:(q + 1) * P], qs[rows(h), u % slots, s, q * P:(q + 1) * P],
                                         ks[rows(h), u % slots, s, 0:(q + 1) * P], start=True, stop=False)
                        nc.tensor.matmul(ps_s[j % 2][:, q * P:(q + 1) * P], core.identb[:], core.maskb[:],
                                         start=False, stop=True).then_inc(s_ready, 1)

                    def transpose(j):
                        u, q, h = items[j]
                        g = i * n_items + j
                        pe.wait_ge(probs_ready, g + 1 + 2)
                        pe.wait_ge(pt_ready, g + 1)
                        for k in range(q + 1):
                            last = nc.tensor.transpose(ps_t[j % 2][:, k * P:(k + 1) * P], probs[:, j % 2, k * P:(k + 1) * P], core.ident[:])
                        last.then_inc(pt_psum, 1)

                    def values(j):
                        u, q, h = items[j]
                        g = i * n_items + j
                        if q == 0 and h == 0:
                            pe.wait_ge(proj_out, n_proj * (i * units + u) + n_proj + 1)
                        if h == 0:
                            pe.wait_ge(y_ready, i * n_tiles + u * QT + q + 1)
                        pe.wait_ge(pt_ready, g + 1 + 2)
                        for k in range(q + 1):
                            last = nc.tensor.matmul(ps_y[:, h * dv:(h + 1) * dv], probs_t[:, j % 2, k, :], vs[:, u % slots, k, h * dv:(h + 1) * dv],
                                                    start=k == 0, stop=k == q)
                        last.then_inc(y_psum, 1)

                    def y_transpose(u, q):
                        if q == 0:
                            pe.wait_ge(sum_done, i * units + u + 1)
                        pe.wait_ge(y_ready, i * n_tiles + u * QT + q + 1 + 1)
                        nc.tensor.transpose(ps_o[:, q * P:(q + 1) * P], y[:, q % 2, :], core.ident[:]).then_inc(yt_psum, 1)

                    def out(u):
                        pe.wait_ge(yt_ready, i * units + u + 1)
                        nc.tensor.matmul(ps_o, w_of(u, 3 if rope else 5), y_t[:], start=True, stop=True).then_inc(unit_done, 1)

                    if not rope:
                        pe.wait_ge(x_ready, i + 1)
                    for u in range(min(ahead, units)):
                        for part in range(3):
                            project(u, part)
                    scores(0)
                    for j in range(n_items + 3):
                        if j + 1 < n_items:
                            scores(j + 1)
                        if j < n_items:
                            transpose(j)
                        if 1 <= j <= n_items:
                            values(j - 1)
                        if j >= 3 and (j - 3) % per_unit == per_unit - 1:
                            out(items[j - 3][0])
                        if j >= 2 and j - 2 < n_items and items[j - 2][2] == heads - 1:
                            y_transpose(*items[j - 2][:2])
                        if j < n_items and j % per_unit < 3 and items[j][0] + ahead < units:
                            project(items[j][0] + ahead, j % per_unit)

            @block.scalar
            def _(act):
                nc.scalar.preload_act_table_set("natural_log_exp_and_others")
                act.sem_inc(probs_ready, 2)
                with act.Fori(0, iters) as i:
                    def swap(u, part):
                        U = i * units + u
                        act.wait_ge(qk_ready, 2 * U + part + 1)
                        act.wait_ge(proj_ready, n_proj * U + part + 1)
                        for lo in range(0, P, half):
                            hi = lo + half if lo // half % 2 == 0 else lo - half
                            with_bias = {"bias": w_all[lo:lo + half, u // slots, 4 * P + part:4 * P + part + 1]} if qk_bias else {}
                            last = nc.scalar.activation(swapped[hi:hi + half, part, :], ps_p[part][lo:lo + half, :], ACT.Identity, **with_bias)
                        last.then_inc(swap_ready, 1)

                    if rope:
                        for u in range(ahead):
                            swap(u, 0)
                            swap(u, 1)
                    for j, (u, q, h) in enumerate(items):
                        g = i * n_items + j
                        act.wait_ge(max_ready, g + 1)
                        act.wait_ge(pt_psum, g + 1)
                        nc.scalar.activation(probs[:, j % 2, 0:(q + 1) * P], ps_s[j % 2][:, 0:(q + 1) * P], ACT.Exp,
                                             bias=nmax[:, j % 4:j % 4 + 1], accum_out=rsum[:, q, h:h + 1]).then_inc(probs_ready, 1)
                        if rope and 1 <= j % per_unit < 3 and u + ahead < units:
                            swap(u + ahead, j % per_unit - 1)

            @block.vector
            def _(dve):
                dve.sem_inc(proj_out, 1)
                dve.sem_inc(pt_ready, 2)
                dve.sem_inc(y_ready, 1)
                dve.sem_inc(sum_done, 1)
                with dve.Fori(0, iters) as i:
                    def project(u, part):
                        U = i * units + u
                        if part == 2:
                            dve.wait_ge(unit_done, U + 1 + units - slots)
                            dve.wait_ge(proj_ready, n_proj * U + n_proj)
                            to = vs[:, u % slots, :, :]
                            of = ps_p[0].rearrange("p (t d) -> p t d", d=P)
                            if v_bias is None:
                                nc.vector.tensor_copy(to, of).then_inc(proj_out, 1)
                            else:
                                nc.vector.tensor_tensor(to, of, v_bias[:, bass.ds((i * groups + u // slots) * P, P)].unsqueeze(1).to_broadcast([P, QT, P]),
                                                        ALU.add).then_inc(proj_out, 1)
                        elif rope:
                            dve.wait_ge(swap_ready, 2 * U + part + 1)
                            if not qk_bias:
                                nc.vector.tensor_tensor(rot[:, part, :], ps_p[part], tables[:, 2 * part, :], ALU.mult).then_inc(proj_out, 1)
                            else:
                                nc.vector.scalar_tensor_tensor(rot[:, part, :], ps_p[part], w_all[:, u // slots, 4 * P + part:4 * P + part + 1], tables[:, 2 * part, :],
                                                               ALU.add, ALU.mult).then_inc(proj_out, 1)
                        else:
                            dve.wait_ge(unit_done, U + 1)
                            for k in range(2):
                                n = 2 * part + k
                                dve.wait_ge(proj_ready, n_proj * U + n + 1)
                                nc.vector.tensor_copy((qs, ks)[part][:, u, k, :], ps_p[k]).then_inc(proj_out, 1)

                    def maximum(j):
                        u, q, h = items[j]
                        dve.wait_ge(s_ready, i * n_items + j + 1)
                        nc.vector.tensor_reduce(nmax[:, j % 4:j % 4 + 1], ps_s[j % 2][:, 0:(q + 1) * P], AX.X, ALU.max, negate=True).then_inc(max_ready, 1)

                    def copy_t(j):
                        u, q, h = items[j]
                        g = i * n_items + j
                        dve.wait_ge(pt_psum, g + 1 + 2)
                        dve.wait_ge(y_psum, g + 1)
                        nc.vector.tensor_copy(probs_t[:, j % 2, 0:q + 1, :].rearrange("p k n -> p (k n)"), ps_t[j % 2][:, 0:(q + 1) * P]).then_inc(pt_ready, 1)

                    def normalise(j):
                        u, q, h = items[j]
                        tile = i * n_tiles + u * QT + q
                        dve.wait_ge(y_psum, i * n_items + j + 1 + 2)
                        nc.vector.reciprocal(rinv[:, q, :], rsum[:, q, :]).then_inc(rinv_ready, 1)
                        dve.wait_ge(rinv_ready, tile + 1)
                        dve.wait_ge(yt_psum, tile + 1)
                        nc.vector.tensor_tensor(y[:, q % 2, :].rearrange("p (h d) -> p h d", h=heads), ps_y.rearrange("p (h d) -> p h d", h=heads),
                                                rinv[:, q, :].unsqueeze(2).to_broadcast([P, heads, dv]), ALU.mult).then_inc(y_ready, 1)

                    def copy_y(u):
                        U = i * units + u
                        dve.wait_ge(yt_psum, (U + 1) * QT + 2)
                        dve.wait_ge(unit_done, U + units)
                        nc.vector.tensor_copy(y_t[:], ps_o).then_inc(yt_ready, 1)

                    def add_out(u):
                        U = i * units + u
                        dve.wait_ge(unit_done, U + 1 + units)
                        dve.wait_ge(sum_done, U + 1)
                        to = core.sum[:, cols(u % slots if rope else i)]
                        nc.vector.tensor_tensor(to, ps_o, to, ALU.add).then_inc(sum_done, 1)

                    for u in range(min(ahead, units)):
                        for part in range(3):
                            project(u, part)
                    maximum(0)
                    for j in range(n_items + 3):
                        if j + 1 < n_items:
                            maximum(j + 1)
                        if j < n_items:
                            copy_t(j)
                        if j >= 3 and (j - 3) % per_unit == per_unit - 1:
                            add_out(items[j - 3][0])
                        if 1 <= j <= n_items and items[j - 1][2] == heads - 1:
                            normalise(j - 1)
                        if 2 <= j and (j - 2) % per_unit == per_unit - 1:
                            copy_y(items[j - 2][0])
                        if j < n_items and 1 <= j % per_unit < 4 and items[j][0] + ahead < units:
                            project(items[j][0] + ahead, j % per_unit - 1)


def attn2(core):
    nc = core.nc
    init_sum(core, "i2", core.x)
    with Stage(core, "a2t") as st:
        tables = st.sb("tables", [P, 4, T])
        loaded = st.sem("loaded")
        with nc.Block() as block:
            @block.sync
            def _(sp):
                sp.dma_start(tables[:], core.dram["c_rope2"]).then_inc(loaded, 16)
                sp.wait_ge(loaded, 16)
        attention(core, "a2", x=core.x, iters=4, units=2 * B, heads=1, q_rows=P, w_dram=core.dram["l2_heads"], tables=tables)


def attn1(core):
    nc = core.nc
    init_sum(core, "i1", core.x)
    with Stage(core, "a1w") as st:
        w = st.sb("w", [P, 6 * P])
        w3 = st.sb("w3", [24, 2, P])
        spread = st.sb("spread", [24, 2 * P])
        scale = st.sb("scale", [P, 1])
        loaded, wide_psum, wide_ready = (st.sem(n) for n in ("loaded", "wide_psum", "wide_ready"))
        with nc.Block() as block:
            @block.sync
            def _(sp):
                sp.dma_start(w3[:, 0, :], core.dram["l1_wq"]).then_inc(loaded, 16)
                sp.dma_start(w3[:, 1, :], core.dram["l1_wk"]).then_inc(loaded, 16)
                sp.dma_start(spread[:], core.dram["c_spread"]).then_inc(loaded, 16)
                sp.dma_start(scale[:], core.dram["l1_scale"].partition_broadcast(P)).then_inc(loaded, 16)
                sp.dma_start(w[:, 4 * P:6 * P], core.dram["l1_wvo"]).then_inc(loaded, 16)

            @block.tensor
            def _(pe):
                pe.wait_ge(loaded, 5 * 16)
                for k in range(2):
                    nc.tensor.matmul(core.psum[:, k, 0:2 * P], w3[:, k, :], spread[:], start=True, stop=True).then_inc(wide_psum, 1)

            @block.vector
            def _(dve):
                dve.wait_ge(loaded, 5 * 16)
                dve.wait_ge(wide_psum, 2)
                nc.vector.tensor_copy(w[:, 2 * P:4 * P], core.psum[:, 1, 0:2 * P])
                nc.vector.tensor_copy(w[:, 0:2 * P], core.psum[:, 0, 0:2 * P]).then_inc(wide_ready, 1)
                dve.wait_ge(wide_ready, 1)
                q3 = w[:, 0:2 * P].rearrange("p (h r) -> p h r", r=32)[:, :, 0:3]
                nc.vector.tensor_scalar(q3, q3, scale[:], None, ALU.mult)
        attention(core, "a1", x=core.x, iters=B, units=1, heads=8, q_rows=4, w_static=w)


def rope_tables(core, tables, theta_dram, scale):
    nc = core.nc
    two_pi = 2 * np.pi
    c1 = 6.28125
    c2 = float(np.float32(np.round((two_pi - c1) * 2 ** 22) / 2 ** 22))
    c3 = float(two_pi - c1 - c2)
    magic = 1.5 * 2 ** 23
    with Stage(core, "rt") as st:
        pos, ang, turns, sin_h = (st.sb(n, [P, T]) for n in ("pos", "ang", "turns", "sin_h"))
        col = st.sb("col", [P, 2])
        loaded, reduced, sin_ready, dve_step = (st.sem(n) for n in ("loaded", "reduced", "sin_ready", "dve_step"))
        sin = tables[:, 3, :]
        with nc.Block() as block:
            @block.sync
            def _(sp):
                sp.dma_start(pos[:], core.dram["c_pos"].partition_broadcast(P)).then_inc(loaded, 16)
                sp.dma_start(col[:, 0:1], theta_dram).then_inc(loaded, 16)
                sp.dma_start(col[:, 1:2], core.dram["c_ropesign"]).then_inc(loaded, 16)

            @block.scalar
            def _(act):
                act.wait_ge(reduced, 1)
                nc.scalar.activation(sin, ang[:], ACT.Sin).then_inc(sin_ready, 1)
                nc.scalar.activation(sin_h[:], ang[:], ACT.Sin, scale=0.5).then_inc(sin_ready, 1)

            @block.vector
            def _(dve):
                step = Steps(dve, dve_step)
                dve.wait_ge(loaded, 3 * 16)
                step(nc.vector.tensor_scalar(ang[:], pos[:], col[:, 0:1], None, ALU.mult))
                step(nc.vector.tensor_scalar(turns[:], ang[:], 1 / two_pi, None, ALU.mult))
                step(nc.vector.tensor_scalar(turns[:], turns[:], magic, None, ALU.add))
                step(nc.vector.tensor_scalar(turns[:], turns[:], magic, None, ALU.subtract))
                for c in (c1, c2, c3):
                    step(nc.vector.scalar_tensor_tensor(ang[:], turns[:], -c, ang[:], ALU.mult, ALU.add))
                nc.vector.tensor_scalar(ang[:], ang[:], 3.1415925, -3.1415925, ALU.min, ALU.max).then_inc(reduced, 1)
                dve.wait_ge(sin_ready, 2)
                step(nc.vector.tensor_scalar(sin, sin, col[:, 1:2], None, ALU.mult))
                step(nc.vector.tensor_tensor(sin_h[:], sin_h[:], sin_h[:], ALU.mult))
                step(nc.vector.tensor_scalar(tables[:, 2, :], sin_h[:], -2.0, 1.0, ALU.mult, ALU.add))
                nc.vector.tensor_scalar(tables[:, 0:2, :], tables[:, 2:4, :], scale, None, ALU.mult)


def ffn2(core):
    nc, d = core.nc, core.dram
    with Stage(core, "f2") as st:
        xn = st.sb("xn", [P, N])
        gammas = st.sb("gammas", [P, 2])
        loaded = st.sem("loaded")
        with nc.Block() as block:
            @block.sync
            def _(sp):
                sp.dma_start(gammas[:], d["l2_gammas"]).then_inc(loaded, 16)
                sp.wait_ge(loaded, 16)
        norm(core, "g1", core.x, xn, False, 0, gammas[:, 0:1])
        init_sum(core, "if2", xn, d["l2_ob"])
        with Stage(core, "a2f") as sa:
            tables = sa.sb("tables", [P, 4, T])
            v_bias = sa.sb("v_bias", [P, 8 * P])
            b_loaded = sa.sem("b_loaded")
            rope_tables(core, tables, d["l2_theta"], 64 ** -0.5)
            with nc.Block() as block:
                @block.sync
                def _(sp):
                    sp.dma_start(v_bias[:], d["l2_vb"].partition_broadcast(P)).then_inc(b_loaded, 16)
                    sp.wait_ge(b_loaded, 16)
            attention(core, "h2", x=xn, iters=4, units=2 * B, heads=2, q_rows=64, w_dram=d["l2f_heads"], tables=tables,
                      qk_bias=True, v_bias=v_bias)
        an = st.sb("an", [P, N])
        norm(core, "g2", core.sum, an, False, 0, gammas[:, 1:2])
        added = st.sem("added")
        with nc.Block() as block:
            @block.vector
            def _(dve):
                nc.vector.tensor_tensor(xn[:], an[:], core.sum[:], ALU.add).then_inc(added, 1)
                dve.wait_ge(added, 1)
                nc.vector.tensor_tensor(xn[:], xn[:], core.x[:], ALU.add)
        gt, g3 = st.sb("gates_t", [32, N]), st.sb("gates3", [GR, N], BF16)
        b2 = st.sb("b2", [32, P])
        b2_loaded = st.sem("b2_loaded")
        with nc.Block() as block:
            @block.sync
            def _(sp):
                sp.dma_start(b2[:], d["l2_b2"]).then_inc(b2_loaded, 16)
                sp.wait_ge(b2_loaded, 16)
        router(core, "r2", "softmax_top", x=an, w_dram=d["l2_router"], n_experts=31, top=3, gates_t=gt, gates3=g3,
               bias_dram=d["l2_rbias"])
        experts(core, "e2", act_func=ACT.Gelu, x=an, resid=xn, gates_t=gt, gates3=g3, n_slots=32, unroll=2, tiles=1,
                w_dram=d["l2_experts"], with_b1=True, b2=b2, b2_rows=32)


def hawk(core):
    nc, d = core.nc, core.dram
    with Stage(core, "h3") as st:
        xn = st.sb("xn", [P, N])
        x2 = st.sb("x2", [P, N])
        gammas = st.sb("gammas", [P, 2])
        loaded = st.sem("loaded")
        with nc.Block() as block:
            @block.sync
            def _(sp):
                sp.dma_start(gammas[:], d["l3_gammas"]).then_inc(loaded, 16)
                sp.wait_ge(loaded, 16)
        norm(core, "g3", core.x, xn, False, 2, gammas[:, 0:1])
        recurrence(core, xn, x2)
        norm(core, "g4", x2, xn, False, 2, gammas[:, 1:2])
        gated_mlp(core, xn, x2)


def recurrence(core, xn, x2):
    nc, d = core.nc, core.dram
    K = 4
    C = 2
    with Stage(core, "rc") as st:
        w_in = st.sb("w_in", [P, 4 * P])
        w_g = st.sb("w_g", [P, C, 4 * P])
        w_out = st.sb("w_out", [P, C, P])
        taps = st.sb("taps", [P, C, K])
        cols_ = st.sb("cols", [P, 8])
        coef = st.sb("coef", [P, C])
        small = st.sb("small", [P, 6, C])
        gate = st.sb("gate", [P, C, T])
        padded = st.sb("padded", [P, C, K - 1 + T])
        xc, alpha, inp, beta, h = (st.sb(n, [P, C, T]) for n in ("xc", "alpha", "inp", "beta", "h"))
        (loaded, abs_ready, u_ready, coef_ready, z_ready, gate_ready, conv_ready, g_ready, sig_ready, alpha_ready,
         sq_ready, rest_ready, ln_ready, beta_ready, scan_ready, h_ready, out_ready, chunk_done, dve_step) = (st.sem(n) for n in (
             "loaded", "abs_ready", "u_ready", "coef_ready", "z_ready", "gate_ready", "conv_ready", "g_ready", "sig_ready",
             "alpha_ready", "sq_ready", "rest_ready", "ln_ready", "beta_ready", "scan_ready", "h_ready", "out_ready", "chunk_done", "dve_step"))
        bank = [core.psum[:, k, :] for k in range(8)]
        loads = [(w_in[:], d["l3_win"]), (w_g[:], d["l3_wgates"]), (w_out[:], d["l3_wout"]), (taps[:], d["l3_taps"]), (cols_[:], d["l3_cols"])]
        DVE_STEPS = 4 + 1 + 1

        with nc.Block() as block:
            @block.sync
            def _(sp):
                for to, of in loads:
                    sp.dma_start(to, of).then_inc(loaded, 16)

            @block.tensor
            def _(pe):
                pe.wait_ge(loaded, 16 * len(loads))
                with pe.Fori(0, B) as c:
                    pe.wait_ge(chunk_done, c + 1)
                    for k in range(4):
                        nc.tensor.matmul(bank[k], w_in[:, k * P:(k + 1) * P], xn[:, cols(c)], start=True, stop=True).then_inc(z_ready, 1)
                    pe.wait_ge(conv_ready, c + 1)
                    for m in range(4):
                        for k in range(C):
                            last = nc.tensor.matmul(bank[4 + m], w_g[:, k, m * P:(m + 1) * P], xc[:, k, :], start=k == 0, stop=k == C - 1)
                        last.then_inc(g_ready, 1)
                    pe.wait_ge(h_ready, c + 1)
                    for k in range(C):
                        last = nc.tensor.matmul(bank[0], w_out[:, k, :], h[:, k, :], start=k == 0, stop=k == C - 1)
                    last.then_inc(out_ready, 1)

            @block.scalar
            def _(act):
                act.wait_ge(loaded, 16 * len(loads))
                nc.scalar.activation(small[:, 0, :], cols_[:, 6:8], ACT.Abs).then_inc(abs_ready, 1)
                act.wait_ge(abs_ready, 1)
                nc.scalar.activation(small[:, 1, :], small[:, 0, :], ACT.Exp, scale=-1.0).then_inc(u_ready, 1)
                act.wait_ge(coef_ready, 1)
                with act.Fori(0, B) as c:
                    for k in range(C):
                        act.wait_ge(z_ready, 4 * c + k + 1)
                        nc.scalar.activation(gate[:, k, :], bank[k], ACT.Gelu).then_inc(gate_ready, 1)
                    for m in range(4):
                        act.wait_ge(g_ready, 4 * c + m + 1)
                        to = alpha[:, m, :] if m < C else inp[:, m - C, :]
                        nc.scalar.activation(to, bank[4 + m], ACT.Sigmoid, bias=cols_[:, 2 + m:3 + m]).then_inc(sig_ready, 1)
                    nc.scalar.preload_act_table_set("natural_log_exp_and_others")
                    act.wait_ge(sig_ready, 4 * c + 4)
                    for k in range(C):
                        nc.scalar.activation(alpha[:, k, :], alpha[:, k, :], ACT.Exp, scale=coef[:, k:k + 1]).then_inc(alpha_ready, 1)
                    for k in range(C):
                        act.wait_ge(alpha_ready, 2 * c + k + 1)
                        nc.scalar.activation(beta[:, k, :], alpha[:, k, :], ACT.Square).then_inc(sq_ready, 1)
                    act.wait_ge(rest_ready, c + 1)
                    nc.scalar.activation(beta[:], beta[:], ACT.Ln, bias=core.eps[:, 1:2]).then_inc(ln_ready, 1)
                    act.wait_ge(ln_ready, c + 1)
                    nc.scalar.activation(beta[:], beta[:], ACT.Exp, scale=0.5).then_inc(beta_ready, 1)

            @block.vector
            def _(dve):
                u, s, s2, p, pos = (small[:, k, :] for k in range(1, 6))
                dve.sem_inc(chunk_done, 1)
                dve.wait_ge(loaded, 16 * len(loads))
                dve.wait_ge(u_ready, 1)
                pre = Steps(dve, dve_step)
                pre(nc.vector.tensor_scalar(s2, u, 2.0, None, ALU.add))
                pre(nc.vector.reciprocal(s2, s2))
                pre(nc.vector.tensor_tensor(s, u, s2, ALU.mult))
                pre(nc.vector.tensor_tensor(s2, s, s, ALU.mult))
                pre(nc.vector.memset(p, 1 / 19))
                for n in range(17, 0, -2):
                    pre(nc.vector.tensor_tensor(p, p, s2, ALU.mult))
                    pre(nc.vector.tensor_scalar(p, p, 1 / n, None, ALU.add))
                pre(nc.vector.tensor_tensor(p, p, s, ALU.mult))
                pre(nc.vector.tensor_scalar(p, p, 2.0, None, ALU.mult))
                pre(nc.vector.tensor_scalar(pos, cols_[:, 6:8], 0.0, None, ALU.max))
                pre(nc.vector.tensor_tensor(p, p, pos, ALU.add))
                nc.vector.tensor_scalar(coef[:], p, -8.0, None, ALU.mult).then_inc(coef_ready, 1)
                pre(nc.vector.memset(padded[:, :, 0:K - 1], 0.0))
                before = pre.n
                with dve.Fori(0, B) as c:
                    step = Steps(dve, dve_step, c * DVE_STEPS + before)
                    for k in range(C):
                        dve.wait_ge(z_ready, 4 * c + 2 + k + 1)
                        last = nc.vector.tensor_copy(padded[:, k, K - 1:], bank[2 + k])
                    step(last)
                    for t in range(K):
                        for k in range(C):
                            seen = padded[:, k, t:t + T]
                            if t == 0:
                                last = nc.vector.tensor_scalar(xc[:, k, :], seen, taps[:, k, 0:1], cols_[:, k:k + 1], ALU.mult, ALU.add)
                            else:
                                last = nc.vector.scalar_tensor_tensor(xc[:, k, :], seen, taps[:, k, t:t + 1], xc[:, k, :], ALU.mult, ALU.add)
                        if t < K - 1:
                            step(last)
                    last.then_inc(conv_ready, 1)
                    dve.wait_ge(sq_ready, 2 * c + 2)
                    nc.vector.tensor_scalar(beta[:], beta[:], -1.0, 1.0, ALU.mult, ALU.add).then_inc(rest_ready, 1)
                    dve.wait_ge(sig_ready, 4 * c + 4)
                    step(nc.vector.tensor_tensor(inp[:], inp[:], xc[:], ALU.mult))
                    dve.wait_ge(beta_ready, c + 1)
                    step(nc.vector.tensor_tensor(inp[:], inp[:], beta[:], ALU.mult))
                    dve.wait_ge(gate_ready, 2 * c + 2)
                    for k in range(C):
                        last = nc.vector.tensor_tensor_scan(h[:, k, :], alpha[:, k, :], inp[:, k, :], 0.0, ALU.mult, ALU.add)
                    assert step.n == DVE_STEPS, step.n
                    last.then_inc(scan_ready, 1)
                    dve.wait_ge(scan_ready, c + 1)
                    nc.vector.tensor_tensor(h[:], h[:], gate[:], ALU.mult).then_inc(h_ready, 1)
                    dve.wait_ge(out_ready, c + 1)
                    nc.vector.tensor_tensor(x2[:, cols(c)], bank[0], core.x[:, cols(c)], ALU.add).then_inc(chunk_done, 1)


def gated_mlp(core, xn, x2):
    nc, d = core.nc, core.dram
    C = 2
    with Stage(core, "gm") as st:
        w_grow = st.sb("w_grow", [P, 4 * P])
        w_shrink = st.sb("w_shrink", [P, C, P])
        gate = st.sb("gate", [P, C, T])
        both = st.sb("both", [P, T])
        loaded, z_ready, gate_ready, prod_ready, out_ready, both_ready, chunk_done = (st.sem(n) for n in (
            "loaded", "z_ready", "gate_ready", "prod_ready", "out_ready", "both_ready", "chunk_done"))
        bank = [core.psum[:, k, :] for k in range(8)]
        with nc.Block() as block:
            @block.sync
            def _(sp):
                sp.dma_start(w_grow[:], d["l3_wgrow"]).then_inc(loaded, 16)
                sp.dma_start(w_shrink[:], d["l3_wshrink"]).then_inc(loaded, 16)

            @block.gpsimd
            def _(pool):
                with pool.Fori(0, B) as c:
                    pool.wait_ge(chunk_done, c + 1)
                    nc.gpsimd.tensor_tensor(both[:], core.x[:, cols(c)], x2[:, cols(c)], ALU.add).then_inc(both_ready, 1)

            @block.tensor
            def _(pe):
                pe.wait_ge(loaded, 32)
                with pe.Fori(0, B) as c:
                    pe.wait_ge(chunk_done, c + 1)
                    for k in range(4):
                        nc.tensor.matmul(bank[k], w_grow[:, k * P:(k + 1) * P], xn[:, cols(c)], start=True, stop=True).then_inc(z_ready, 1)
                    for k in range(C):
                        pe.wait_ge(prod_ready, 2 * c + k + 1)
                        last = nc.tensor.matmul(bank[4], w_shrink[:, k, :], gate[:, k, :], start=k == 0, stop=k == C - 1)
                    last.then_inc(out_ready, 1)

            @block.scalar
            def _(act):
                with act.Fori(0, B) as c:
                    for k in range(C):
                        act.wait_ge(z_ready, 4 * c + k + 1)
                        nc.scalar.activation(gate[:, k, :], bank[k], ACT.Gelu).then_inc(gate_ready, 1)

            @block.vector
            def _(dve):
                dve.sem_inc(chunk_done, 1)
                with dve.Fori(0, B) as c:
                    for k in range(C):
                        dve.wait_ge(gate_ready, 2 * c + k + 1)
                        dve.wait_ge(z_ready, 4 * c + 2 + k + 1)
                        nc.vector.tensor_tensor(gate[:, k, :], gate[:, k, :], bank[2 + k], ALU.mult).then_inc(prod_ready, 1)
                    dve.wait_ge(both_ready, c + 1)
                    dve.wait_ge(out_ready, c + 1)
                    nc.vector.tensor_tensor(core.sum[:, cols(c)], bank[4], both[:], ALU.add).then_inc(chunk_done, 1)


def post_norm(core, name):
    norm(core, name, core.sum, core.x, True, 0)
    recycle(core)


def build_program(nc, dram):
    with ExitStack() as ctx:
        core = Core(nc, ctx, dram)
        load_start(core)
        window_attention(core)
        post_norm(core, "n0a")
        ffn0(core)
        post_norm(core, "n0f")
        attn1(core)
        post_norm(core, "n1a")
        ffn1(core)
        post_norm(core, "n1f")
        attn2(core)
        post_norm(core, "n2a")
        ffn2(core)
        post_norm(core, "n2f")
        hawk(core)
        post_norm(core, "n3a")
        ffn3(core)
        post_norm(core, "n3f")
        store_end(core)


def arrays(i):
    f = np.float32
    d = {}
    c = np.ascontiguousarray
    eye = np.eye(128, dtype=f)
    idx = np.arange(128)
    d["c_ident"] = eye
    d["c_mean_w"] = np.full((128, 128), 1 / 128, f)
    d["c_center_w"] = (eye - f(1 / 128)).astype(f)
    d["c_eps"] = np.tile(np.array([1e-5, 1e-6, 0, 0], f), (128, 1))
    d["c_mask"] = np.where(idx[None, :] > idx[:, None], f(-1e30), f(0)).astype(f)
    d["c_headmask"] = ((idx[:, None] % 32) // 8 == np.arange(4)[None, :]).astype(f)
    d["c_wmask"] = np.where(np.arange(32)[None, :] > (idx[:, None] % 32), f(-1e30), f(0)).astype(f)
    d["l0_wqkv"] = i["L0_attn_w_qkv"]
    d["l0_wproj"] = i["L0_attn_w_proj"]
    d["l0_lnw"] = i["L0_attn_ln_w"].reshape(128, 1)
    d["c_sel"] = (np.arange(96)[:, None] % 32 == np.arange(32)[None, :]).astype(f)
    pair = (np.arange(96)[:, None, None] % 32 == 2 * np.arange(9)[:, None] + idx[None, :] // 64)
    d["c_selpair"] = pair.astype(f).reshape(96, 9 * 128)
    ij = np.arange(16)
    tri = np.stack([ij % 4 < ij // 4, ij % 4 > ij // 4]).astype(f)
    d["c_tri"] = np.broadcast_to(tri, (128, 2, 16))

    def pairs(w, shared):
        return np.concatenate([w.reshape(8, 128, 128).transpose(0, 2, 1), shared.T[None]])
    down = np.concatenate([i["L0_ffn_down_w"].transpose(0, 2, 1).reshape(8, 128, 128), i["L0_ffn_sh_down_w"].T[None]])
    d["l0_experts"] = np.concatenate([pairs(i["L0_ffn_gate_w"], i["L0_ffn_sh_gate_w"]),
                                      pairs(i["L0_ffn_up_w"], i["L0_ffn_sh_up_w"]), down], axis=2)
    d["l0_router"] = i["L0_ffn_router_weight"].T.reshape(128, 1, 16)
    d["l0_ebias"] = i["L0_ffn_e_bias"]

    def two_layers(w1, w2):
        e, dim, hid = w1.shape
        w2 = w2.reshape(e, hid // 128, 128, dim).transpose(0, 2, 1, 3).reshape(e, 128, hid)
        return np.concatenate([w1, w2], axis=2)
    d["l1_experts"] = two_layers(i["L1_ffn_c_fc"], i["L1_ffn_c_proj"])
    d["l1_router"] = i["L1_ffn_w_g"].reshape(128, 1, 8)
    d["l2_experts"] = np.concatenate([np.concatenate([
        two_layers(i["L2_ffn_re_w1"], i["L2_ffn_re_w2"]), two_layers(i["L2_ffn_sh_w1"][None], i["L2_ffn_sh_w2"][None])]),
        np.concatenate([i["L2_ffn_re_b1"], i["L2_ffn_sh_b1"][None]])[:, :, None]], axis=2)
    d["l2_b2"] = np.concatenate([i["L2_ffn_re_b2"], i["L2_ffn_sh_b2"][None]])
    d["l2_router"] = i["L2_ffn_router_w"].reshape(128, 1, 31)
    d["l2_rbias"] = i["L2_ffn_router_b"]
    d["l3_experts"] = np.concatenate([np.concatenate([
        two_layers(i["L3_ffn_We1"], i["L3_ffn_We2"]), two_layers(i["L3_ffn_Ws1"][None], i["L3_ffn_Ws2"][None])]),
        np.concatenate([i["L3_ffn_be1"], i["L3_ffn_bs1"][None]]).reshape(9, 2, 128).transpose(0, 2, 1)], axis=2)
    d["l3_b2"] = np.concatenate([i["L3_ffn_be2"], i["L3_ffn_bs2"][None]])
    d["l3_gw1"] = i["L3_ffn_gw1"]
    d["l3_gb1"] = i["L3_ffn_gb1"].reshape(2, 128).T
    d["l3_router"] = i["L3_ffn_gw2"].reshape(2, 128, 8).transpose(1, 0, 2)
    d["l3_rbias"] = i["L3_ffn_gb2"]

    wq, wk, wv = (i["L2_attn_w_a" + n].transpose(1, 0, 2) for n in "qkv")
    d["l2_heads"] = np.concatenate([wq, wk, wv, i["L2_attn_w_ao"]], axis=2)
    freqs = np.power(f(10000.0), -np.arange(64, dtype=f) / f(64)).astype(f)
    angles = (np.arange(512, dtype=f)[None, :] * freqs[:, None]).astype(f)
    cos, sin = np.cos(angles).astype(f), np.sin(angles).astype(f)
    cos, sin = np.concatenate([cos, cos]), np.concatenate([-sin, sin])
    d["c_rope2"] = np.stack([cos / f(128), sin / f(128), cos, sin], axis=1)
    signs = np.array([[a, b, e] for a in (-1, 1) for b in (-1, 1) for e in (-1, 1)], f)
    dirs = signs / np.linalg.norm(signs, axis=1, keepdims=True)
    spread = np.zeros((24, 256), f)
    for h in range(8):
        at = 128 * (h // 4) + 32 * (h % 4)
        spread[3 * h:3 * h + 3, at:at + 3] = np.eye(3)
        spread[3 * h:3 * h + 3, at + 3] = dirs[h]
    d["c_spread"] = spread
    d["l1_wq"], d["l1_wk"] = i["L1_attn_Wq"], i["L1_attn_Wk"]
    d["l1_scale"] = i["L1_attn_scale"].reshape(1)
    d["l1_wvo"] = np.concatenate([i["L1_attn_Wv"].T, i["L1_attn_Wo"].T], axis=1)

    def even_odd(w):
        w = w.reshape(w.shape[:-1] + (16, 32, 2)).swapaxes(-1, -2)
        return w.reshape(w.shape[:-3] + (8, 128))
    parts = [even_odd(i["L2_ffn_q_w"]), even_odd(i["L2_ffn_k_w"]), i["L2_ffn_v_w"].reshape(128, 8, 128)]
    d["l2f_heads"] = np.concatenate([w.transpose(1, 0, 2) for w in parts] + [
        i["L2_ffn_o_w"].reshape(8, 128, 128), even_odd(i["L2_ffn_q_b"])[:, :, None], even_odd(i["L2_ffn_k_b"])[:, :, None]], axis=2)
    d["l2_vb"] = i["L2_ffn_v_b"]
    d["l2_ob"] = i["L2_ffn_o_b"].reshape(128, 1)
    d["l2_gammas"] = np.stack([i["L2_ffn_gamma1"], i["L2_ffn_gamma2"]], axis=1)
    d["l2_theta"] = np.tile(i["L2_ffn_theta"], 4).reshape(128, 1)
    d["c_pos"] = np.arange(512, dtype=f)
    d["c_ropesign"] = np.where(idx % 64 < 32, f(-1), f(1)).astype(f).reshape(128, 1)

    d["l3_gammas"] = np.stack([i["L3_attn_gamma1"], i["L3_attn_gamma2"]], axis=1)
    d["l3_win"] = i["L3_attn_W_in"].T
    d["l3_wgates"] = i["L3_attn_W_gates"].T.reshape(2, 128, 512).transpose(1, 0, 2)
    d["l3_wout"] = i["L3_attn_W_out"].T.reshape(2, 128, 128).transpose(1, 0, 2)
    d["l3_taps"] = i["L3_attn_conv_w"].reshape(2, 128, 4).transpose(1, 0, 2)
    d["l3_cols"] = np.concatenate([i["L3_attn_conv_b"].reshape(2, 128), i["L3_attn_b_gates"].reshape(4, 128),
                                   i["L3_attn_forget_base"].reshape(2, 128)]).T
    d["l3_wgrow"] = i["L3_attn_W_grow"].T
    d["l3_wshrink"] = i["L3_attn_W_shrink"].T.reshape(2, 128, 128).transpose(1, 0, 2)
    return {k: c(v) for k, v in d.items()}


def kernel(**inputs):
    import concourse.bacc as bacc
    from concourse.bass_utils import run_bass_kernel_spmd

    inputs = {name: np.asarray(a) for name, a in inputs.items()}
    laid = arrays(inputs)
    laid["x"] = np.ascontiguousarray(inputs["L0_attn_x"].reshape(N, P))
    nc = bacc.Bacc("TRN2", target_bir_lowering=False, num_devices=1)
    dram = {name: nc.dram_tensor(f"in_{name}", a.shape, mybir.dt.from_np(a.dtype), kind="ExternalInput").ap() for name, a in laid.items()}
    dram["out"] = nc.dram_tensor("out_tokens", (N, P), F32, kind="ExternalOutput").ap()
    build_program(nc, dram)
    result = run_bass_kernel_spmd(nc, [{f"in_{name}": a for name, a in laid.items()}], core_ids=[0])
    return result.results[0]["out_tokens"].reshape(B, T, P)
```

```python
from contextlib import ExitStack

import numpy as np
import concourse.bass as bass
from concourse import mybir

F32 = mybir.dt.float32
BF16 = mybir.dt.bfloat16
F32R = mybir.dt.float32r
ACT = mybir.ActivationFunctionType
ALU = mybir.AluOpType
AX = mybir.AxisListType

P = 128
B = 4
T = 512
N = B * T
NT = N // P
QT = T // P
NEG = -1.0e30


def cols(c, n=T):
    return bass.ds(c * n, n)


class Stage:

    def __init__(self, core, name):
        self.core, self.nc, self.name = core, core.nc, name
        self.ctx = ExitStack()
        self.sems = []

    def __enter__(self):
        self.ctx.__enter__()
        return self

    def __exit__(self, *e):
        self.core.spent += self.sems
        return self.ctx.__exit__(*e)

    def sb(self, name, shape, dtype=F32):
        return self.ctx.enter_context(self.nc.sbuf_tensor(f"{self.name}_{name}", shape, dtype))

    def sem(self, name):
        self.sems.append(self.nc.alloc_semaphore(f"{self.name}_{name}"))
        return self.sems[-1]


class Steps:

    def __init__(self, engine, sem, base=0):
        self.engine, self.sem, self.base, self.n = engine, sem, base, 0

    def __call__(self, instruction):
        self.n += 1
        instruction.then_inc(self.sem, 1)
        self.engine.wait_ge(self.sem, self.base + self.n)


class Core:

    def __init__(self, nc, ctx, dram):
        self.nc, self.dram = nc, dram
        self.spent = []

        def sb(name, shape, dtype=F32):
            return ctx.enter_context(nc.sbuf_tensor(name, shape, dtype))

        self.x = sb("x_fm", [P, N])
        self.sum = sb("sum_fm", [P, N])
        self.psum = ctx.enter_context(nc.psum_tensor("psum", [P, 8, T], F32))
        self.ident = sb("ident", [P, P])
        self.mean_w = sb("mean_w", [P, P])
        self.center_w = sb("center_w", [P, P])
        self.eps = sb("eps", [P, 4])
        self.identb = sb("identb", [P, P], BF16)
        self.maskb = sb("maskb", [P, P], BF16)


def recycle(core):
    core.nc.clear_and_free_semaphores(core.spent)
    core.nc.all_engine_barrier()
    core.spent = []


def load_start(core):
    nc, dram = core.nc, core.dram
    with Stage(core, "load") as st:
        xt = st.sb("x_tm", [P, NT, P])
        idf = st.sb("maskf", [P, P])
        x_loaded, consts_loaded, tiles_ready = (st.sem(n) for n in ("x_loaded", "consts_loaded", "tiles_ready"))
        with nc.Block() as block:
            @block.sync
            def _(sp):
                sp.dma_start(xt[:], dram["x"].rearrange("(t p) c -> p t c", p=P)).then_inc(x_loaded, 16)
                for to, name in ((core.ident, "c_ident"), (core.mean_w, "c_mean_w"), (core.center_w, "c_center_w"), (core.eps, "c_eps")):
                    sp.dma_start(to[:], dram[name]).then_inc(consts_loaded, 16)
                sp.dma_start(idf[:], dram["c_mask"]).then_inc(consts_loaded, 16)

            @block.tensor
            def _(pe):
                pe.wait_ge(consts_loaded, 5 * 16)
                pe.wait_ge(x_loaded, 16)
                for b in range(B):
                    for q in range(QT):
                        last = nc.tensor.transpose(core.psum[:, b, q * P:(q + 1) * P], xt[:, b * QT + q, :], core.ident[:])
                    last.then_inc(tiles_ready, 1)

            @block.vector
            def _(dve):
                dve.wait_ge(consts_loaded, 5 * 16)
                nc.vector.tensor_copy(core.identb[:], core.ident[:])
                nc.vector.tensor_copy(core.maskb[:], idf[:])
                for b in range(B):
                    dve.wait_ge(tiles_ready, b + 1)
                    nc.vector.tensor_copy(core.x[:, cols(b)], core.psum[:, b, :])


def norm(core, name, src, dst, center, eps_col, gamma=None):
    nc = core.nc
    with Stage(core, name) as st:
        sq = st.sb("sq", [P, 2, T])
        lnv = st.sb("lnv", [P, 2, T])
        rs = st.sb("rs", [P, 2, T])
        centered, squared, var_ready, ln_ready, rs_ready, out_ready = (
            st.sem(n) for n in ("centered", "squared", "var_ready", "ln_ready", "rs_ready", "out_ready"))
        xc = [core.psum[:, b, :] for b in range(4)]
        var = [core.psum[:, 4 + b, :] for b in range(4)]
        with nc.Block() as block:
            @block.tensor
            def _(pe):
                if center:
                    for b in range(B):
                        nc.tensor.matmul(xc[b], core.center_w[:], src[:, cols(b)], start=True, stop=True).then_inc(centered, 1)
                for b in range(B):
                    pe.wait_ge(squared, b + 1)
                    nc.tensor.matmul(var[b], core.mean_w[:], sq[:, b % 2, :], start=True, stop=True).then_inc(var_ready, 1)

            @block.scalar
            def _(act):
                def square(b):
                    if center:
                        act.wait_ge(centered, b + 1)
                    if b >= 2:
                        act.wait_ge(var_ready, b - 1)
                    nc.scalar.activation(sq[:, b % 2, :], xc[b] if center else src[:, cols(b)], ACT.Square).then_inc(squared, 1)

                nc.scalar.preload_act_table_set("natural_log_exp_and_others")
                square(0)
                for b in range(B):
                    if b + 1 < B:
                        square(b + 1)
                    act.wait_ge(var_ready, b + 1)
                    nc.scalar.activation(lnv[:, b % 2, :], var[b], ACT.Ln, bias=core.eps[:, eps_col:eps_col + 1]).then_inc(ln_ready, 1)
                    act.wait_ge(ln_ready, b + 1)
                    if b >= 2:
                        act.wait_ge(out_ready, b - 1)
                    nc.scalar.activation(rs[:, b % 2, :], lnv[:, b % 2, :], ACT.Exp, scale=-0.5).then_inc(rs_ready, 1)

            @block.vector
            def _(dve):
                for b in range(B):
                    dve.wait_ge(rs_ready, b + 1)
                    x_in = xc[b] if center else src[:, cols(b)]
                    if gamma is None:
                        nc.vector.tensor_tensor(dst[:, cols(b)], x_in, rs[:, b % 2, :], ALU.mult).then_inc(out_ready, 1)
                    else:
                        nc.vector.scalar_tensor_tensor(dst[:, cols(b)], x_in, gamma, rs[:, b % 2, :], ALU.mult, ALU.mult).then_inc(out_ready, 1)


def store_end(core):
    nc, dram = core.nc, core.dram
    with Stage(core, "store") as st:
        xt = st.sb("x_tm", [P, NT, P])
        tiles_ready, tiles_out, stored = (st.sem(n) for n in ("tiles_ready", "tiles_out", "stored"))
        out = dram["out"].rearrange("(t p) c -> p t c", p=P)
        with nc.Block() as block:
            @block.tensor
            def _(pe):
                for b in range(B):
                    for q in range(QT):
                        last = nc.tensor.transpose(core.psum[:, b, q * P:(q + 1) * P], core.x[:, (b * QT + q) * P:(b * QT + q + 1) * P], core.ident[:])
                    last.then_inc(tiles_ready, 1)

            @block.vector
            def _(dve):
                for b in range(B):
                    dve.wait_ge(tiles_ready, b + 1)
                    nc.vector.tensor_copy(xt[:, b * QT:(b + 1) * QT, :].rearrange("p t c -> p (t c)"), core.psum[:, b, :]).then_inc(tiles_out, 1)

            @block.sync
            def _(sp):
                for b in range(B):
                    sp.wait_ge(tiles_out, b + 1)
                    sp.dma_start(out[:, b * QT:(b + 1) * QT, :], xt[:, b * QT:(b + 1) * QT, :]).then_inc(stored, 16)
                sp.wait_ge(stored, 16 * B)


def window_attention(core):
    nc, dram = core.nc, core.dram
    G, HG, W = 4, 4, 4
    L = 32
    with Stage(core, "l0a") as st:
        wqkv = st.sb("wqkv", [P, 3 * P])
        wproj = st.sb("wproj", [P, P])
        vecs = st.sb("vecs", [P, 8])
        wmask = st.sb("wmask", [P, L])
        xs = st.sb("xs", [P, T])
        q_raw, k_raw, qn, kn = (st.sb(n, [P, T]) for n in ("q_raw", "k_raw", "qn", "kn"))
        sq = st.sb("sq", [P, 2, T])
        lnm = st.sb("lnm", [P, 2, T])
        rs = st.sb("rs", [P, 2, T])
        v_tm = st.sb("v_tm", [P, QT, P])
        kx = st.sb("kx", [P, QT, W, HG, L])
        s_sb = st.sb("s_sb", [P, G, QT * HG * L])
        p_sb = st.sb("p_sb", [P, G, QT * HG * L])
        smax = st.sb("smax", [P, G, QT * HG])
        ssum = st.sb("ssum", [P, G, QT * HG])
        y_fm = st.sb("y_fm", [P, QT, W, L])
        (loaded, x_ready, qkv_ready, raw_ready, squared, ms_ready, ln_ready, rs_ready, qk_ready, s_ready, shifted,
         exp_ready, pt_ready, av_ready, y_ready, out_ready, chunk_done, dve_step, passed) = (st.sem(n) for n in (
            "loaded", "x_ready", "qkv_ready", "raw_ready", "squared", "ms_ready", "ln_ready", "rs_ready", "qk_ready", "s_ready",
            "shifted", "exp_ready", "pt_ready", "av_ready", "y_ready", "out_ready", "chunk_done", "dve_step", "passed"))
        ps_s = [core.psum[:, g, :] for g in range(G)]
        ps_o = [core.psum[:, 4 + w, :] for w in range(W)]
        DVE_STEPS = 19

        with nc.Block() as block:
            @block.sync
            def _(sp):
                sp.dma_start(wqkv[:], dram["l0_wqkv"]).then_inc(loaded, 16)
                sp.dma_start(wproj[:], dram["l0_wproj"]).then_inc(loaded, 16)
                sp.dma_start(vecs[:, 0:1], dram["l0_lnw"]).then_inc(loaded, 16)
                sp.dma_start(vecs[:, 1:5], dram["c_headmask"]).then_inc(loaded, 16)
                sp.dma_start(wmask[:], dram["c_wmask"]).then_inc(loaded, 16)

            @block.gpsimd
            def _(pool):
                with pool.Fori(0, B) as c:
                    pool.wait_ge(chunk_done, c + 1)
                    pool.sem_inc(passed, 1)
                    nc.gpsimd.tensor_copy(xs[:], core.x[:, cols(c)]).then_inc(x_ready, 1)

            @block.tensor
            def _(pe):
                pe.wait_ge(loaded, 5 * 16)
                with pe.Fori(0, B) as c:
                    pe.wait_ge(x_ready, c + 1)
                    nc.tensor.matmul(ps_s[0], wqkv[:, 0:P], xs[:], start=True, stop=True).then_inc(qkv_ready, 1)
                    nc.tensor.matmul(ps_s[1], wqkv[:, P:2 * P], xs[:], start=True, stop=True).then_inc(qkv_ready, 1)
                    for t in range(QT):
                        last = nc.tensor.matmul(ps_s[2][:, t * P:(t + 1) * P], xs[:, t * P:(t + 1) * P], wqkv[:, 2 * P:], start=True, stop=True)
                    last.then_inc(qkv_ready, 1)
                    for j in range(2):
                        pe.wait_ge(squared, 2 * c + j + 1)
                        nc.tensor.matmul(ps_o[j], core.mean_w[:], sq[:, j, :], start=True, stop=True).then_inc(ms_ready, 1)
                    pe.wait_ge(qk_ready, c + 1)
                    pe.sem_inc(passed, 1)
                    for t in range(QT):
                        for w in range(W):
                            for g in range(G):
                                rows, q_at = slice(32 * g, 32 * g + 32), t * P + w * L
                                last = nc.tensor.matmul(ps_s[g][32 * w:32 * w + 32, t * P:(t + 1) * P], qn[rows, q_at:q_at + L],
                                                        kx[rows, t, w, :, :].rearrange("p h k -> p (h k)"), start=True, stop=True)
                    last.then_inc(s_ready, 1)
                    pe.wait_ge(pt_ready, c + 1)
                    pe.sem_inc(passed, 1)
                    for t in range(QT):
                        for g in range(G):
                            for w in range(W):
                                rows = slice(32 * w, 32 * w + 32)
                                last = nc.tensor.matmul(ps_o[w][32 * g:32 * g + 32, t * P:(t + 1) * P], v_tm[rows, t, 32 * g:32 * g + 32],
                                                        s_sb[rows, g, t * P:(t + 1) * P], start=True, stop=True)
                    last.then_inc(av_ready, 1)
                    pe.wait_ge(y_ready, c + 1)
                    nc.tensor.matmul(ps_s[0], wproj[:], y_fm[:].rearrange("p t w q -> p (t w q)"), start=True, stop=True).then_inc(out_ready, 1)

            @block.scalar
            def _(act):
                nc.scalar.preload_act_table_set("natural_log_exp_and_others")
                act.wait_ge(loaded, 5 * 16)
                with act.Fori(0, B) as c:
                    for j, raw in enumerate((q_raw, k_raw)):
                        act.wait_ge(qkv_ready, 3 * c + j + 1)
                        nc.scalar.activation(raw[:], ps_s[j], ACT.Copy).then_inc(raw_ready, 1)
                        nc.scalar.activation(sq[:, j, :], ps_s[j], ACT.Square).then_inc(squared, 1)
                    for j in range(2):
                        act.wait_ge(ms_ready, 2 * c + j + 1)
                        nc.scalar.activation(lnm[:, j, :], ps_o[j], ACT.Ln, bias=core.eps[:, 1:2]).then_inc(ln_ready, 1)
                        act.wait_ge(ln_ready, 2 * c + j + 1)
                        nc.scalar.activation(rs[:, j, :], lnm[:, j, :], ACT.Exp, scale=-0.5).then_inc(rs_ready, 1)
                    for g in range(G):
                        act.wait_ge(shifted, G * c + g + 1)
                        nc.scalar.activation(p_sb[:, g, :], s_sb[:, g, :], ACT.Exp, scale=8 ** -0.5).then_inc(exp_ready, 1)

            @block.vector
            def _(dve):
                dve.wait_ge(loaded, 5 * 16)
                dve.sem_inc(chunk_done, 1)
                with dve.Fori(0, B) as c:
                    step = Steps(dve, dve_step, c * DVE_STEPS)
                    dve.wait_ge(qkv_ready, 3 * c + 3)
                    step(nc.vector.tensor_copy(v_tm[:].rearrange("p t d -> p (t d)"), ps_s[2]))
                    dve.wait_ge(rs_ready, 2 * c + 2)
                    dve.wait_ge(raw_ready, 2 * c + 2)
                    nc.vector.scalar_tensor_tensor(qn[:], q_raw[:], vecs[:, 0:1], rs[:, 0, :], ALU.mult, ALU.mult)
                    step(nc.vector.scalar_tensor_tensor(kn[:], k_raw[:], vecs[:, 0:1], rs[:, 1, :], ALU.mult, ALU.mult))
                    for h in range(HG):
                        last = nc.vector.tensor_scalar(kx[:, :, :, h, :], kn[:].rearrange("p (t w k) -> p t w k", w=W, k=L),
                                                       vecs[:, 1 + h:2 + h], None, ALU.mult)
                    last.then_inc(qk_ready, 1)
                    dve.wait_ge(s_ready, c + 1)
                    blocks = [s_sb[:, g, :].rearrange("p (b k) -> p b k", k=L) for g in range(G)]
                    for g in range(G):
                        step(nc.vector.tensor_tensor(blocks[g], ps_s[g].rearrange("p (b k) -> p b k", k=L),
                                                     wmask[:].unsqueeze(1).to_broadcast([P, QT * HG, L]), ALU.add))
                        step(nc.vector.tensor_reduce(smax[:, g, :], blocks[g], AX.X, ALU.max))
                        nc.vector.tensor_tensor(blocks[g], blocks[g], smax[:, g, :].unsqueeze(2).to_broadcast([P, QT * HG, L]),
                                                ALU.subtract).then_inc(shifted, 1)
                    for g in range(G):
                        pb = p_sb[:, g, :].rearrange("p (b k) -> p b k", k=L)
                        dve.wait_ge(exp_ready, G * c + g + 1)
                        step(nc.vector.tensor_reduce(ssum[:, g, :], pb, AX.X, ALU.add))
                        if g == G - 1:
                            step(nc.vector.reciprocal(ssum[:], ssum[:]))
                    for g in range(G):
                        pb = p_sb[:, g, :].rearrange("p (b k) -> p b k", k=L)
                        last = nc.vector.tensor_tensor(pb, pb, ssum[:, g, :].unsqueeze(2).to_broadcast([P, QT * HG, L]), ALU.mult)
                    step(last)
                    last = nc.vector.transpose(s_sb[:].rearrange("p g n -> p (g n)"), p_sb[:].rearrange("p g n -> p (g n)"))
                    last.then_inc(pt_ready, 1)
                    dve.wait_ge(av_ready, c + 1)
                    for h in range(HG):
                        for w in range(W):
                            o = ps_o[w].rearrange("p (t h q) -> p t h q", h=HG, q=L)[:, :, h, :]
                            if h == 0:
                                last = nc.vector.tensor_scalar(y_fm[:, :, w, :], o, vecs[:, 1:2], None, ALU.mult)
                            else:
                                last = nc.vector.scalar_tensor_tensor(y_fm[:, :, w, :], o, vecs[:, 1 + h:2 + h], y_fm[:, :, w, :], ALU.mult, ALU.add)
                        if h < HG - 1:
                            step(last)
                    last.then_inc(y_ready, 1)
                    dve.wait_ge(out_ready, c + 1)
                    nc.vector.tensor_tensor(core.sum[:, cols(c)], ps_s[0], core.x[:, cols(c)], ALU.add).then_inc(chunk_done, 1)
                    assert step.n == DVE_STEPS, step.n


GR = 96
SENT = -3.0e38
PLACES = 4
HIT = 3.0e38


def experts(core, name, *, act_func, x, resid, gates_t, gates3, n_slots, unroll, tiles, w_dram, with_b1=False,
            b2=None, b2_rows=0, glu=False):
    nc = core.nc
    up = 2 if glu else 1
    w1_cols = up * tiles * P
    biases = tiles if with_b1 else 0
    w_cols = w1_cols + tiles * P + biases
    iters = n_slots // unroll
    assert iters * unroll == n_slots
    items = [(s, b, t) for s in range(unroll) for b in range(B) for t in range(tiles)]
    n_items = len(items)
    assert n_items % PLACES == 0
    lag = 2 if glu else 3
    gated_credit = tiles + PLACES
    out_credit = n_items
    with Stage(core, name) as st:
        w = st.sb("w", [P, unroll, w_cols])
        w_hi, w_lo = (st.sb(f"w_{n}", [P, unroll, w_cols - biases], F32R) for n in ("hi", "lo"))
        x_hi, x_lo = (st.sb(f"x_{n}", [P, N], F32R) for n in ("hi", "lo"))
        act_sb = st.sb("act", [P, PLACES, T])
        glu_sb = st.sb("glu", [P, 2, T]) if glu else None
        gated = st.sb("gated", [P, PLACES, T])
        gated_hi, gated_lo = (st.sb(f"gated_{n}", [P, PLACES, T], F32R) for n in ("hi", "lo"))
        sel_cols = n_slots * P if glu else 32
        selb = st.sb("selb", [GR, sel_cols], BF16)
        self32 = st.sb("self32", [GR, sel_cols])
        w_loaded = [st.sem(f"w{s}_loaded") for s in range(unroll)]
        w_split = [st.sem(f"w{s}_split") for s in range(unroll)]
        w_hi_ready = [st.sem(f"w{s}_hi_ready") for s in range(unroll)]
        (consts_loaded, sel_ready, x_hi_ready, x_split, hid_ready, gate_ready, act_ready, glu_ready, gated_ready, hi_ready,
         lo_ready, out_done) = (st.sem(n) for n in (
             "consts_loaded", "sel_ready", "x_hi_ready", "x_split", "hid_ready", "gate_ready", "act_ready", "glu_ready",
             "gated_ready", "hi_ready", "lo_ready", "out_done"))
        passed = st.sem("passed")
        acc = [core.psum[:, b, :] for b in range(B)]
        hid = [core.psum[:, 4 + k, :] for k in range(2)]
        gate = [core.psum[:, 6 + k, :] for k in range(2)]

        with nc.Block() as block:
            @block.sync
            def _(sp):
                sp.dma_start(self32[:], core.dram["c_selpair" if glu else "c_sel"]).then_inc(consts_loaded, 16)
                with sp.Fori(0, iters) as i:
                    for s in range(unroll):
                        sp.wait_ge(out_done, i * n_items + (s + 1) * B * tiles)
                        sp.dma_start(w[:, s, :], w_dram[bass.ds(i * unroll + s, 1)].rearrange("o p n -> p (o n)")).then_inc(w_loaded[s], 16)

            @block.gpsimd
            def _(pool):
                with pool.Fori(0, iters) as i:
                    for s in range(unroll):
                        whole = w[:, s, 0:w_cols - biases]
                        pool.wait_ge(w_loaded[s], 16 * i + 16)
                        pool.sem_inc(passed, 1)
                        nc.gpsimd.tensor_copy(w_hi[:, s, :], whole).then_inc(w_hi_ready[s], 1)
                        pool.wait_ge(w_hi_ready[s], i + 1)
                        nc.gpsimd.tensor_tensor(w_lo[:, s, :], whole, w_hi[:, s, :].bitcast(F32), ALU.subtract).then_inc(w_split[s], 1)

            @block.tensor
            def _(pe):
                pe.sem_inc(out_done, out_credit)
                for b in range(B):
                    nc.tensor.matmul(acc[b], core.ident[:], resid[:, cols(b)], start=True, stop=b2 is None)
                    if b2 is not None:
                        nc.tensor.matmul(acc[b], b2[0:b2_rows, :], gates_t[0:b2_rows, cols(b)], start=False, stop=True)
                pe.wait_ge(sel_ready, 1)
                pe.wait_ge(x_split, B)

                def product(out, s, at, hi, lo, start):
                    w_h, w_l = w_hi[:, s, at:at + P], w_lo[:, s, at:at + P]
                    nc.tensor.matmul(out, w_h, hi, start=start, stop=False, skip_group_check=True)
                    nc.tensor.matmul(out, w_l, hi, start=False, stop=False, skip_group_check=True)
                    return nc.tensor.matmul(out, w_h, lo, start=False, stop=True, skip_group_check=True)

                def hidden(i, n):
                    s, b, t = items[n]
                    g = i * n_items + n
                    if b == 0 and t == 0:
                        pe.wait_ge(w_split[s], i + 1)
                    if t == 0:
                        pair, e = i * (unroll * B) + s * B + b, i * unroll + s
                        pe.wait_ge(gated_ready, pair * tiles - tiles + gated_credit)
                        sel = (selb[:, bass.ds(e * P, P)] if glu
                               else selb[:, bass.ds(e, 1)].to_broadcast([GR, P]))
                        nc.tensor.matmul(gate[b % 2], sel, gates3[:, cols(b)], start=True, stop=True).then_inc(gate_ready, 1)
                    if glu:
                        pe.wait_ge(glu_ready, g + 1)
                    else:
                        pe.wait_ge(act_ready, g + 1)
                    for k in range(up):
                        product(hid[k if glu else n % 2], s, (k * tiles + t) * P, x_hi[:, cols(b)], x_lo[:, cols(b)],
                                True).then_inc(hid_ready, 1)

                def output(i, n):
                    s, b, t = items[n]
                    pe.wait_ge(lo_ready, i * n_items + n + 1)
                    product(acc[b], s, w1_cols + t * P, gated_hi[:, n % PLACES, :], gated_lo[:, n % PLACES, :],
                            False).then_inc(out_done, 1)

                for n in range(lag):
                    hidden(0, n)
                with pe.Fori(0, iters - 1) as i:
                    for n in range(n_items):
                        ahead = n + lag
                        hidden(i + ahead // n_items, ahead % n_items)
                        output(i, n)
                for n in range(n_items):
                    if n + lag < n_items:
                        hidden(iters - 1, n + lag)
                    output(iters - 1, n)

            @block.scalar
            def _(act):
                act.wait_ge(consts_loaded, 16)
                nc.scalar.activation(selb[:], self32[:], ACT.Copy).then_inc(sel_ready, 1)
                for b in range(B):
                    nc.scalar.activation(x_hi[:, cols(b)], x[:, cols(b)], ACT.Copy).then_inc(x_hi_ready, 1)
                nc.scalar.preload_act_table(act_func)
                act.sem_inc(act_ready, 2)
                with act.Fori(0, iters) as i:
                    def activate(n):
                        s, b, t = items[n]
                        g = i * n_items + n
                        act.wait_ge(hid_ready, g * up + 1)
                        act.wait_ge(gated_ready, g - PLACES + 1 + gated_credit)
                        bias = {"bias": w[:, s, w_cols - tiles + t:w_cols - tiles + t + 1]} if with_b1 else {}
                        nc.scalar.activation(act_sb[:, n % PLACES, :], hid[0] if glu else hid[n % 2], act_func, **bias).then_inc(act_ready, 1)

                    activate(0)
                    for n in range(n_items):
                        if n + 1 < n_items:
                            activate(n + 1)
                        g = i * n_items + n
                        act.wait_ge(gated_ready, g + 1 + gated_credit)
                        act.wait_ge(out_done, g - PLACES + 1 + out_credit)
                        nc.scalar.activation(gated_hi[:, n % PLACES, :], gated[:, n % PLACES, :], ACT.Copy).then_inc(hi_ready, 1)

            @block.vector
            def _(dve):
                for b in range(B):
                    dve.wait_ge(x_hi_ready, b + 1)
                    nc.vector.tensor_tensor(x_lo[:, cols(b)], x[:, cols(b)], x_hi[:, cols(b)].bitcast(F32), ALU.subtract).then_inc(x_split, 1)
                dve.sem_inc(gated_ready, gated_credit)
                if glu:
                    dve.sem_inc(glu_ready, 1)
                with dve.Fori(0, iters) as i:
                    def gate_item(n):
                        s, b, t = items[n]
                        g = i * n_items + n
                        dve.wait_ge(act_ready, g + 3)
                        src = act_sb[:, n % PLACES, :]
                        if glu:
                            dve.wait_ge(hid_ready, g * 2 + 2)
                            nc.vector.tensor_tensor(glu_sb[:, n % 2, :], src, hid[1], ALU.mult).then_inc(glu_ready, 1)
                            dve.wait_ge(glu_ready, g + 2)
                            src = glu_sb[:, n % 2, :]
                        dve.wait_ge(gate_ready, i * (unroll * B) + s * B + b + 1)
                        nc.vector.tensor_tensor(gated[:, n % PLACES, :], src, gate[b % 2], ALU.mult).then_inc(gated_ready, 1)

                    gate_item(0)
                    for n in range(n_items):
                        if n + 1 < n_items:
                            gate_item(n + 1)
                        g = i * n_items + n
                        dve.wait_ge(hi_ready, g + 1)
                        dve.wait_ge(out_done, g - PLACES + 1 + out_credit)
                        nc.vector.tensor_tensor(gated_lo[:, n % PLACES, :], gated[:, n % PLACES, :],
                                                gated_hi[:, n % PLACES, :].bitcast(F32), ALU.subtract).then_inc(lo_ready, 1)
                dve.wait_ge(out_done, iters * n_items + out_credit)
                for b in range(B):
                    nc.vector.tensor_copy(core.sum[:, cols(b)], acc[b])


def router(core, name, kind, *, x, w_dram, n_experts, top, gates_t, gates3, bias_dram=None, hid_dram=None,
           hid_bias_dram=None, tri_dram=None, capacity=None):
    nc = core.nc
    E, KT = n_experts, 2 if hid_dram is not None else 1
    W = P if kind == "top_capacity" else 32
    with Stage(core, name) as st:
        rw = st.sb("rw", [P, KT, E])
        bias = st.sb("bias", [P, E])
        scores = st.sb("scores", [P, NT, E])
        ranked = st.sb("ranked", [P, NT, E + 8])
        marked = st.sb("marked", [P, NT, E + 8])
        top8 = st.sb("top8", [P, NT, 8])
        mask = st.sb("mask", [P, NT, E])
        g_tm = st.sb("g_tm", [P, NT, W])
        small = st.sb("small", [P, NT, 8])
        rest = st.sb("rest", [32, N])
        part = st.sb("part", [32, N], BF16)
        if kind == "sigmoid_groups":
            tri = st.sb("tri", [P, 2, 16])
            gsum = st.sb("gsum", [P, NT, 4])
            work = st.sb("work", [P, NT, 16])
            work2 = st.sb("work2", [P, NT, 16])
        if hid_dram is not None:
            hw = st.sb("hw", [P, KT * P])
            hb = st.sb("hb", [P, KT])
            hid = st.sb("hid", [P, KT, N])
        if kind == "top_capacity":
            masks_t = st.sb("masks_t", [8, 2, N])
            probs_t = st.sb("probs_t", [8, 2, N])
            count = st.sb("count", [8, 2, N])
            ones = st.sb("ones", [8, N])
        (loaded, hid_psum, hid_ready, logits_ready, scores_ready, shifted, exp_ready, gates_ready, gates_t_psum,
         dve_step) = (st.sem(n) for n in ("loaded", "hid_psum", "hid_ready", "logits_ready", "scores_ready", "shifted",
                                          "exp_ready", "gates_ready", "gates_t_psum", "dve_step"))
        logits = core.psum[:, 0, 0:NT * E].rearrange("p (t e) -> p t e", e=E)
        loads = [(rw[:], w_dram)]
        if bias_dram is not None:
            loads.append((bias[:], bias_dram.partition_broadcast(P)))
        if tri_dram is not None:
            loads.append((tri[:], tri_dram))
        if hid_dram is not None:
            loads += [(hw[:], hid_dram), (hb[:], hid_bias_dram)]

        with nc.Block() as block:
            @block.sync
            def _(sp):
                for to, of in loads:
                    sp.dma_start(to, of).then_inc(loaded, 16)

            @block.tensor
            def _(pe):
                pe.wait_ge(loaded, 16 * len(loads))
                if hid_dram is not None:
                    for b in range(B):
                        for k in range(KT):
                            n = b * KT + k
                            if n >= 2:
                                pe.wait_ge(hid_ready, n - 1)
                            nc.tensor.matmul(core.psum[:, 4 + n % 2, :], hw[:, k * P:(k + 1) * P], x[:, cols(b)],
                                             start=True, stop=True).then_inc(hid_psum, 1)
                    pe.wait_ge(hid_ready, B * KT)
                for t in range(NT):
                    for k in range(KT):
                        src = x[:, t * P:(t + 1) * P] if hid_dram is None else hid[:, k, t * P:(t + 1) * P]
                        last = nc.tensor.matmul(logits[:, t, :], src, rw[:, k, :], start=k == 0, stop=k == KT - 1)
                last.then_inc(logits_ready, 1)
                pe.wait_ge(gates_ready, 1)
                for t in range(NT):
                    last = nc.tensor.transpose(core.psum[0:W, t // QT, (t % QT) * P:(t % QT + 1) * P], g_tm[:, t, :], core.ident[:])
                    if t % QT == QT - 1:
                        last.then_inc(gates_t_psum, 1)

            @block.scalar
            def _(act):
                act.wait_ge(loaded, 16 * len(loads))
                if hid_dram is not None:
                    for b in range(B):
                        for k in range(KT):
                            act.wait_ge(hid_psum, b * KT + k + 1)
                            nc.scalar.activation(hid[:, k, cols(b)], core.psum[:, 4 + (b * KT + k) % 2, :], ACT.Gelu,
                                                 bias=hb[:, k:k + 1]).then_inc(hid_ready, 1)
                if kind == "sigmoid_groups":
                    act.wait_ge(logits_ready, 1)
                    nc.scalar.activation(scores[:], logits, ACT.Sigmoid).then_inc(scores_ready, 1)
                else:
                    act.wait_ge(shifted, 1)
                    to, of = (small[:, :, 1:2], small[:, :, 0:1]) if kind == "top_capacity" else (scores[:], scores[:])
                    nc.scalar.activation(to, of, ACT.Exp).then_inc(exp_ready, 1)

            @block.vector
            def _(dve):
                step = Steps(dve, dve_step)

                def wide(ap, n):
                    return ap.to_broadcast([P, NT, n])

                def find_top(k, out):
                    if k < 8:
                        step(nc.vector.memset(top8[:, :, k:8], SENT))
                    for t in range(NT):
                        last = nc.vector.match_replace(marked[:, t, :], top8[:, t, :], ranked[:, t, :], HIT)
                    step(last)
                    step(nc.vector.tensor_scalar(out, marked[:, :, 0:E], HIT, None, ALU.is_equal))

                def rank():
                    for t in range(NT):
                        last = nc.vector.max(top8[:, t, :], ranked[:, t, 0:E])
                    step(last)

                dve.wait_ge(loaded, 16 * len(loads))
                step(nc.vector.memset(ranked[:], SENT))
                step(nc.vector.memset(g_tm[:], 0.0))
                if kind == "sigmoid_groups":
                    dve.wait_ge(scores_ready, 1)
                    step(nc.vector.tensor_tensor(ranked[:, :, 0:E], scores[:], bias[:].unsqueeze(1).to_broadcast([P, NT, E]), ALU.add))
                    four = ranked[:, :, 0:E].rearrange("p t (g k) -> p t g k", k=4)
                    hi1, lo1, hi2, lo2 = (work[:, :, 4 * k:4 * k + 4] for k in range(4))
                    nc.vector.tensor_tensor(hi1, four[:, :, :, 0], four[:, :, :, 1], ALU.max)
                    nc.vector.tensor_tensor(lo1, four[:, :, :, 0], four[:, :, :, 1], ALU.min)
                    nc.vector.tensor_tensor(hi2, four[:, :, :, 2], four[:, :, :, 3], ALU.max)
                    step(nc.vector.tensor_tensor(lo2, four[:, :, :, 2], four[:, :, :, 3], ALU.min))
                    m1, m2, m3 = (work2[:, :, 4 * k:4 * k + 4] for k in range(3))
                    nc.vector.tensor_tensor(m1, hi1, hi2, ALU.max)
                    nc.vector.tensor_tensor(m2, hi1, hi2, ALU.min)
                    step(nc.vector.tensor_tensor(m3, lo1, lo2, ALU.max))
                    step(nc.vector.tensor_tensor(m2, m2, m3, ALU.max))
                    step(nc.vector.tensor_tensor(gsum[:], m1, m2, ALU.add))
                    of_j = gsum[:].unsqueeze(2).to_broadcast([P, NT, 4, 4])
                    of_i = gsum[:].unsqueeze(3).to_broadcast([P, NT, 4, 4])
                    nc.vector.tensor_tensor(work[:].rearrange("p t (i j) -> p t i j", j=4), of_j, of_i, ALU.is_ge)
                    step(nc.vector.tensor_tensor(work2[:].rearrange("p t (i j) -> p t i j", j=4), of_j, of_i, ALU.is_gt))
                    nc.vector.tensor_tensor(work[:], work[:], tri[:, 0:1, :].to_broadcast([P, NT, 16]), ALU.mult)
                    step(nc.vector.tensor_tensor(work2[:], work2[:], tri[:, 1:2, :].to_broadcast([P, NT, 16]), ALU.mult))
                    step(nc.vector.tensor_tensor(work[:], work[:], work2[:], ALU.add))
                    step(nc.vector.tensor_reduce(gsum[:], work[:].rearrange("p t (i j) -> p t i j", j=4), AX.X, ALU.add))
                    step(nc.vector.tensor_scalar(gsum[:], gsum[:], 2.0, None, ALU.is_lt))
                    step(nc.vector.tensor_tensor(four, four, gsum[:].unsqueeze(3).to_broadcast([P, NT, 4, 4]), ALU.mult))
                    step(nc.vector.tensor_scalar(ranked[:, :, 0:E], ranked[:, :, 0:E], 0.0, None, ALU.add))
                    rank()
                    find_top(top, mask[:])
                    step(nc.vector.tensor_tensor(mask[:], mask[:], scores[:], ALU.mult))
                    step(nc.vector.tensor_reduce(small[:, :, 0:1], mask[:], AX.X, ALU.add))
                    step(nc.vector.tensor_scalar(small[:, :, 0:1], small[:, :, 0:1], 1e-20, None, ALU.add))
                    step(nc.vector.reciprocal(small[:, :, 0:1], small[:, :, 0:1]))
                    step(nc.vector.tensor_tensor(mask[:], mask[:], wide(small[:, :, 0:1], E), ALU.mult))
                    nc.vector.tensor_scalar(g_tm[:, :, 0:E], mask[:], 2.5, None, ALU.mult)
                    nc.vector.memset(g_tm[:, :, E:E + 2], 1.0).then_inc(gates_ready, 1)
                elif kind == "softmax_top":
                    dve.wait_ge(logits_ready, 1)
                    step(nc.vector.tensor_tensor(scores[:], logits, bias[:].unsqueeze(1).to_broadcast([P, NT, E]), ALU.add))
                    step(nc.vector.tensor_reduce(small[:, :, 0:1], scores[:], AX.X, ALU.max))
                    nc.vector.tensor_tensor(scores[:], scores[:], wide(small[:, :, 0:1], E), ALU.subtract).then_inc(shifted, 1)
                    dve.wait_ge(exp_ready, 1)
                    step(nc.vector.tensor_reduce(small[:, :, 1:2], scores[:], AX.X, ALU.add))
                    step(nc.vector.reciprocal(small[:, :, 1:2], small[:, :, 1:2]))
                    step(nc.vector.tensor_tensor(ranked[:, :, 0:E], scores[:], wide(small[:, :, 1:2], E), ALU.mult))
                    rank()
                    find_top(top, mask[:])
                    nc.vector.tensor_tensor(g_tm[:, :, 0:E], mask[:], ranked[:, :, 0:E], ALU.mult)
                    nc.vector.memset(g_tm[:, :, E:E + 1], 1.0).then_inc(gates_ready, 1)
                else:
                    dve.wait_ge(logits_ready, 1)
                    step(nc.vector.tensor_copy(ranked[:, :, 0:E], logits))
                    rank()
                    nc.vector.tensor_tensor(small[:, :, 0:1], top8[:, :, 1:2], top8[:, :, 0:1], ALU.subtract).then_inc(shifted, 1)
                    dve.wait_ge(exp_ready, 1)
                    find_top(2, g_tm[:, :, 32:32 + E])
                    find_top(1, g_tm[:, :, 0:E])
                    step(nc.vector.tensor_tensor(g_tm[:, :, 32:32 + E], g_tm[:, :, 32:32 + E], g_tm[:, :, 0:E], ALU.subtract))
                    step(nc.vector.tensor_scalar(small[:, :, 2:3], small[:, :, 1:2], 1.0, None, ALU.add))
                    step(nc.vector.reciprocal(small[:, :, 2:3], small[:, :, 2:3]))
                    step(nc.vector.tensor_tensor(small[:, :, 3:4], small[:, :, 1:2], small[:, :, 2:3], ALU.mult))
                    nc.vector.tensor_tensor(g_tm[:, :, 64:64 + E], g_tm[:, :, 0:E], wide(small[:, :, 2:3], E), ALU.mult)
                    nc.vector.tensor_tensor(g_tm[:, :, 96:96 + E], g_tm[:, :, 32:32 + E], wide(small[:, :, 3:4], E), ALU.mult).then_inc(gates_ready, 1)

                dve.wait_ge(gates_t_psum, B)
                flat = core.psum[:, 0:4, :].rearrange("p b n -> p (b n)")
                if kind == "top_capacity":
                    step(nc.vector.memset(gates_t[:], 0.0))
                    for k in range(2):
                        nc.vector.tensor_copy(masks_t[:, k, :], flat[32 * k:32 * k + E, :])
                        nc.vector.tensor_copy(probs_t[:, k, :], flat[64 + 32 * k:64 + 32 * k + E, :])
                    step(nc.vector.memset(ones[:], 1.0))
                    step(nc.vector.tensor_tensor_scan(count[:, 0, :], ones[:], masks_t[:, 0, :], 0.0, ALU.mult, ALU.add))
                    step(nc.vector.tensor_tensor_scan(count[:, 1, :], ones[:], masks_t[:, 1, :], count[:, 0, N - 1:N], ALU.mult, ALU.add))
                    for k in range(2):
                        step(nc.vector.scalar_tensor_tensor(probs_t[:, k, :], count[:, k, :], float(capacity), probs_t[:, k, :], ALU.is_le, ALU.mult))
                    step(nc.vector.tensor_tensor(gates_t[0:E, :], probs_t[:, 0, :], probs_t[:, 1, :], ALU.add))
                else:
                    step(nc.vector.tensor_copy(gates_t[:], flat[0:32, :]))
                nc.vector.tensor_copy(gates3[0:32, :], gates_t[:])
                step(nc.vector.tensor_copy(part[:], gates_t[:]))
                step(nc.vector.tensor_tensor(rest[:], gates_t[:], part[:], ALU.subtract))
                nc.vector.tensor_copy(gates3[32:64, :], rest[:])
                step(nc.vector.tensor_copy(part[:], rest[:]))
                nc.vector.tensor_tensor(gates3[64:96, :], rest[:], part[:], ALU.subtract)


def ffn0(core):
    d = core.dram
    with Stage(core, "f0") as st:
        gt, g3 = st.sb("gates_t", [32, N]), st.sb("gates3", [GR, N], BF16)
        router(core, "r0", "sigmoid_groups", x=core.x, w_dram=d["l0_router"], n_experts=16, top=4, gates_t=gt, gates3=g3,
               bias_dram=d["l0_ebias"], tri_dram=d["c_tri"])
        experts(core, "e0", act_func=ACT.Silu, x=core.x, resid=core.x, gates_t=gt, gates3=g3, n_slots=9, unroll=3, tiles=1,
                w_dram=d["l0_experts"], glu=True)


def ffn1(core):
    d = core.dram
    with Stage(core, "f1") as st:
        gt, g3 = st.sb("gates_t", [32, N]), st.sb("gates3", [GR, N], BF16)
        capacity = int(2 * 1.25 * N / 8)
        capacity += capacity % 2
        router(core, "r1", "top_capacity", x=core.x, w_dram=d["l1_router"], n_experts=8, top=2, gates_t=gt, gates3=g3,
               capacity=capacity)
        experts(core, "e1", act_func=ACT.Gelu, x=core.x, resid=core.x, gates_t=gt, gates3=g3, n_slots=8, unroll=2, tiles=4,
                w_dram=d["l1_experts"])


def ffn3(core):
    d = core.dram
    with Stage(core, "f3") as st:
        gt, g3 = st.sb("gates_t", [32, N]), st.sb("gates3", [GR, N], BF16)
        b2 = st.sb("b2", [9, P])
        b2_loaded = st.sem("b2_loaded")
        with core.nc.Block() as block:
            @block.sync
            def _(sp):
                sp.dma_start(b2[:], d["l3_b2"]).then_inc(b2_loaded, 16)
                sp.wait_ge(b2_loaded, 16)
        router(core, "r3", "softmax_top", x=core.x, w_dram=d["l3_router"], n_experts=8, top=2, gates_t=gt, gates3=g3,
               bias_dram=d["l3_rbias"], hid_dram=d["l3_gw1"], hid_bias_dram=d["l3_gb1"])
        experts(core, "e3", act_func=ACT.Gelu_apprx_tanh, x=core.x, resid=core.x, gates_t=gt, gates3=g3, n_slots=9, unroll=3, tiles=2,
                w_dram=d["l3_experts"], with_b1=True, b2=b2, b2_rows=9)


def init_sum(core, name, src, bias_dram=None):
    nc = core.nc
    with Stage(core, name) as st:
        bias = st.sb("bias", [P, 1])
        loaded = st.sem("loaded")
        with nc.Block() as block:
            @block.sync
            def _(sp):
                if bias_dram is not None:
                    sp.dma_start(bias[:], bias_dram).then_inc(loaded, 16)

            @block.vector
            def _(dve):
                if bias_dram is None:
                    nc.vector.tensor_copy(core.sum[:], src[:])
                else:
                    dve.wait_ge(loaded, 16)
                    nc.vector.tensor_scalar(core.sum[:], src[:], bias[:], None, ALU.add)


def rope_attention(core, name, *, x, groups, heads, q_rows, w_dram, tables, qk_bias=False, v_bias=None):
    nc = core.nc
    dv = P // heads
    half = q_rows // 2
    halves = [(lo, lo + half if lo // half % 2 == 0 else lo - half) for lo in range(0, P, half)]
    AHEAD = 2
    wq_cols = P + 1 if qk_bias else P
    items = [(u, q, h) for u in range(B) for q in range(QT) for h in range(heads)]
    n_items, n_tiles = len(items), B * QT
    per_unit = QT * heads
    parts = [(0, wq_cols), (wq_cols, wq_cols), (2 * wq_cols, P), (2 * wq_cols + P, P)]
    with Stage(core, name) as st:
        w = [st.sb(f"w{n}", [P, size]) for n, (_, size) in zip("qkvo", parts)]
        raw = st.sb("raw", [P, 2, T])
        swapped = st.sb("swapped", [P, 2, T])
        rot = st.sb("rot", [P, 2, T])
        qs = st.sb("q", [P, B, T])
        ks = st.sb("k", [P, B, T])
        vs = st.sb("v", [P, B, QT, P])
        probs = st.sb("probs", [P, 2, T])
        probs_t = st.sb("probs_t", [P, 2, QT, P])
        nmax = st.sb("nmax", [P, 4])
        rsum = st.sb("rsum", [P, QT, heads])
        rinv = st.sb("rinv", [P, QT, heads])
        y = st.sb("y", [P, 2, P])
        y_t = st.sb("y_t", [P, T])
        w_loaded = [st.sem(f"w{n}_loaded") for n in "qkvo"]
        swap_loaded = [st.sem(f"{n}_swapped") for n in "qk"]
        (raw_ready, cos_ready, sin_ready, proj_ready, v_ready, qk_ready, s_ready, max_ready, probs_ready, pt_psum, pt_ready,
         y_psum, rinv_ready, y_ready, yt_psum, yt_ready, unit_done, sum_done) = (st.sem(n) for n in (
             "raw_ready", "cos_ready", "sin_ready", "proj_ready", "v_ready", "qk_ready", "s_ready", "max_ready", "probs_ready",
             "pt_psum", "pt_ready", "y_psum", "rinv_ready", "y_ready", "yt_psum", "yt_ready", "unit_done", "sum_done"))
        ps_s = [core.psum[:, k, :] for k in range(2)]
        ps_t = [core.psum[:, 2 + k, :] for k in range(2)]
        ps_y = core.psum[:, 4, 0:P]
        ps_o = core.psum[:, 5, :]
        ps_p = [core.psum[:, 6 + k, :] for k in range(2)]

        def whole(i, j):
            return i + j // n_items, j % n_items

        def per_group(engine, body):
            body(0, True, False)
            with engine.Fori(1, groups - 1) as i:
                body(i, False, False)
            body(groups - 1, False, True)

        with nc.Block() as block:
            @block.sync
            def _(sp):
                def load(i, k):
                    at, size = parts[k]
                    sp.dma_start(w[k][:], w_dram[bass.ds(i, 1), :, at:at + size].rearrange("o p n -> p (o n)")).then_inc(w_loaded[k], 16)

                def group(i, first, last):
                    for u in range(B):
                        U = i * B + u
                        for j in range(2):
                            sp.wait_ge(raw_ready, 2 * U + j + 1)
                            sp.wait_ge(qk_ready, 2 * U + j + 1)
                            for lo, hi in halves:
                                sp.dma_start(swapped[hi:hi + half, j, :], raw[lo:lo + half, j, :]).then_inc(swap_loaded[j], 16)
                            if u == B - 1 and not last:
                                load(i + 1, j)
                        if u == B - 1 and not last:
                            sp.wait_ge(proj_ready, 3 * U + 3)
                            load(i + 1, 2)
                        if u == 2:
                            sp.wait_ge(unit_done, i * B + B)
                            load(i, 3)

                for k in range(3):
                    load(0, k)
                per_group(sp, group)

            @block.gpsimd
            def _(pool):
                pool.sem_inc(qk_ready, 2)
                with pool.Fori(0, groups) as i:
                    for u in range(B):
                        U = i * B + u
                        pool.wait_ge(unit_done, U + 1)
                        for j, to in enumerate((qs, ks)):
                            pool.wait_ge(swap_loaded[j], (U + 1) * (16 * len(halves)))
                            nc.gpsimd.tensor_tensor(swapped[:, j, :], swapped[:, j, :], tables[:, 2 * j + 1, :], ALU.mult).then_inc(sin_ready, 1)
                            pool.wait_ge(sin_ready, 2 * U + j + 1)
                            pool.wait_ge(cos_ready, 2 * U + j + 1)
                            nc.gpsimd.tensor_tensor(to[:, u, :], rot[:, j, :], swapped[:, j, :], ALU.add).then_inc(qk_ready, 1)

            @block.tensor
            def _(pe):
                pe.sem_inc(unit_done, B)
                pe.sem_inc(pt_psum, 2)
                pe.sem_inc(y_psum, 2)
                pe.sem_inc(yt_psum, 2)

                def project(i, u, part):
                    U = i * B + u
                    if u == 0:
                        pe.wait_ge(w_loaded[part], 16 * i + 16)
                    if part == 2:
                        pe.wait_ge(raw_ready, 2 * U + 1)
                        for t in range(QT):
                            last = nc.tensor.matmul(ps_p[0][:, t * P:(t + 1) * P], x[:, u * T + t * P:u * T + (t + 1) * P], w[2][:], start=True, stop=True)
                        last.then_inc(proj_ready, 1)
                    else:
                        pe.wait_ge(v_ready if part == 0 else raw_ready, U + 1 if part == 0 else 2 * U + 1)
                        nc.tensor.matmul(ps_p[part], w[part][:, 0:P], x[:, cols(u)], start=True, stop=True).then_inc(proj_ready, 1)

                def scores(i, j):
                    u, q, h = items[j]
                    if q == 0 and h == 0:
                        pe.wait_ge(qk_ready, 2 * (i * B + u) + 2 + 2)
                    pe.wait_ge(probs_ready, i * n_items + j + 1)
                    rows = slice(h * q_rows, (h + 1) * q_rows)
                    nc.tensor.matmul(ps_s[j % 2][:, 0:(q + 1) * P], qs[rows, u, q * P:(q + 1) * P], ks[rows, u, 0:(q + 1) * P],
                                     start=True, stop=False)
                    nc.tensor.matmul(ps_s[j % 2][:, q * P:(q + 1) * P], core.identb[:], core.maskb[:],
                                     start=False, stop=True).then_inc(s_ready, 1)

                def transpose(i, j):
                    q = items[j][1]
                    g = i * n_items + j
                    pe.wait_ge(probs_ready, g + 1 + 2)
                    pe.wait_ge(pt_ready, g + 1)
                    for k in range(q + 1):
                        last = nc.tensor.transpose(ps_t[j % 2][:, k * P:(k + 1) * P], probs[:, j % 2, k * P:(k + 1) * P], core.ident[:])
                    last.then_inc(pt_psum, 1)

                def values(i, j):
                    u, q, h = items[j]
                    if q == 0 and h == 0:
                        pe.wait_ge(v_ready, i * B + u + 1 + 1)
                    if h == 0:
                        pe.wait_ge(y_ready, i * n_tiles + u * QT + q + 1)
                    pe.wait_ge(pt_ready, i * n_items + j + 1 + 2)
                    for k in range(q + 1):
                        last = nc.tensor.matmul(ps_y[:, h * dv:(h + 1) * dv], probs_t[:, j % 2, k, :], vs[:, u, k, h * dv:(h + 1) * dv],
                                                start=k == 0, stop=k == q)
                    last.then_inc(y_psum, 1)

                def y_transpose(i, j):
                    u, q, h = items[j]
                    if h == heads - 1:
                        if q == 0:
                            pe.wait_ge(sum_done, i * B + u + 1)
                        pe.wait_ge(y_ready, i * n_tiles + u * QT + q + 1 + 1)
                        nc.tensor.transpose(ps_o[:, q * P:(q + 1) * P], y[:, q % 2, :], core.ident[:]).then_inc(yt_psum, 1)

                def out(i, j):
                    u = items[j][0]
                    if j % per_unit == per_unit - 1:
                        if u == 0:
                            pe.wait_ge(w_loaded[3], 16 * i + 16)
                        pe.wait_ge(yt_ready, i * B + u + 1)
                        nc.tensor.matmul(ps_o, w[3][:], y_t[:], start=True, stop=True).then_inc(unit_done, 1)

                def group(i, first, last):
                    for j in range(n_items + (3 if last else 0)):
                        if j + 1 < n_items or not last:
                            scores(*whole(i, j + 1))
                        if j < n_items:
                            transpose(i, j)
                        for step, back in ((values, 1), (out, 3), (y_transpose, 2)):
                            if (j >= back or not first) and j - back < n_items:
                                step(*whole(i, j - back))
                        u = j // per_unit + AHEAD
                        if j % per_unit < 3 and (u < B or not last):
                            project(i + u // B, u % B, j % per_unit)

                for u in range(AHEAD):
                    for part in range(3):
                        project(0, u, part)
                scores(0, 0)
                per_group(pe, group)

            @block.scalar
            def _(act):
                nc.scalar.preload_act_table_set("natural_log_exp_and_others")
                act.sem_inc(probs_ready, 2)

                def unrotated(i, u, part):
                    U = i * B + u
                    act.wait_ge(qk_ready, 2 * U + part + 1)
                    act.wait_ge(proj_ready, 3 * U + part + 1)
                    bias = {"bias": w[part][:, P:P + 1]} if qk_bias else {}
                    nc.scalar.activation(raw[:, part, :], ps_p[part], ACT.Identity, **bias).then_inc(raw_ready, 1)

                def group(i, first, last):
                    for j, (u, q, h) in enumerate(items):
                        g = i * n_items + j
                        act.wait_ge(max_ready, g + 1)
                        act.wait_ge(pt_psum, g + 1)
                        nc.scalar.activation(probs[:, j % 2, 0:(q + 1) * P], ps_s[j % 2][:, 0:(q + 1) * P], ACT.Exp,
                                             bias=nmax[:, j % 4:j % 4 + 1], accum_out=rsum[:, q, h:h + 1]).then_inc(probs_ready, 1)
                        if 1 <= j % per_unit < 3 and (u + AHEAD < B or not last):
                            unrotated(i + (u + AHEAD) // B, (u + AHEAD) % B, j % per_unit - 1)

                for u in range(AHEAD):
                    unrotated(0, u, 0)
                    unrotated(0, u, 1)
                per_group(act, group)

            @block.vector
            def _(dve):
                dve.sem_inc(v_ready, 1)
                dve.sem_inc(pt_ready, 2)
                dve.sem_inc(y_ready, 1)
                dve.sem_inc(sum_done, 1)

                def project(i, u, part):
                    U = i * B + u
                    if part == 2:
                        dve.wait_ge(unit_done, U + 1)
                        dve.wait_ge(proj_ready, 3 * U + 3)
                        of = ps_p[0].rearrange("p (t d) -> p t d", d=P)
                        if v_bias is None:
                            nc.vector.tensor_copy(vs[:, u, :, :], of).then_inc(v_ready, 1)
                        else:
                            bias = v_bias[:, bass.ds(i * P, P)].unsqueeze(1).to_broadcast([P, QT, P])
                            nc.vector.tensor_tensor(vs[:, u, :, :], of, bias, ALU.add).then_inc(v_ready, 1)
                    else:
                        dve.wait_ge(raw_ready, 2 * U + part + 1)
                        dve.wait_ge(qk_ready, 2 * U + part + 1)
                        nc.vector.tensor_tensor(rot[:, part, :], raw[:, part, :], tables[:, 2 * part, :], ALU.mult).then_inc(cos_ready, 1)

                def maximum(i, j):
                    q = items[j][1]
                    dve.wait_ge(s_ready, i * n_items + j + 1)
                    nc.vector.tensor_reduce(nmax[:, j % 4:j % 4 + 1], ps_s[j % 2][:, 0:(q + 1) * P], AX.X, ALU.max, negate=True).then_inc(max_ready, 1)

                def copy_t(i, j):
                    q = items[j][1]
                    g = i * n_items + j
                    dve.wait_ge(pt_psum, g + 1 + 2)
                    dve.wait_ge(y_psum, g + 1)
                    nc.vector.tensor_copy(probs_t[:, j % 2, 0:q + 1, :].rearrange("p k n -> p (k n)"), ps_t[j % 2][:, 0:(q + 1) * P]).then_inc(pt_ready, 1)

                def normalise(i, j):
                    u, q, h = items[j]
                    if h == heads - 1:
                        tile = i * n_tiles + u * QT + q
                        dve.wait_ge(y_psum, i * n_items + j + 1 + 2)
                        nc.vector.reciprocal(rinv[:, q, :], rsum[:, q, :]).then_inc(rinv_ready, 1)
                        dve.wait_ge(rinv_ready, tile + 1)
                        dve.wait_ge(yt_psum, tile + 1)
                        nc.vector.tensor_tensor(y[:, q % 2, :].rearrange("p (h d) -> p h d", h=heads), ps_y.rearrange("p (h d) -> p h d", h=heads),
                                                rinv[:, q, :].unsqueeze(2).to_broadcast([P, heads, dv]), ALU.mult).then_inc(y_ready, 1)

                def copy_y(i, j):
                    if j % per_unit == per_unit - 1:
                        U = i * B + items[j][0]
                        dve.wait_ge(yt_psum, (U + 1) * QT + 2)
                        dve.wait_ge(unit_done, U + B)
                        nc.vector.tensor_copy(y_t[:], ps_o).then_inc(yt_ready, 1)

                def add_out(i, j):
                    if j % per_unit == per_unit - 1:
                        u = items[j][0]
                        U = i * B + u
                        dve.wait_ge(unit_done, U + 1 + B)
                        dve.wait_ge(sum_done, U + 1)
                        nc.vector.tensor_tensor(core.sum[:, cols(u)], ps_o, core.sum[:, cols(u)], ALU.add).then_inc(sum_done, 1)

                def group(i, first, last):
                    for j in range(n_items + (3 if last else 0)):
                        if j + 1 < n_items or not last:
                            maximum(*whole(i, j + 1))
                        if j < n_items:
                            copy_t(i, j)
                        for step, back in ((add_out, 3), (normalise, 1), (copy_y, 2)):
                            if (j >= back or not first) and j - back < n_items:
                                step(*whole(i, j - back))
                        u, part = j // per_unit + AHEAD, j % per_unit - 1
                        if 0 <= part < 3 and (u < B or not last) and j < n_items:
                            project(i + u // B, u % B, part)

                for u in range(AHEAD):
                    for part in range(3):
                        project(0, u, part)
                maximum(0, 0)
                per_group(dve, group)


def attn2(core):
    nc = core.nc
    init_sum(core, "i2", core.x)
    with Stage(core, "a2t") as st:
        tables = st.sb("tables", [P, 4, T])
        loaded = st.sem("loaded")
        with nc.Block() as block:
            @block.sync
            def _(sp):
                sp.dma_start(tables[:], core.dram["c_rope2"]).then_inc(loaded, 16)
                sp.wait_ge(loaded, 16)
        rope_attention(core, "a2", x=core.x, groups=8, heads=1, q_rows=P, w_dram=core.dram["l2_heads"], tables=tables)


def direction_scores(core, w_wide, q_parts, k_parts, v_aug):
    nc, dram = core.nc, core.dram
    with Stage(core, "a1p") as st:
        wv = st.sb("wv", [P, P])
        part_cols = st.sb("part_cols", [P, 5])
        raw = st.sb("raw", [P, 4, T])
        high = st.sb("high", [P, 4, T], BF16)
        rest = st.sb("rest", [P, 4, T])
        middle = st.sb("middle", [P, 4, T], BF16)
        (loaded, proj_ready, raw_ready, high_ready, rest_ready, middle_ready, parts_ready, v_psum, v_zero, v_ones) = (
            st.sem(n) for n in ("loaded", "proj_ready", "raw_ready", "high_ready", "rest_ready", "middle_ready", "parts_ready",
                                "v_psum", "v_zero", "v_ones"))
        items = [(b, kind, g) for b in range(B) for kind in range(2) for g in range(2)]
        ps = [core.psum[:, k, :] for k in range(4)]
        with nc.Block() as block:
            @block.sync
            def _(sp):
                sp.dma_start(wv[:], dram["l1_wv"]).then_inc(loaded, 16)
                sp.dma_start(part_cols[:], dram["c_parts"]).then_inc(loaded, 16)

            @block.tensor
            def _(pe):
                pe.wait_ge(loaded, 2 * 16)
                for n, (b, kind, g) in enumerate(items):
                    if n >= 4:
                        pe.wait_ge(high_ready, n - 3)
                    nc.tensor.matmul(ps[n % 4], w_wide[:, kind, g, :], core.x[:, cols(b)], start=True, stop=True).then_inc(proj_ready, 1)
                    if kind == 1 and g == 1:
                        for t in range(QT):
                            at = b * T + t * P
                            last = nc.tensor.matmul(core.psum[:, 4 + b, t * P:(t + 1) * P], core.x[:, at:at + P], wv[:], start=True, stop=True)
                        last.then_inc(v_psum, 1)

            @block.scalar
            def _(act):
                act.wait_ge(loaded, 2 * 16)
                for n, (b, kind, g) in enumerate(items):
                    act.wait_ge(proj_ready, n + 1)
                    if n >= 4:
                        act.wait_ge(parts_ready, n - 3)
                    bias = {"bias": part_cols[:, 4:5]} if kind == 1 else {}
                    nc.scalar.activation(raw[:, n % 4, :], ps[n % 4], ACT.Identity, **bias).then_inc(raw_ready, 1)
                    nc.scalar.activation(high[:, n % 4, :], ps[n % 4], ACT.Identity, **bias).then_inc(high_ready, 1)

            @block.gpsimd
            def _(pool):
                nc.gpsimd.memset(v_aug[:], 0.0).then_inc(v_zero, 1)
                for n in range(len(items)):
                    pool.wait_ge(rest_ready, n + 1)
                    if n >= 4:
                        pool.wait_ge(parts_ready, n - 3)
                    nc.gpsimd.tensor_copy(middle[:, n % 4, :], rest[:, n % 4, :]).then_inc(middle_ready, 1)

            @block.vector
            def _(dve):
                dve.wait_ge(loaded, 2 * 16)

                def remainder(n):
                    kind = items[n][1]
                    dve.wait_ge(high_ready, n + 1)
                    nc.vector.scalar_tensor_tensor(rest[:, n % 4, :], high[:, n % 4, :], part_cols[:, 2 * kind:2 * kind + 1],
                                                   raw[:, n % 4, :], ALU.mult, ALU.add).then_inc(rest_ready, 1)

                remainder(0)
                for n, (b, kind, g) in enumerate(items):
                    if n + 1 < len(items):
                        remainder(n + 1)
                    dve.wait_ge(middle_ready, n + 1)
                    to = (q_parts, k_parts)[kind][:, g, cols(b)]
                    nc.vector.scalar_tensor_tensor(to, middle[:, n % 4, :], part_cols[:, 2 * kind + 1:2 * kind + 2],
                                                   rest[:, n % 4, :], ALU.mult, ALU.add).then_inc(parts_ready, 1)
                    if kind == 1 and g == 1:
                        if b == 0:
                            dve.wait_ge(v_zero, 1)
                            nc.vector.memset(v_aug[:, :, :, 16:17], 1.0).then_inc(v_ones, 1)
                        dve.wait_ge(v_psum, b + 1)
                        nc.vector.tensor_copy(v_aug[:, b * QT:(b + 1) * QT, :, 0:16].rearrange("p t h d -> p (t h) d"),
                                              core.psum[:, 4 + b, :].rearrange("p (n d) -> p n d", d=16))


def direction_attention(core, q_parts, k_parts, v_aug, w_out, sum_spread):
    nc = core.nc
    first_items = [(h, q) for h in range(4) for q in range(QT)]
    second_items = [(h, k) for h in range(4) for k in range(QT)]
    n = len(first_items)
    in_slot = [[k for k in range(n) if k * 3 // 4 == j] for j in range(n)]
    with Stage(core, "a1") as st:
        nmax = st.sb("nmax", [P, QT, 4])
        nrest = st.sb("nrest", [P, QT, 4])
        nparts = st.sb("nparts", [P, QT, 4, 32], BF16)
        q_first, k_first, k_second = (st.sb(name, [P, 2, T], BF16) for name in ("q_first", "k_first", "k_second"))
        q_less = st.sb("q_less", [P, 2, T], BF16)
        v = st.sb("v", [P, 2, QT, P])
        probs_t = st.sb("probs_t", [P, 2, T])
        y = st.sb("y", [P, 2, T])
        ln_sum = st.sb("ln_sum", [P, T])
        inv_sum = st.sb("inv_sum", [P, T])
        yn = st.sb("yn", [P, 2, T])
        (zeroed, a_ready, max_ready, nparts_ready, rows_ready, q_ready, s_ready, probs_ready, first_ready, second_ready, values_done, y_ready,
         sums_ready, ln_ready, inv_ready, yn_ready, out_done, sum_done, split_step, passed) = (st.sem(n) for n in (
             "zeroed", "a_ready", "max_ready", "nparts_ready", "rows_ready", "q_ready", "s_ready", "probs_ready", "first_ready", "second_ready",
             "values_done", "y_ready", "sums_ready", "ln_ready", "inv_ready", "yn_ready", "out_done", "sum_done", "split_step",
             "passed"))
        ps_a = [core.psum[:, k, :] for k in range(2)]
        ps_s = [core.psum[:, 2 + k, :] for k in range(2)]
        ps_y = [core.psum[:, 4 + k, :] for k in range(2)]
        ps_m = core.psum[:, 6, :]
        ps_o = core.psum[:, 7, :]

        def per_sequence(engine, body):
            body(0, True, False)
            with engine.Fori(1, B - 1) as b:
                body(b, False, False)
            body(B - 1, False, True)

        def ahead(b, g):
            return (b, 1) if g == 0 else (b + 1, 0)

        def behind(b, g):
            return (b, 0) if g == 1 else (b - 1, 1)

        with nc.Block() as block:
            @block.gpsimd
            def _(pool):
                nc.gpsimd.memset(nparts[:], 0.0).then_inc(zeroed, 1)
                with pool.Fori(0, B) as b:
                    for g in range(2):
                        pool.wait_ge(a_ready, (2 * b + g) * n + n)
                        pool.sem_inc(passed, 1)
                        nc.gpsimd.tensor_copy(q_first[:, g, :], q_parts[:, g, cols(b)])
                        nc.gpsimd.tensor_copy(k_first[:, g, :], k_parts[:, g, cols(b)]).then_inc(first_ready, 1)
                        pool.wait_ge(values_done, (2 * b + g) * n + n)
                        pool.sem_inc(passed, 1)
                        nc.gpsimd.tensor_copy(k_second[:, g, :], k_parts[:, g, cols(b)])
                        nc.gpsimd.tensor_copy(v[:, g, :, :], v_aug[:].rearrange("p t h d -> p t (h d)")[:, bass.ds(b * QT, QT), g * P:(g + 1) * P]).then_inc(second_ready, 1)

            @block.tensor
            def _(pe):
                pe.sem_inc(a_ready, 2 * n)
                pe.sem_inc(values_done, 2 * n)
                pe.sem_inc(out_done, 2)

                def first_scores(b, g, k):
                    h, q = first_items[k]
                    rows = slice(32 * h, 32 * h + 32)
                    if k == 0:
                        pe.wait_ge(first_ready, 2 * b + g + 1)
                    pe.wait_ge(max_ready, (2 * b + g) * n + k + 1)
                    nc.tensor.matmul(ps_a[k % 2][:, 0:(q + 1) * P], q_first[rows, g, q * P:(q + 1) * P],
                                     k_first[rows, g, 0:(q + 1) * P], start=True, stop=False)
                    nc.tensor.matmul(ps_a[k % 2][:, q * P:(q + 1) * P], core.identb[:], core.maskb[:],
                                     start=False, stop=True).then_inc(a_ready, 1)

                def max_rows(b, g):
                    U = 2 * b + g
                    pe.wait_ge(nparts_ready, U + 1)
                    pe.wait_ge(ln_ready, U + 1)
                    for t in range(QT):
                        last = nc.tensor.matmul(ps_m[:, t * P:(t + 1) * P], nparts[:, t, :, :].rearrange("p h r -> p (h r)"), core.identb[:],
                                                start=True, stop=True)
                    last.then_inc(rows_ready, 1)

                def second_scores(b, g, j):
                    h, k = second_items[j]
                    rows, size = slice(32 * h, 32 * h + 32), (QT - k) * P
                    U = 2 * b + g
                    if j == 0:
                        pe.wait_ge(second_ready, U + 1)
                        pe.wait_ge(q_ready, U + 1)
                    pe.wait_ge(probs_ready, U * n + j + 1)
                    nc.tensor.matmul(ps_s[j % 2][:, 0:size], k_second[rows, g, k * P:(k + 1) * P], q_less[rows, g, k * P:T],
                                     start=True, stop=False)
                    nc.tensor.matmul(ps_s[j % 2][:, 0:P], core.maskb[:], core.identb[:], start=False, stop=True).then_inc(s_ready, 1)

                def values(b, g, j):
                    h, k = second_items[j]
                    U = 2 * b + g
                    if j == 0:
                        pe.wait_ge(y_ready, U + 1)
                    pe.wait_ge(probs_ready, U * n + j + 1 + 2)
                    nc.tensor.matmul(ps_y[g][32 * h:32 * h + 32, k * P:T], v[:, g, k, 32 * h:32 * h + 32], probs_t[:, j % 2, 0:(QT - k) * P],
                                     start=k == 0, stop=k == QT - 1, skip_group_check=True).then_inc(values_done, 1)

                def spread_sums(b, g):
                    pe.wait_ge(y_ready, 2 * b + g + 1 + 2)
                    nc.tensor.matmul(ps_m, sum_spread[:], y[:, g, :], start=True, stop=True).then_inc(sums_ready, 1)

                def out(b, g):
                    pe.wait_ge(yn_ready, 2 * b + g + 1 + 2)
                    if g == 0:
                        pe.wait_ge(sum_done, b + 1)
                    nc.tensor.matmul(ps_o, w_out[:, g, :], yn[:, g, :], start=g == 0, stop=g == 1, skip_group_check=True).then_inc(out_done, 1)

                def sequence(b, first, last):
                    for g in range(2):
                        nxt = None if last and g == 1 else ahead(b, g)
                        for j in range(n):
                            if j + 1 < n:
                                second_scores(b, g, j + 1)
                            elif nxt:
                                second_scores(*nxt, 0)
                            for k in in_slot[j] if nxt else []:
                                first_scores(*nxt, k)
                            values(b, g, j)
                            if j == 1 and not (first and g == 0):
                                spread_sums(*behind(b, g))
                            if j == 6 and not (first and g == 0):
                                out(*behind(b, g))
                            if j == 13 and nxt:
                                max_rows(*nxt)

                for k in range(n):
                    first_scores(0, 0, k)
                max_rows(0, 0)
                second_scores(0, 0, 0)
                per_sequence(pe, sequence)
                spread_sums(B - 1, 1)
                out(B - 1, 1)

            @block.scalar
            def _(act):
                nc.scalar.preload_act_table_set("natural_log_exp_and_others")
                act.sem_inc(probs_ready, 2)
                act.sem_inc(y_ready, 2)
                act.sem_inc(ln_ready, 2)

                def probabilities(b, g, j):
                    size = (QT - second_items[j][1]) * P
                    U = 2 * b + g
                    act.wait_ge(s_ready, U * n + j + 1)
                    act.wait_ge(values_done, U * n + j - 1 + 2 * n)
                    nc.scalar.activation(probs_t[:, j % 2, 0:size], ps_s[j % 2][:, 0:size], ACT.Exp).then_inc(probs_ready, 1)

                def copy_y(b, g):
                    U = 2 * b + g
                    act.wait_ge(values_done, U * n + n + 2 * n)
                    act.wait_ge(yn_ready, U + 1)
                    nc.scalar.activation(y[:, g, :], ps_y[g], ACT.Identity).then_inc(y_ready, 1)

                def inverse(b, g):
                    U = 2 * b + g
                    act.wait_ge(sums_ready, U + 1)
                    nc.scalar.activation(ln_sum[:], ps_m, ACT.Ln).then_inc(ln_ready, 1)
                    act.wait_ge(ln_ready, U + 1 + 2)
                    act.wait_ge(yn_ready, U + 2)
                    nc.scalar.activation(inv_sum[:], ln_sum[:], ACT.Exp, scale=-1.0).then_inc(inv_ready, 1)

                def sequence(b, first, last):
                    for g in range(2):
                        for j in range(n):
                            probabilities(b, g, j)
                            if j == 0 and not (first and g == 0):
                                copy_y(*behind(b, g))
                            if j == 2 and not (first and g == 0):
                                inverse(*behind(b, g))

                per_sequence(act, sequence)
                copy_y(B - 1, 1)
                inverse(B - 1, 1)

            @block.vector
            def _(dve):
                dve.sem_inc(max_ready, 2)
                dve.sem_inc(yn_ready, 2)
                dve.sem_inc(sum_done, 1)
                dve.wait_ge(zeroed, 1)

                def maximum(b, g, k):
                    h, q = first_items[k]
                    dve.wait_ge(a_ready, (2 * b + g) * n + k + 1 + 2 * n)
                    nc.vector.tensor_reduce(nmax[:, q, h:h + 1], ps_a[k % 2][:, 0:(q + 1) * P], AX.X, ALU.max, negate=True).then_inc(max_ready, 1)

                def split_maxima(b, g):
                    U = 2 * b + g
                    step = Steps(dve, split_step, U * 3)
                    dve.wait_ge(max_ready, U * n + n + 2)
                    step(nc.vector.tensor_copy(nparts[:, :, :, 24], nmax[:]))
                    step(nc.vector.tensor_tensor(nrest[:], nmax[:], nparts[:, :, :, 24], ALU.subtract))
                    step(nc.vector.tensor_copy(nparts[:, :, :, 25], nrest[:]))
                    nc.vector.tensor_tensor(nparts[:, :, :, 26], nrest[:], nparts[:, :, :, 25], ALU.subtract).then_inc(nparts_ready, 1)

                def less_maxima(b, g):
                    dve.wait_ge(rows_ready, 2 * b + g + 1)
                    nc.vector.tensor_tensor(q_less[:, g, :], ps_m, q_parts[:, g, cols(b)], ALU.add).then_inc(q_ready, 1)

                def normalise(b, g):
                    U = 2 * b + g
                    dve.wait_ge(inv_ready, U + 1)
                    dve.wait_ge(out_done, U + 1)
                    nc.vector.tensor_tensor(yn[:, g, :], y[:, g, :], inv_sum[:], ALU.mult).then_inc(yn_ready, 1)

                def add_out(b):
                    dve.wait_ge(out_done, 2 * b + 2 + 2)
                    nc.vector.tensor_tensor(core.sum[:, cols(b)], ps_o, core.x[:, cols(b)], ALU.add).then_inc(sum_done, 1)

                def sequence(b, first, last):
                    for g in range(2):
                        nxt = None if last and g == 1 else ahead(b, g)
                        for j in range(n):
                            for k in in_slot[j] if nxt else []:
                                maximum(*nxt, k)
                            if j == 4 and not (first and g == 0):
                                normalise(*behind(b, g))
                            if j == 8 and g == 0 and not first:
                                add_out(b - 1)
                            if j == 12 and nxt:
                                split_maxima(*nxt)
                            if j == 14 and nxt:
                                less_maxima(*nxt)

                for k in range(n):
                    maximum(0, 0, k)
                split_maxima(0, 0)
                less_maxima(0, 0)
                per_sequence(dve, sequence)
                normalise(B - 1, 1)
                add_out(B - 1)



def attn1(core):
    nc, dram = core.nc, core.dram
    with Stage(core, "a1w") as st:
        w_wide = st.sb("w_wide", [P, 2, 2, P])
        w_out = st.sb("w_out", [P, 2, P])
        sum_spread = st.sb("sum_spread", [P, P])
        q_parts, k_parts = (st.sb(n, [P, 2, N], BF16) for n in ("q_parts", "k_parts"))
        v_aug = st.sb("v_aug", [P, NT, 8, 32])
        w3 = st.sb("w3", [24, 2, P])
        spread = st.sb("spread", [24, 2 * P])
        scale = st.sb("scale", [P, 1])
        loaded, wide_psum, wide_ready = (st.sem(n) for n in ("loaded", "wide_psum", "wide_ready"))
        with nc.Block() as block:
            @block.sync
            def _(sp):
                sp.dma_start(w3[:, 0, :], dram["l1_wq"]).then_inc(loaded, 16)
                sp.dma_start(w3[:, 1, :], dram["l1_wk"]).then_inc(loaded, 16)
                sp.dma_start(spread[:], dram["c_spread"]).then_inc(loaded, 16)
                sp.dma_start(scale[:], dram["l1_scale"].partition_broadcast(P)).then_inc(loaded, 16)
                sp.dma_start(w_out[:], dram["l1_wout"]).then_inc(loaded, 16)
                sp.dma_start(sum_spread[:], dram["c_sumspread"]).then_inc(loaded, 16)

            @block.tensor
            def _(pe):
                pe.wait_ge(loaded, 6 * 16)
                for k in range(2):
                    nc.tensor.matmul(core.psum[:, k, 0:2 * P], w3[:, k, :], spread[:], start=True, stop=True).then_inc(wide_psum, 1)

            @block.vector
            def _(dve):
                dve.wait_ge(loaded, 6 * 16)
                dve.wait_ge(wide_psum, 2)
                for k in range(2):
                    last = nc.vector.tensor_copy(w_wide[:, k, :, :].rearrange("p g r -> p (g r)"), core.psum[:, k, 0:2 * P])
                last.then_inc(wide_ready, 1)
                dve.wait_ge(wide_ready, 1)
                rows = w_wide[:, 0, :, :].rearrange("p g (h r) -> p (g h) r", r=32)[:, :, 0:24].rearrange("p h (m c) -> p h m c", c=4)
                nc.vector.tensor_scalar(rows[:, :, :, 0:3], rows[:, :, :, 0:3], scale[:], None, ALU.mult)
        direction_scores(core, w_wide, q_parts, k_parts, v_aug)
        direction_attention(core, q_parts, k_parts, v_aug, w_out, sum_spread)


def rope_tables(core, tables, theta_dram, scale):
    nc = core.nc
    two_pi = 2 * np.pi
    c1 = 6.28125
    c2 = float(np.float32(np.round((two_pi - c1) * 2 ** 22) / 2 ** 22))
    c3 = float(two_pi - c1 - c2)
    magic = 1.5 * 2 ** 23
    with Stage(core, "rt") as st:
        pos, ang, turns, sin_h = (st.sb(n, [P, T]) for n in ("pos", "ang", "turns", "sin_h"))
        col = st.sb("col", [P, 2])
        loaded, reduced, sin_ready, dve_step = (st.sem(n) for n in ("loaded", "reduced", "sin_ready", "dve_step"))
        sin = tables[:, 3, :]
        with nc.Block() as block:
            @block.sync
            def _(sp):
                sp.dma_start(pos[:], core.dram["c_pos"].partition_broadcast(P)).then_inc(loaded, 16)
                sp.dma_start(col[:, 0:1], theta_dram).then_inc(loaded, 16)
                sp.dma_start(col[:, 1:2], core.dram["c_ropesign"]).then_inc(loaded, 16)

            @block.scalar
            def _(act):
                act.wait_ge(reduced, 1)
                nc.scalar.activation(sin, ang[:], ACT.Sin).then_inc(sin_ready, 1)
                nc.scalar.activation(sin_h[:], ang[:], ACT.Sin, scale=0.5).then_inc(sin_ready, 1)

            @block.vector
            def _(dve):
                step = Steps(dve, dve_step)
                dve.wait_ge(loaded, 3 * 16)
                step(nc.vector.tensor_scalar(ang[:], pos[:], col[:, 0:1], None, ALU.mult))
                step(nc.vector.tensor_scalar(turns[:], ang[:], 1 / two_pi, None, ALU.mult))
                step(nc.vector.tensor_scalar(turns[:], turns[:], magic, None, ALU.add))
                step(nc.vector.tensor_scalar(turns[:], turns[:], magic, None, ALU.subtract))
                for c in (c1, c2, c3):
                    step(nc.vector.scalar_tensor_tensor(ang[:], turns[:], -c, ang[:], ALU.mult, ALU.add))
                nc.vector.tensor_scalar(ang[:], ang[:], 3.1415925, -3.1415925, ALU.min, ALU.max).then_inc(reduced, 1)
                dve.wait_ge(sin_ready, 2)
                step(nc.vector.tensor_scalar(sin, sin, col[:, 1:2], None, ALU.mult))
                step(nc.vector.tensor_tensor(sin_h[:], sin_h[:], sin_h[:], ALU.mult))
                step(nc.vector.tensor_scalar(tables[:, 2, :], sin_h[:], -2.0, 1.0, ALU.mult, ALU.add))
                nc.vector.tensor_scalar(tables[:, 0:2, :], tables[:, 2:4, :], scale, None, ALU.mult)


def ffn2(core):
    nc, d = core.nc, core.dram
    with Stage(core, "f2") as st:
        xn = st.sb("xn", [P, N])
        gammas = st.sb("gammas", [P, 2])
        loaded = st.sem("loaded")
        with nc.Block() as block:
            @block.sync
            def _(sp):
                sp.dma_start(gammas[:], d["l2_gammas"]).then_inc(loaded, 16)
                sp.wait_ge(loaded, 16)
        norm(core, "g1", core.x, xn, False, 0, gammas[:, 0:1])
        init_sum(core, "if2", xn, d["l2_ob"])
        with Stage(core, "a2f") as sa:
            tables = sa.sb("tables", [P, 4, T])
            v_bias = sa.sb("v_bias", [P, 8 * P])
            b_loaded = sa.sem("b_loaded")
            rope_tables(core, tables, d["l2_theta"], 64 ** -0.5)
            with nc.Block() as block:
                @block.sync
                def _(sp):
                    sp.dma_start(v_bias[:], d["l2_vb"].partition_broadcast(P)).then_inc(b_loaded, 16)
                    sp.wait_ge(b_loaded, 16)
            rope_attention(core, "h2", x=xn, groups=8, heads=2, q_rows=64, w_dram=d["l2f_heads"], tables=tables,
                      qk_bias=True, v_bias=v_bias)
        an = st.sb("an", [P, N])
        norm(core, "g2", core.sum, an, False, 0, gammas[:, 1:2])
        added = st.sem("added")
        with nc.Block() as block:
            @block.vector
            def _(dve):
                nc.vector.tensor_tensor(xn[:], an[:], core.sum[:], ALU.add).then_inc(added, 1)
                dve.wait_ge(added, 1)
                nc.vector.tensor_tensor(xn[:], xn[:], core.x[:], ALU.add)
        gt, g3 = st.sb("gates_t", [32, N]), st.sb("gates3", [GR, N], BF16)
        b2 = st.sb("b2", [32, P])
        b2_loaded = st.sem("b2_loaded")
        with nc.Block() as block:
            @block.sync
            def _(sp):
                sp.dma_start(b2[:], d["l2_b2"]).then_inc(b2_loaded, 16)
                sp.wait_ge(b2_loaded, 16)
        router(core, "r2", "softmax_top", x=an, w_dram=d["l2_router"], n_experts=31, top=3, gates_t=gt, gates3=g3,
               bias_dram=d["l2_rbias"])
        experts(core, "e2", act_func=ACT.Gelu, x=an, resid=xn, gates_t=gt, gates3=g3, n_slots=32, unroll=4, tiles=1,
                w_dram=d["l2_experts"], with_b1=True, b2=b2, b2_rows=32)


def hawk(core):
    nc, d = core.nc, core.dram
    with Stage(core, "h3") as st:
        xn = st.sb("xn", [P, N])
        x2 = st.sb("x2", [P, N])
        gammas = st.sb("gammas", [P, 2])
        loaded = st.sem("loaded")
        with nc.Block() as block:
            @block.sync
            def _(sp):
                sp.dma_start(gammas[:], d["l3_gammas"]).then_inc(loaded, 16)
                sp.wait_ge(loaded, 16)
        norm(core, "g3", core.x, xn, False, 2, gammas[:, 0:1])
        recurrence(core, xn, x2)
        norm(core, "g4", x2, xn, False, 2, gammas[:, 1:2])
        gated_mlp(core, xn, x2)


def recurrence(core, xn, x2):
    nc, d = core.nc, core.dram
    K = 4
    C = 2
    with Stage(core, "rc") as st:
        w_in = st.sb("w_in", [P, 4 * P])
        w_g = st.sb("w_g", [P, C, 4 * P])
        w_out = st.sb("w_out", [P, C, P])
        taps = st.sb("taps", [P, C, K])
        cols_ = st.sb("cols", [P, 8])
        coef = st.sb("coef", [P, C])
        small = st.sb("small", [P, 6, C])
        gate = st.sb("gate", [P, C, T])
        padded = st.sb("padded", [P, C, K - 1 + T])
        xc, alpha, inp, beta, h = (st.sb(n, [P, C, T]) for n in ("xc", "alpha", "inp", "beta", "h"))
        (loaded, abs_ready, u_ready, coef_ready, z_ready, gate_ready, conv_ready, g_ready, sig_ready, alpha_ready,
         sq_ready, rest_ready, ln_ready, beta_ready, scan_ready, h_ready, out_ready, chunk_done, dve_step) = (st.sem(n) for n in (
             "loaded", "abs_ready", "u_ready", "coef_ready", "z_ready", "gate_ready", "conv_ready", "g_ready", "sig_ready",
             "alpha_ready", "sq_ready", "rest_ready", "ln_ready", "beta_ready", "scan_ready", "h_ready", "out_ready", "chunk_done", "dve_step"))
        bank = [core.psum[:, k, :] for k in range(8)]
        loads = [(w_in[:], d["l3_win"]), (w_g[:], d["l3_wgates"]), (w_out[:], d["l3_wout"]), (taps[:], d["l3_taps"]), (cols_[:], d["l3_cols"])]
        DVE_STEPS = 4 + 1 + 1

        with nc.Block() as block:
            @block.sync
            def _(sp):
                for to, of in loads:
                    sp.dma_start(to, of).then_inc(loaded, 16)

            @block.tensor
            def _(pe):
                pe.wait_ge(loaded, 16 * len(loads))
                with pe.Fori(0, B) as c:
                    pe.wait_ge(chunk_done, c + 1)
                    for k in range(4):
                        nc.tensor.matmul(bank[k], w_in[:, k * P:(k + 1) * P], xn[:, cols(c)], start=True, stop=True).then_inc(z_ready, 1)
                    pe.wait_ge(conv_ready, c + 1)
                    for m in range(4):
                        for k in range(C):
                            last = nc.tensor.matmul(bank[4 + m], w_g[:, k, m * P:(m + 1) * P], xc[:, k, :], start=k == 0, stop=k == C - 1)
                        last.then_inc(g_ready, 1)
                    pe.wait_ge(h_ready, c + 1)
                    for k in range(C):
                        last = nc.tensor.matmul(bank[0], w_out[:, k, :], h[:, k, :], start=k == 0, stop=k == C - 1)
                    last.then_inc(out_ready, 1)

            @block.scalar
            def _(act):
                act.wait_ge(loaded, 16 * len(loads))
                nc.scalar.activation(small[:, 0, :], cols_[:, 6:8], ACT.Abs).then_inc(abs_ready, 1)
                act.wait_ge(abs_ready, 1)
                nc.scalar.activation(small[:, 1, :], small[:, 0, :], ACT.Exp, scale=-1.0).then_inc(u_ready, 1)
                act.wait_ge(coef_ready, 1)
                with act.Fori(0, B) as c:
                    for k in range(C):
                        act.wait_ge(z_ready, 4 * c + k + 1)
                        nc.scalar.activation(gate[:, k, :], bank[k], ACT.Gelu).then_inc(gate_ready, 1)
                    for m in range(4):
                        act.wait_ge(g_ready, 4 * c + m + 1)
                        to = alpha[:, m, :] if m < C else inp[:, m - C, :]
                        nc.scalar.activation(to, bank[4 + m], ACT.Sigmoid, bias=cols_[:, 2 + m:3 + m]).then_inc(sig_ready, 1)
                    nc.scalar.preload_act_table_set("natural_log_exp_and_others")
                    act.wait_ge(sig_ready, 4 * c + 4)
                    for k in range(C):
                        nc.scalar.activation(alpha[:, k, :], alpha[:, k, :], ACT.Exp, scale=coef[:, k:k + 1]).then_inc(alpha_ready, 1)
                    for k in range(C):
                        act.wait_ge(alpha_ready, 2 * c + k + 1)
                        nc.scalar.activation(beta[:, k, :], alpha[:, k, :], ACT.Square).then_inc(sq_ready, 1)
                    act.wait_ge(rest_ready, c + 1)
                    nc.scalar.activation(beta[:], beta[:], ACT.Ln, bias=core.eps[:, 1:2]).then_inc(ln_ready, 1)
                    act.wait_ge(ln_ready, c + 1)
                    nc.scalar.activation(beta[:], beta[:], ACT.Exp, scale=0.5).then_inc(beta_ready, 1)

            @block.vector
            def _(dve):
                u, s, s2, p, pos = (small[:, k, :] for k in range(1, 6))
                dve.sem_inc(chunk_done, 1)
                dve.wait_ge(loaded, 16 * len(loads))
                dve.wait_ge(u_ready, 1)
                pre = Steps(dve, dve_step)
                pre(nc.vector.tensor_scalar(s2, u, 2.0, None, ALU.add))
                pre(nc.vector.reciprocal(s2, s2))
                pre(nc.vector.tensor_tensor(s, u, s2, ALU.mult))
                pre(nc.vector.tensor_tensor(s2, s, s, ALU.mult))
                pre(nc.vector.memset(p, 1 / 19))
                for n in range(17, 0, -2):
                    pre(nc.vector.tensor_tensor(p, p, s2, ALU.mult))
                    pre(nc.vector.tensor_scalar(p, p, 1 / n, None, ALU.add))
                pre(nc.vector.tensor_tensor(p, p, s, ALU.mult))
                pre(nc.vector.tensor_scalar(p, p, 2.0, None, ALU.mult))
                pre(nc.vector.tensor_scalar(pos, cols_[:, 6:8], 0.0, None, ALU.max))
                pre(nc.vector.tensor_tensor(p, p, pos, ALU.add))
                nc.vector.tensor_scalar(coef[:], p, -8.0, None, ALU.mult).then_inc(coef_ready, 1)
                pre(nc.vector.memset(padded[:, :, 0:K - 1], 0.0))
                before = pre.n
                with dve.Fori(0, B) as c:
                    step = Steps(dve, dve_step, c * DVE_STEPS + before)
                    for k in range(C):
                        dve.wait_ge(z_ready, 4 * c + 2 + k + 1)
                        last = nc.vector.tensor_copy(padded[:, k, K - 1:], bank[2 + k])
                    step(last)
                    for t in range(K):
                        for k in range(C):
                            seen = padded[:, k, t:t + T]
                            if t == 0:
                                last = nc.vector.tensor_scalar(xc[:, k, :], seen, taps[:, k, 0:1], cols_[:, k:k + 1], ALU.mult, ALU.add)
                            else:
                                last = nc.vector.scalar_tensor_tensor(xc[:, k, :], seen, taps[:, k, t:t + 1], xc[:, k, :], ALU.mult, ALU.add)
                        if t < K - 1:
                            step(last)
                    last.then_inc(conv_ready, 1)
                    dve.wait_ge(sq_ready, 2 * c + 2)
                    nc.vector.tensor_scalar(beta[:], beta[:], -1.0, 1.0, ALU.mult, ALU.add).then_inc(rest_ready, 1)
                    dve.wait_ge(sig_ready, 4 * c + 4)
                    step(nc.vector.tensor_tensor(inp[:], inp[:], xc[:], ALU.mult))
                    dve.wait_ge(beta_ready, c + 1)
                    step(nc.vector.tensor_tensor(inp[:], inp[:], beta[:], ALU.mult))
                    dve.wait_ge(gate_ready, 2 * c + 2)
                    for k in range(C):
                        last = nc.vector.tensor_tensor_scan(h[:, k, :], alpha[:, k, :], inp[:, k, :], 0.0, ALU.mult, ALU.add)
                    assert step.n == DVE_STEPS, step.n
                    last.then_inc(scan_ready, 1)
                    dve.wait_ge(scan_ready, c + 1)
                    nc.vector.tensor_tensor(h[:], h[:], gate[:], ALU.mult).then_inc(h_ready, 1)
                    dve.wait_ge(out_ready, c + 1)
                    nc.vector.tensor_tensor(x2[:, cols(c)], bank[0], core.x[:, cols(c)], ALU.add).then_inc(chunk_done, 1)


def gated_mlp(core, xn, x2):
    nc, d = core.nc, core.dram
    C = 2
    with Stage(core, "gm") as st:
        w_grow = st.sb("w_grow", [P, 4 * P])
        w_shrink = st.sb("w_shrink", [P, C, P])
        gate = st.sb("gate", [P, C, T])
        both = st.sb("both", [P, T])
        loaded, z_ready, gate_ready, prod_ready, out_ready, both_ready, chunk_done = (st.sem(n) for n in (
            "loaded", "z_ready", "gate_ready", "prod_ready", "out_ready", "both_ready", "chunk_done"))
        bank = [core.psum[:, k, :] for k in range(8)]
        with nc.Block() as block:
            @block.sync
            def _(sp):
                sp.dma_start(w_grow[:], d["l3_wgrow"]).then_inc(loaded, 16)
                sp.dma_start(w_shrink[:], d["l3_wshrink"]).then_inc(loaded, 16)

            @block.gpsimd
            def _(pool):
                with pool.Fori(0, B) as c:
                    pool.wait_ge(chunk_done, c + 1)
                    nc.gpsimd.tensor_tensor(both[:], core.x[:, cols(c)], x2[:, cols(c)], ALU.add).then_inc(both_ready, 1)

            @block.tensor
            def _(pe):
                pe.wait_ge(loaded, 32)
                with pe.Fori(0, B) as c:
                    pe.wait_ge(chunk_done, c + 1)
                    for k in range(4):
                        nc.tensor.matmul(bank[k], w_grow[:, k * P:(k + 1) * P], xn[:, cols(c)], start=True, stop=True).then_inc(z_ready, 1)
                    for k in range(C):
                        pe.wait_ge(prod_ready, 2 * c + k + 1)
                        last = nc.tensor.matmul(bank[4], w_shrink[:, k, :], gate[:, k, :], start=k == 0, stop=k == C - 1)
                    last.then_inc(out_ready, 1)

            @block.scalar
            def _(act):
                with act.Fori(0, B) as c:
                    for k in range(C):
                        act.wait_ge(z_ready, 4 * c + k + 1)
                        nc.scalar.activation(gate[:, k, :], bank[k], ACT.Gelu).then_inc(gate_ready, 1)

            @block.vector
            def _(dve):
                dve.sem_inc(chunk_done, 1)
                with dve.Fori(0, B) as c:
                    for k in range(C):
                        dve.wait_ge(gate_ready, 2 * c + k + 1)
                        dve.wait_ge(z_ready, 4 * c + 2 + k + 1)
                        nc.vector.tensor_tensor(gate[:, k, :], gate[:, k, :], bank[2 + k], ALU.mult).then_inc(prod_ready, 1)
                    dve.wait_ge(both_ready, c + 1)
                    dve.wait_ge(out_ready, c + 1)
                    nc.vector.tensor_tensor(core.sum[:, cols(c)], bank[4], both[:], ALU.add).then_inc(chunk_done, 1)


def post_norm(core, name):
    norm(core, name, core.sum, core.x, True, 0)
    recycle(core)


def build_program(nc, dram):
    with ExitStack() as ctx:
        core = Core(nc, ctx, dram)
        load_start(core)
        window_attention(core)
        post_norm(core, "n0a")
        ffn0(core)
        post_norm(core, "n0f")
        attn1(core)
        post_norm(core, "n1a")
        ffn1(core)
        post_norm(core, "n1f")
        attn2(core)
        post_norm(core, "n2a")
        ffn2(core)
        post_norm(core, "n2f")
        hawk(core)
        post_norm(core, "n3a")
        ffn3(core)
        post_norm(core, "n3f")
        store_end(core)


def arrays(i):
    f = np.float32
    d = {}
    c = np.ascontiguousarray
    eye = np.eye(128, dtype=f)
    idx = np.arange(128)
    d["c_ident"] = eye
    d["c_mean_w"] = np.full((128, 128), 1 / 128, f)
    d["c_center_w"] = (eye - f(1 / 128)).astype(f)
    d["c_eps"] = np.tile(np.array([1e-5, 1e-6, 0, 0], f), (128, 1))
    d["c_mask"] = np.where(idx[None, :] > idx[:, None], f(-1e30), f(0)).astype(f)
    d["c_headmask"] = ((idx[:, None] % 32) // 8 == np.arange(4)[None, :]).astype(f)
    d["c_wmask"] = np.where(np.arange(32)[None, :] > (idx[:, None] % 32), f(-1e30), f(0)).astype(f)
    d["l0_wqkv"] = i["L0_attn_w_qkv"]
    d["l0_wproj"] = i["L0_attn_w_proj"]
    d["l0_lnw"] = i["L0_attn_ln_w"].reshape(128, 1)
    d["c_sel"] = (np.arange(96)[:, None] % 32 == np.arange(32)[None, :]).astype(f)
    pair = (np.arange(96)[:, None, None] % 32 == 2 * np.arange(9)[:, None] + idx[None, :] // 64)
    d["c_selpair"] = pair.astype(f).reshape(96, 9 * 128)
    ij = np.arange(16)
    tri = np.stack([ij % 4 < ij // 4, ij % 4 > ij // 4]).astype(f)
    d["c_tri"] = np.broadcast_to(tri, (128, 2, 16))

    def pairs(w, shared):
        return np.concatenate([w.reshape(8, 128, 128).transpose(0, 2, 1), shared.T[None]])
    down = np.concatenate([i["L0_ffn_down_w"].transpose(0, 2, 1).reshape(8, 128, 128), i["L0_ffn_sh_down_w"].T[None]])
    d["l0_experts"] = np.concatenate([pairs(i["L0_ffn_gate_w"], i["L0_ffn_sh_gate_w"]),
                                      pairs(i["L0_ffn_up_w"], i["L0_ffn_sh_up_w"]), down], axis=2)
    d["l0_router"] = i["L0_ffn_router_weight"].T.reshape(128, 1, 16)
    d["l0_ebias"] = i["L0_ffn_e_bias"]

    def two_layers(w1, w2):
        e, dim, hid = w1.shape
        w2 = w2.reshape(e, hid // 128, 128, dim).transpose(0, 2, 1, 3).reshape(e, 128, hid)
        return np.concatenate([w1, w2], axis=2)
    d["l1_experts"] = two_layers(i["L1_ffn_c_fc"], i["L1_ffn_c_proj"])
    d["l1_router"] = i["L1_ffn_w_g"].reshape(128, 1, 8)
    d["l2_experts"] = np.concatenate([np.concatenate([
        two_layers(i["L2_ffn_re_w1"], i["L2_ffn_re_w2"]), two_layers(i["L2_ffn_sh_w1"][None], i["L2_ffn_sh_w2"][None])]),
        np.concatenate([i["L2_ffn_re_b1"], i["L2_ffn_sh_b1"][None]])[:, :, None]], axis=2)
    d["l2_b2"] = np.concatenate([i["L2_ffn_re_b2"], i["L2_ffn_sh_b2"][None]])
    d["l2_router"] = i["L2_ffn_router_w"].reshape(128, 1, 31)
    d["l2_rbias"] = i["L2_ffn_router_b"]
    d["l3_experts"] = np.concatenate([np.concatenate([
        two_layers(i["L3_ffn_We1"], i["L3_ffn_We2"]), two_layers(i["L3_ffn_Ws1"][None], i["L3_ffn_Ws2"][None])]),
        np.concatenate([i["L3_ffn_be1"], i["L3_ffn_bs1"][None]]).reshape(9, 2, 128).transpose(0, 2, 1)], axis=2)
    d["l3_b2"] = np.concatenate([i["L3_ffn_be2"], i["L3_ffn_bs2"][None]])
    d["l3_gw1"] = i["L3_ffn_gw1"]
    d["l3_gb1"] = i["L3_ffn_gb1"].reshape(2, 128).T
    d["l3_router"] = i["L3_ffn_gw2"].reshape(2, 128, 8).transpose(1, 0, 2)
    d["l3_rbias"] = i["L3_ffn_gb2"]

    wq, wk, wv = (i["L2_attn_w_a" + n].transpose(1, 0, 2) for n in "qkv")
    d["l2_heads"] = np.concatenate([wq, wk, wv, i["L2_attn_w_ao"]], axis=2)
    freqs = np.power(f(10000.0), -np.arange(64, dtype=f) / f(64)).astype(f)
    angles = (np.arange(512, dtype=f)[None, :] * freqs[:, None]).astype(f)
    cos, sin = np.cos(angles).astype(f), np.sin(angles).astype(f)
    cos, sin = np.concatenate([cos, cos]), np.concatenate([-sin, sin])
    d["c_rope2"] = np.stack([cos / f(128), sin / f(128), cos, sin], axis=1)
    signs = np.array([[a, b, e] for a in (-1, 1) for b in (-1, 1) for e in (-1, 1)], f)
    dirs = signs / np.linalg.norm(signs, axis=1, keepdims=True)
    spread = np.zeros((24, 256), f)
    for h in range(8):
        for at in range(32 * h, 32 * h + 24, 4):
            spread[3 * h:3 * h + 3, at:at + 3] = np.eye(3)
            spread[3 * h:3 * h + 3, at + 3] = dirs[h]
    d["c_spread"] = spread
    q_part, k_part = (np.repeat(p + [0, 0], 4)[idx % 32] for p in ([0, 0, 1, 1, 0, 2], [0, 1, 0, 1, 2, 0]))
    d["c_parts"] = np.stack([-1.0 * (q_part >= 1), -1.0 * (q_part == 2), -1.0 * (k_part >= 1), -1.0 * (k_part == 2),
                             (idx % 32 >= 24) & (idx % 32 < 27)], axis=1).astype(f)
    d["c_sumspread"] = ((idx[:, None] % 32 == 16) & (idx[:, None] // 32 == idx[None, :] // 32)).astype(f)
    d["l1_wq"], d["l1_wk"] = i["L1_attn_Wq"], i["L1_attn_Wk"]
    d["l1_scale"] = i["L1_attn_scale"].reshape(1)
    d["l1_wv"] = i["L1_attn_Wv"].T
    w_out = np.zeros((2, 4, 32, 128), f)
    w_out[:, :, :16] = i["L1_attn_Wo"].T.reshape(2, 4, 16, 128)
    d["l1_wout"] = w_out.reshape(2, 128, 128).transpose(1, 0, 2)

    def even_odd(w):
        w = w.reshape(w.shape[:-1] + (16, 32, 2)).swapaxes(-1, -2)
        return w.reshape(w.shape[:-3] + (8, 128))
    q_b, k_b = (even_odd(i[f"L2_ffn_{n}_b"])[:, :, None] for n in "qk")
    q_w, k_w = (even_odd(i[f"L2_ffn_{n}_w"]).transpose(1, 0, 2) for n in "qk")
    v_w = i["L2_ffn_v_w"].reshape(128, 8, 128).transpose(1, 0, 2)
    d["l2f_heads"] = np.concatenate([q_w, q_b, k_w, k_b, v_w, i["L2_ffn_o_w"].reshape(8, 128, 128)], axis=2)
    d["l2_vb"] = i["L2_ffn_v_b"]
    d["l2_ob"] = i["L2_ffn_o_b"].reshape(128, 1)
    d["l2_gammas"] = np.stack([i["L2_ffn_gamma1"], i["L2_ffn_gamma2"]], axis=1)
    d["l2_theta"] = np.tile(i["L2_ffn_theta"], 4).reshape(128, 1)
    d["c_pos"] = np.arange(512, dtype=f)
    d["c_ropesign"] = np.where(idx % 64 < 32, f(-1), f(1)).astype(f).reshape(128, 1)

    d["l3_gammas"] = np.stack([i["L3_attn_gamma1"], i["L3_attn_gamma2"]], axis=1)
    d["l3_win"] = i["L3_attn_W_in"].T
    d["l3_wgates"] = i["L3_attn_W_gates"].T.reshape(2, 128, 512).transpose(1, 0, 2)
    d["l3_wout"] = i["L3_attn_W_out"].T.reshape(2, 128, 128).transpose(1, 0, 2)
    d["l3_taps"] = i["L3_attn_conv_w"].reshape(2, 128, 4).transpose(1, 0, 2)
    d["l3_cols"] = np.concatenate([i["L3_attn_conv_b"].reshape(2, 128), i["L3_attn_b_gates"].reshape(4, 128),
                                   i["L3_attn_forget_base"].reshape(2, 128)]).T
    d["l3_wgrow"] = i["L3_attn_W_grow"].T
    d["l3_wshrink"] = i["L3_attn_W_shrink"].T.reshape(2, 128, 128).transpose(1, 0, 2)
    return {k: c(v) for k, v in d.items()}


def kernel(**inputs):
    import concourse.bacc as bacc
    from concourse.bass_utils import run_bass_kernel_spmd

    inputs = {name: np.asarray(a) for name, a in inputs.items()}
    laid = arrays(inputs)
    laid["x"] = np.ascontiguousarray(inputs["L0_attn_x"].reshape(N, P))
    nc = bacc.Bacc("TRN2", target_bir_lowering=False, num_devices=1)
    dram = {name: nc.dram_tensor(f"in_{name}", a.shape, mybir.dt.from_np(a.dtype), kind="ExternalInput").ap() for name, a in laid.items()}
    dram["out"] = nc.dram_tensor("out_tokens", (N, P), F32, kind="ExternalOutput").ap()
    build_program(nc, dram)
    result = run_bass_kernel_spmd(nc, [{f"in_{name}": a for name, a in laid.items()}], core_ids=[0])
    return result.results[0]["out_tokens"].reshape(B, T, P)
```

```python
from contextlib import ExitStack

import numpy as np
import concourse.bass as bass
from concourse import mybir

F32 = mybir.dt.float32
BF16 = mybir.dt.bfloat16
F32R = mybir.dt.float32r
ACT = mybir.ActivationFunctionType
ALU = mybir.AluOpType
AX = mybir.AxisListType

P = 128
B = 4
T = 512
N = B * T
NT = N // P
QT = T // P
NEG = -1.0e30


def cols(c, n=T):
    return bass.ds(c * n, n)


class Stage:

    def __init__(self, core, name):
        self.core, self.nc, self.name = core, core.nc, name
        self.ctx = ExitStack()
        self.sems = []

    def __enter__(self):
        self.ctx.__enter__()
        return self

    def __exit__(self, *e):
        self.core.spent += self.sems
        return self.ctx.__exit__(*e)

    def sb(self, name, shape, dtype=F32):
        return self.ctx.enter_context(self.nc.sbuf_tensor(f"{self.name}_{name}", shape, dtype))

    def sem(self, name):
        self.sems.append(self.nc.alloc_semaphore(f"{self.name}_{name}"))
        return self.sems[-1]


class Steps:

    def __init__(self, engine, sem, base=0):
        self.engine, self.sem, self.base, self.n = engine, sem, base, 0

    def __call__(self, instruction):
        self.n += 1
        instruction.then_inc(self.sem, 1)
        self.engine.wait_ge(self.sem, self.base + self.n)


class Core:

    def __init__(self, nc, ctx, dram):
        self.nc, self.dram = nc, dram
        self.spent = []

        def sb(name, shape, dtype=F32):
            return ctx.enter_context(nc.sbuf_tensor(name, shape, dtype))

        self.x = sb("x_fm", [P, N])
        self.sum = sb("sum_fm", [P, N])
        self.psum = ctx.enter_context(nc.psum_tensor("psum", [P, 8, T], F32))
        self.ident = sb("ident", [P, P])
        self.mean_w = sb("mean_w", [P, P])
        self.center_w = sb("center_w", [P, P])
        self.eps = sb("eps", [P, 4])
        self.gammas = sb("gammas", [P, 2, 2])
        self.identb = sb("identb", [P, P], BF16)
        self.maskb = sb("maskb", [P, P], BF16)


def recycle(core):
    core.nc.clear_and_free_semaphores(core.spent)
    core.nc.all_engine_barrier()
    core.spent = []


def load_start(core):
    nc, dram = core.nc, core.dram
    with Stage(core, "load") as st:
        xt = st.sb("x_tm", [P, NT, P])
        idf = st.sb("maskf", [P, P])
        x_loaded, consts_loaded, tiles_ready = (st.sem(n) for n in ("x_loaded", "consts_loaded", "tiles_ready"))
        with nc.Block() as block:
            @block.sync
            def _(sp):
                sp.dma_start(xt[:], dram["x"].rearrange("(t p) c -> p t c", p=P)).then_inc(x_loaded, 16)
                for to, name in ((core.ident, "c_ident"), (core.mean_w, "c_mean_w"), (core.center_w, "c_center_w"), (core.eps, "c_eps")):
                    sp.dma_start(to[:], dram[name]).then_inc(consts_loaded, 16)
                sp.dma_start(idf[:], dram["c_mask"]).then_inc(consts_loaded, 16)
                for k, layer in enumerate((2, 3)):
                    sp.dma_start(core.gammas[:, k, :], dram[f"l{layer}_gammas"]).then_inc(consts_loaded, 16)

            @block.tensor
            def _(pe):
                pe.wait_ge(consts_loaded, 7 * 16)
                pe.wait_ge(x_loaded, 16)
                for b in range(B):
                    for q in range(QT):
                        last = nc.tensor.transpose(core.psum[:, b, q * P:(q + 1) * P], xt[:, b * QT + q, :], core.ident[:])
                    last.then_inc(tiles_ready, 1)

            @block.vector
            def _(dve):
                dve.wait_ge(consts_loaded, 7 * 16)
                nc.vector.tensor_copy(core.identb[:], core.ident[:])
                nc.vector.tensor_copy(core.maskb[:], idf[:])
                for b in range(B):
                    dve.wait_ge(tiles_ready, b + 1)
                    nc.vector.tensor_copy(core.x[:, cols(b)], core.psum[:, b, :])


def norm(core, name, src, dst, center, eps_col, gamma=None):
    nc = core.nc
    with Stage(core, name) as st:
        sq = st.sb("sq", [P, 2, T])
        lnv = st.sb("lnv", [P, 2, T])
        rs = st.sb("rs", [P, 2, T])
        centered, squared, var_ready, ln_ready, rs_ready, out_ready = (
            st.sem(n) for n in ("centered", "squared", "var_ready", "ln_ready", "rs_ready", "out_ready"))
        xc = [core.psum[:, b, :] for b in range(4)]
        var = [core.psum[:, 4 + b, :] for b in range(4)]
        with nc.Block() as block:
            @block.tensor
            def _(pe):
                if center:
                    for b in range(B):
                        nc.tensor.matmul(xc[b], core.center_w[:], src[:, cols(b)], start=True, stop=True).then_inc(centered, 1)
                for b in range(B):
                    pe.wait_ge(squared, b + 1)
                    nc.tensor.matmul(var[b], core.mean_w[:], sq[:, b % 2, :], start=True, stop=True).then_inc(var_ready, 1)

            @block.scalar
            def _(act):
                def square(b):
                    if center:
                        act.wait_ge(centered, b + 1)
                    if b >= 2:
                        act.wait_ge(var_ready, b - 1)
                    nc.scalar.activation(sq[:, b % 2, :], xc[b] if center else src[:, cols(b)], ACT.Square).then_inc(squared, 1)

                nc.scalar.preload_act_table_set("natural_log_exp_and_others")
                square(0)
                for b in range(B):
                    if b + 1 < B:
                        square(b + 1)
                    act.wait_ge(var_ready, b + 1)
                    nc.scalar.activation(lnv[:, b % 2, :], var[b], ACT.Ln, bias=core.eps[:, eps_col:eps_col + 1]).then_inc(ln_ready, 1)
                    act.wait_ge(ln_ready, b + 1)
                    if b >= 2:
                        act.wait_ge(out_ready, b - 1)
                    nc.scalar.activation(rs[:, b % 2, :], lnv[:, b % 2, :], ACT.Exp, scale=-0.5).then_inc(rs_ready, 1)

            @block.vector
            def _(dve):
                for b in range(B):
                    dve.wait_ge(rs_ready, b + 1)
                    x_in = xc[b] if center else src[:, cols(b)]
                    if gamma is None:
                        nc.vector.tensor_tensor(dst[:, cols(b)], x_in, rs[:, b % 2, :], ALU.mult).then_inc(out_ready, 1)
                    else:
                        nc.vector.scalar_tensor_tensor(dst[:, cols(b)], x_in, gamma, rs[:, b % 2, :], ALU.mult, ALU.mult).then_inc(out_ready, 1)


def store_end(core):
    nc, dram = core.nc, core.dram
    with Stage(core, "store") as st:
        xt = st.sb("x_tm", [P, NT, P])
        tiles_ready, tiles_out, stored = (st.sem(n) for n in ("tiles_ready", "tiles_out", "stored"))
        out = dram["out"].rearrange("(t p) c -> p t c", p=P)
        with nc.Block() as block:
            @block.tensor
            def _(pe):
                for b in range(B):
                    for q in range(QT):
                        last = nc.tensor.transpose(core.psum[:, b, q * P:(q + 1) * P], core.x[:, (b * QT + q) * P:(b * QT + q + 1) * P], core.ident[:])
                    last.then_inc(tiles_ready, 1)

            @block.vector
            def _(dve):
                for b in range(B):
                    dve.wait_ge(tiles_ready, b + 1)
                    nc.vector.tensor_copy(xt[:, b * QT:(b + 1) * QT, :].rearrange("p t c -> p (t c)"), core.psum[:, b, :]).then_inc(tiles_out, 1)

            @block.sync
            def _(sp):
                for b in range(B):
                    sp.wait_ge(tiles_out, b + 1)
                    sp.dma_start(out[:, b * QT:(b + 1) * QT, :], xt[:, b * QT:(b + 1) * QT, :]).then_inc(stored, 16)
                sp.wait_ge(stored, 16 * B)


def window_attention(core):
    nc, dram = core.nc, core.dram
    G, HG, W = 4, 4, 4
    L = 32
    with Stage(core, "l0a") as st:
        wqkv = st.sb("wqkv", [P, 3 * P])
        wproj = st.sb("wproj", [P, P])
        vecs = st.sb("vecs", [P, 8])
        wmask = st.sb("wmask", [P, L])
        wmaskb = st.sb("wmaskb", [P, T], BF16)
        xs = st.sb("xs", [P, T])
        q_raw, k_raw, qn, kn = (st.sb(n, [P, T]) for n in ("q_raw", "k_raw", "qn", "kn"))
        sq = st.sb("sq", [P, 2, T])
        lnm = st.sb("lnm", [P, 2, T])
        rs = st.sb("rs", [P, 2, T])
        v_next = st.sb("v_next", [P, QT * P])
        v_tm = st.sb("v_tm", [P, QT, P])
        kx = st.sb("kx", [P, QT, W, HG, L])
        s_sb = st.sb("s_sb", [P, G, QT * HG * L])
        p_sb = st.sb("p_sb", [P, G, QT * HG * L])
        p_t = st.sb("p_t", [P, G, QT * HG * L])
        smax = st.sb("smax", [P, G, QT * HG])
        ssum = st.sb("ssum", [P, G, QT * HG])
        y_fm = st.sb("y_fm", [P, W, QT, L])
        (loaded, mask_ready, x_ready, qkv_ready, raw_ready, squared, v_next_ready, ms_ready, ln_ready, rs_ready, qk_ready,
         s_ready, shifted, exp_ready, inv_ready, p_ready, pt_ready, v_ready, av_ready, y_ready, out_ready, sum_done, front_step,
         back_step, passed, passed_pe) = (st.sem(n) for n in (
             "loaded", "mask_ready", "x_ready", "qkv_ready", "raw_ready", "squared", "v_next_ready", "ms_ready", "ln_ready",
             "rs_ready", "qk_ready", "s_ready", "shifted", "exp_ready", "inv_ready", "p_ready", "pt_ready", "v_ready", "av_ready",
             "y_ready", "out_ready", "sum_done", "front_step", "back_step", "passed", "passed_pe"))
        ps_s = [core.psum[:, g, :] for g in range(G)]
        ps_o = [core.psum[:, 4 + w, :] for w in range(W)]
        BACK_STEPS = 2 * G + HG - 1

        def per_chunk(engine, body):
            body(0, True, False)
            with engine.Fori(1, B - 1) as c:
                body(c, False, False)
            body(B - 1, False, True)

        with nc.Block() as block:
            @block.sync
            def _(sp):
                sp.dma_start(wqkv[:], dram["l0_wqkv"]).then_inc(loaded, 16)
                sp.dma_start(wproj[:], dram["l0_wproj"]).then_inc(loaded, 16)
                sp.dma_start(vecs[:, 0:1], dram["l0_lnw"]).then_inc(loaded, 16)
                sp.dma_start(vecs[:, 1:5], dram["c_headmask"]).then_inc(loaded, 16)
                sp.dma_start(wmask[:], dram["c_wmask"]).then_inc(loaded, 16)

            @block.gpsimd
            def _(pool):
                def chunk(c, first, last):
                    if not last:
                        pool.wait_ge(qkv_ready, 3 * c + 3)
                        pool.sem_inc(passed, 1)
                        nc.gpsimd.tensor_copy(xs[:], core.x[:, cols(c + 1)]).then_inc(x_ready, 1)
                    pool.wait_ge(v_next_ready, c + 1)
                    if not first:
                        pool.wait_ge(av_ready, c)
                    pool.sem_inc(passed, 1)
                    nc.gpsimd.tensor_copy(v_tm[:].rearrange("p t d -> p (t d)"), v_next[:]).then_inc(v_ready, 1)
                    for g in range(G):
                        pb = p_sb[:, g, :].rearrange("p (b k) -> p b k", k=L)
                        pool.wait_ge(inv_ready, G * c + g + 1)
                        nc.gpsimd.tensor_tensor(pb, pb, ssum[:, g, :].unsqueeze(2).to_broadcast([P, QT * HG, L]), ALU.mult).then_inc(p_ready, 1)

                nc.gpsimd.tensor_copy(xs[:], core.x[:, cols(0)]).then_inc(x_ready, 1)
                per_chunk(pool, chunk)

            @block.tensor
            def _(pe):
                def front(c):
                    pe.wait_ge(x_ready, c + 1)
                    for j in range(2):
                        pe.wait_ge(shifted, G * c + j + 1)
                        nc.tensor.matmul(ps_s[j], wqkv[:, j * P:(j + 1) * P], xs[:], start=True, stop=True).then_inc(qkv_ready, 1)
                    pe.wait_ge(shifted, G * c + 3)
                    for t in range(QT):
                        last = nc.tensor.matmul(ps_s[2][:, t * P:(t + 1) * P], xs[:, t * P:(t + 1) * P], wqkv[:, 2 * P:], start=True, stop=True)
                    last.then_inc(qkv_ready, 1)
                    for j in range(2):
                        pe.wait_ge(squared, 2 * c + j + 1)
                        nc.tensor.matmul(ps_o[1 + j], core.mean_w[:], sq[:, j, :], start=True, stop=True).then_inc(ms_ready, 1)

                def scores(c):
                    pe.wait_ge(v_next_ready, c + 1)
                    pe.wait_ge(shifted, G * c + 4)
                    for g in range(G):
                        nc.tensor.matmul(ps_s[g], core.identb[:], wmaskb[:], start=True, stop=False, skip_group_check=True)
                    pe.wait_ge(qk_ready, c + 1)
                    pe.sem_inc(passed_pe, 1)
                    for t in range(QT):
                        for w in range(W):
                            for g in range(G):
                                rows, q_at = slice(32 * g, 32 * g + 32), t * P + w * L
                                last = nc.tensor.matmul(ps_s[g][32 * w:32 * w + 32, t * P:(t + 1) * P], qn[rows, q_at:q_at + L],
                                                        kx[rows, t, w, :, :].rearrange("p h k -> p (h k)"), start=False, stop=True,
                                                        skip_group_check=True)
                    last.then_inc(s_ready, 1)

                def out(c):
                    pe.wait_ge(y_ready, c + 1)
                    nc.tensor.matmul(ps_o[0], wproj[:], y_fm[:].rearrange("p w t q -> p t w q"), start=True, stop=True).then_inc(out_ready, 1)

                def values(c, first, last):
                    pe.wait_ge(v_ready, c + 1)
                    if not last:
                        pe.wait_ge(ln_ready, 2 * c + 4)
                    if not first:
                        pe.wait_ge(sum_done, c)
                    for g in range(G):
                        pe.wait_ge(pt_ready, G * c + g + 1)
                        pe.sem_inc(passed_pe, 1)
                        for t in range(QT):
                            for w in range(W):
                                rows = slice(32 * w, 32 * w + 32)
                                mm = nc.tensor.matmul(ps_o[w][32 * g:32 * g + 32, t * P:(t + 1) * P], v_tm[rows, t, 32 * g:32 * g + 32],
                                                      p_t[rows, g, t * P:(t + 1) * P], start=True, stop=True)
                    mm.then_inc(av_ready, 1)

                def chunk(c, first, last):
                    scores(c)
                    if not first:
                        out(c - 1)
                    if not last:
                        front(c + 1)
                    values(c, first, last)

                pe.wait_ge(loaded, 5 * 16)
                pe.wait_ge(mask_ready, 1)
                front(0)
                per_chunk(pe, chunk)
                out(B - 1)

            @block.scalar
            def _(act):
                def unnormed(c, j):
                    act.wait_ge(qkv_ready, 3 * c + j + 1)
                    nc.scalar.activation((q_raw, k_raw)[j][:], ps_s[j], ACT.Copy).then_inc(raw_ready, 1)
                    nc.scalar.activation(sq[:, j, :], ps_s[j], ACT.Square).then_inc(squared, 1)

                def copy_v(c):
                    act.wait_ge(qkv_ready, 3 * c + 3)
                    nc.scalar.activation(v_next[:], ps_s[2], ACT.Copy).then_inc(v_next_ready, 1)

                def inverse_rms(c):
                    for j in range(2):
                        act.wait_ge(ms_ready, 2 * c + j + 1)
                        nc.scalar.activation(lnm[:, j, :], ps_o[1 + j], ACT.Ln, bias=core.eps[:, 1:2]).then_inc(ln_ready, 1)
                        act.wait_ge(ln_ready, 2 * c + j + 1)
                        nc.scalar.activation(rs[:, j, :], lnm[:, j, :], ACT.Exp, scale=-0.5).then_inc(rs_ready, 1)

                def exps(c, first, groups):
                    for g in groups:
                        act.wait_ge(shifted, G * c + g + 1 + G)
                        if not first:
                            act.wait_ge(pt_ready, G * (c - 1) + g + 1)
                        nc.scalar.activation(p_sb[:, g, :], s_sb[:, g, :], ACT.Exp, scale=8 ** -0.5).then_inc(exp_ready, 1)

                def chunk(c, first, last):
                    exps(c, first, (0, 1))
                    if not last:
                        act.wait_ge(qk_ready, c + 1)
                        unnormed(c + 1, 0)
                    exps(c, first, (2, 3))
                    if not last:
                        unnormed(c + 1, 1)
                        act.wait_ge(v_ready, c + 1)
                        copy_v(c + 1)
                        inverse_rms(c + 1)

                nc.scalar.preload_act_table_set("natural_log_exp_and_others")
                act.wait_ge(loaded, 5 * 16)
                unnormed(0, 0)
                unnormed(0, 1)
                copy_v(0)
                inverse_rms(0)
                per_chunk(act, chunk)

            @block.vector
            def _(dve):
                blocks = [s_sb[:, g, :].rearrange("p (b k) -> p b k", k=L) for g in range(G)]

                def front(c):
                    step = Steps(dve, front_step, c)
                    dve.wait_ge(rs_ready, 2 * c + 2)
                    dve.wait_ge(raw_ready, 2 * c + 2)
                    nc.vector.scalar_tensor_tensor(qn[:], q_raw[:], vecs[:, 0:1], rs[:, 0, :], ALU.mult, ALU.mult)
                    step(nc.vector.scalar_tensor_tensor(kn[:], k_raw[:], vecs[:, 0:1], rs[:, 1, :], ALU.mult, ALU.mult))
                    for h in range(HG):
                        last = nc.vector.tensor_scalar(kx[:, :, :, h, :], kn[:].rearrange("p (t w k) -> p t w k", w=W, k=L),
                                                       vecs[:, 1 + h:2 + h], None, ALU.mult)
                    last.then_inc(qk_ready, 1)

                def transpose(c, g):
                    dve.wait_ge(p_ready, G * c + g + 1)
                    nc.vector.transpose(p_t[:, g, :], p_sb[:, g, :]).then_inc(pt_ready, 1)

                def add_out(c):
                    dve.wait_ge(out_ready, c + 1)
                    nc.vector.tensor_tensor(core.sum[:, cols(c)], ps_o[0], core.x[:, cols(c)], ALU.add).then_inc(sum_done, 1)

                def chunk(c, first, last):
                    step = Steps(dve, back_step, c * BACK_STEPS)
                    dve.wait_ge(s_ready, c + 1)
                    for g in range(G):
                        in_psum = ps_s[g].rearrange("p (b k) -> p b k", k=L)
                        step(nc.vector.tensor_reduce(smax[:, g, :], in_psum, AX.X, ALU.max))
                        nc.vector.tensor_tensor(blocks[g], in_psum, smax[:, g, :].unsqueeze(2).to_broadcast([P, QT * HG, L]),
                                                ALU.subtract).then_inc(shifted, 1)
                    if not first:
                        add_out(c - 1)
                    for g in range(G):
                        dve.wait_ge(exp_ready, G * c + g + 1)
                        step(nc.vector.tensor_reduce(ssum[:, g, :], p_sb[:, g, :].rearrange("p (b k) -> p b k", k=L), AX.X, ALU.add))
                        nc.vector.reciprocal(ssum[:, g, :], ssum[:, g, :]).then_inc(inv_ready, 1)
                        if g >= 2:
                            transpose(c, g - 2)
                    transpose(c, 2)
                    transpose(c, 3)
                    if not last:
                        front(c + 1)
                    dve.wait_ge(av_ready, c + 1)
                    o = core.psum[:, 4:8, :].rearrange("p w (t h q) -> p (w t) h q", h=HG, q=L)
                    to = y_fm[:].rearrange("p w t q -> p (w t) q")
                    for h in range(HG):
                        if h == 0:
                            step(nc.vector.tensor_scalar(to, o[:, :, h, :], vecs[:, 1:2], None, ALU.mult))
                        else:
                            mix = nc.vector.scalar_tensor_tensor(to, o[:, :, h, :], vecs[:, 1 + h:2 + h], to, ALU.mult, ALU.add)
                            if h < HG - 1:
                                step(mix)
                            else:
                                mix.then_inc(y_ready, 1)
                    assert step.n == BACK_STEPS, step.n

                dve.wait_ge(loaded, 5 * 16)
                nc.vector.tensor_copy(wmaskb[:].rearrange("p (b k) -> p b k", k=L), wmask[:].unsqueeze(1).to_broadcast([P, QT * HG, L])).then_inc(mask_ready, 1)
                dve.sem_inc(shifted, G)
                front(0)
                per_chunk(dve, chunk)
                add_out(B - 1)


GR = 96
SENT = -3.0e38
PLACES = 4
HIT = 3.0e38


def experts(core, name, *, act_func, x, resid, gates_t, gates3, n_slots, unroll, tiles, w_dram, with_b1=False,
            b2=None, b2_rows=0, glu=False):
    nc = core.nc
    up = 2 if glu else 1
    w1_cols = up * tiles * P
    biases = tiles if with_b1 else 0
    w_cols = w1_cols + tiles * P + biases
    iters = n_slots // unroll
    assert iters * unroll == n_slots
    items = [(s, b, t) for s in range(unroll) for b in range(B) for t in range(tiles)]
    n_items = len(items)
    assert n_items % PLACES == 0
    lag = 2 if glu else 3
    gated_credit = tiles + PLACES
    out_credit = n_items
    with Stage(core, name) as st:
        w = st.sb("w", [P, unroll, w_cols])
        w_hi, w_lo = (st.sb(f"w_{n}", [P, unroll, w_cols - biases], F32R) for n in ("hi", "lo"))
        x_hi, x_lo = (st.sb(f"x_{n}", [P, N], F32R) for n in ("hi", "lo"))
        act_sb = st.sb("act", [P, PLACES, T])
        glu_sb = st.sb("glu", [P, 2, T]) if glu else None
        gated = st.sb("gated", [P, PLACES, T])
        gated_hi, gated_lo = (st.sb(f"gated_{n}", [P, PLACES, T], F32R) for n in ("hi", "lo"))
        sel_cols = n_slots * P if glu else 32
        selb = st.sb("selb", [GR, sel_cols], BF16)
        self32 = st.sb("self32", [GR, sel_cols])
        w_loaded = [st.sem(f"w{s}_loaded") for s in range(unroll)]
        w_split = [st.sem(f"w{s}_split") for s in range(unroll)]
        w_hi_ready = [st.sem(f"w{s}_hi_ready") for s in range(unroll)]
        (consts_loaded, sel_ready, x_hi_ready, x_split, hid_ready, gate_ready, act_ready, glu_ready, gated_ready, hi_ready,
         lo_ready, out_done) = (st.sem(n) for n in (
             "consts_loaded", "sel_ready", "x_hi_ready", "x_split", "hid_ready", "gate_ready", "act_ready", "glu_ready",
             "gated_ready", "hi_ready", "lo_ready", "out_done"))
        passed = st.sem("passed")
        acc = [core.psum[:, b, :] for b in range(B)]
        hid = [core.psum[:, 4 + k, :] for k in range(2)]
        gate = [core.psum[:, 6 + k, :] for k in range(2)]

        with nc.Block() as block:
            @block.sync
            def _(sp):
                sp.dma_start(self32[:], core.dram["c_selpair" if glu else "c_sel"]).then_inc(consts_loaded, 16)
                with sp.Fori(0, iters) as i:
                    for s in range(unroll):
                        sp.wait_ge(out_done, i * n_items + (s + 1) * B * tiles)
                        sp.dma_start(w[:, s, :], w_dram[bass.ds(i * unroll + s, 1)].rearrange("o p n -> p (o n)")).then_inc(w_loaded[s], 16)

            @block.gpsimd
            def _(pool):
                with pool.Fori(0, iters) as i:
                    for s in range(unroll):
                        whole = w[:, s, 0:w_cols - biases]
                        pool.wait_ge(w_loaded[s], 16 * i + 16)
                        pool.sem_inc(passed, 1)
                        nc.gpsimd.tensor_copy(w_hi[:, s, :], whole).then_inc(w_hi_ready[s], 1)
                        pool.wait_ge(w_hi_ready[s], i + 1)
                        nc.gpsimd.tensor_tensor(w_lo[:, s, :], whole, w_hi[:, s, :].bitcast(F32), ALU.subtract).then_inc(w_split[s], 1)

            @block.tensor
            def _(pe):
                pe.sem_inc(out_done, out_credit)
                for b in range(B):
                    nc.tensor.matmul(acc[b], core.ident[:], resid[:, cols(b)], start=True, stop=b2 is None)
                    if b2 is not None:
                        nc.tensor.matmul(acc[b], b2[0:b2_rows, :], gates_t[0:b2_rows, cols(b)], start=False, stop=True)
                pe.wait_ge(sel_ready, 1)
                pe.wait_ge(x_split, B)

                def product(out, s, at, hi, lo, start):
                    w_h, w_l = w_hi[:, s, at:at + P], w_lo[:, s, at:at + P]
                    nc.tensor.matmul(out, w_h, hi, start=start, stop=False, skip_group_check=True)
                    nc.tensor.matmul(out, w_l, hi, start=False, stop=False, skip_group_check=True)
                    return nc.tensor.matmul(out, w_h, lo, start=False, stop=True, skip_group_check=True)

                def hidden(i, n):
                    s, b, t = items[n]
                    g = i * n_items + n
                    if b == 0 and t == 0:
                        pe.wait_ge(w_split[s], i + 1)
                    if t == 0:
                        pair, e = i * (unroll * B) + s * B + b, i * unroll + s
                        pe.wait_ge(gated_ready, pair * tiles - tiles + gated_credit)
                        sel = (selb[:, bass.ds(e * P, P)] if glu
                               else selb[:, bass.ds(e, 1)].to_broadcast([GR, P]))
                        nc.tensor.matmul(gate[b % 2], sel, gates3[:, cols(b)], start=True, stop=True).then_inc(gate_ready, 1)
                    if glu:
                        pe.wait_ge(glu_ready, g + 1)
                    else:
                        pe.wait_ge(act_ready, g + 1)
                    for k in range(up):
                        product(hid[k if glu else n % 2], s, (k * tiles + t) * P, x_hi[:, cols(b)], x_lo[:, cols(b)],
                                True).then_inc(hid_ready, 1)

                def output(i, n):
                    s, b, t = items[n]
                    pe.wait_ge(lo_ready, i * n_items + n + 1)
                    product(acc[b], s, w1_cols + t * P, gated_hi[:, n % PLACES, :], gated_lo[:, n % PLACES, :],
                            False).then_inc(out_done, 1)

                for n in range(lag):
                    hidden(0, n)
                with pe.Fori(0, iters - 1) as i:
                    for n in range(n_items):
                        ahead = n + lag
                        hidden(i + ahead // n_items, ahead % n_items)
                        output(i, n)
                for n in range(n_items):
                    if n + lag < n_items:
                        hidden(iters - 1, n + lag)
                    output(iters - 1, n)

            @block.scalar
            def _(act):
                act.wait_ge(consts_loaded, 16)
                nc.scalar.activation(selb[:], self32[:], ACT.Copy).then_inc(sel_ready, 1)
                for b in range(B):
                    nc.scalar.activation(x_hi[:, cols(b)], x[:, cols(b)], ACT.Copy).then_inc(x_hi_ready, 1)
                nc.scalar.preload_act_table(act_func)
                act.sem_inc(act_ready, 2)
                with act.Fori(0, iters) as i:
                    def activate(n):
                        s, b, t = items[n]
                        g = i * n_items + n
                        act.wait_ge(hid_ready, g * up + 1)
                        act.wait_ge(gated_ready, g - PLACES + 1 + gated_credit)
                        bias = {"bias": w[:, s, w_cols - tiles + t:w_cols - tiles + t + 1]} if with_b1 else {}
                        nc.scalar.activation(act_sb[:, n % PLACES, :], hid[0] if glu else hid[n % 2], act_func, **bias).then_inc(act_ready, 1)

                    activate(0)
                    for n in range(n_items):
                        if n + 1 < n_items:
                            activate(n + 1)
                        g = i * n_items + n
                        act.wait_ge(gated_ready, g + 1 + gated_credit)
                        act.wait_ge(out_done, g - PLACES + 1 + out_credit)
                        nc.scalar.activation(gated_hi[:, n % PLACES, :], gated[:, n % PLACES, :], ACT.Copy).then_inc(hi_ready, 1)

            @block.vector
            def _(dve):
                for b in range(B):
                    dve.wait_ge(x_hi_ready, b + 1)
                    nc.vector.tensor_tensor(x_lo[:, cols(b)], x[:, cols(b)], x_hi[:, cols(b)].bitcast(F32), ALU.subtract).then_inc(x_split, 1)
                dve.sem_inc(gated_ready, gated_credit)
                if glu:
                    dve.sem_inc(glu_ready, 1)
                with dve.Fori(0, iters) as i:
                    def gate_item(n):
                        s, b, t = items[n]
                        g = i * n_items + n
                        dve.wait_ge(act_ready, g + 3)
                        src = act_sb[:, n % PLACES, :]
                        if glu:
                            dve.wait_ge(hid_ready, g * 2 + 2)
                            nc.vector.tensor_tensor(glu_sb[:, n % 2, :], src, hid[1], ALU.mult).then_inc(glu_ready, 1)
                            dve.wait_ge(glu_ready, g + 2)
                            src = glu_sb[:, n % 2, :]
                        dve.wait_ge(gate_ready, i * (unroll * B) + s * B + b + 1)
                        nc.vector.tensor_tensor(gated[:, n % PLACES, :], src, gate[b % 2], ALU.mult).then_inc(gated_ready, 1)

                    gate_item(0)
                    for n in range(n_items):
                        if n + 1 < n_items:
                            gate_item(n + 1)
                        g = i * n_items + n
                        dve.wait_ge(hi_ready, g + 1)
                        dve.wait_ge(out_done, g - PLACES + 1 + out_credit)
                        nc.vector.tensor_tensor(gated_lo[:, n % PLACES, :], gated[:, n % PLACES, :],
                                                gated_hi[:, n % PLACES, :].bitcast(F32), ALU.subtract).then_inc(lo_ready, 1)
                dve.wait_ge(out_done, iters * n_items + out_credit)
                for b in range(B):
                    nc.vector.tensor_copy(core.sum[:, cols(b)], acc[b])


def router(core, name, kind, *, x, w_dram, n_experts, top, gates_t, gates3, bias_dram=None, hid_dram=None,
           hid_bias_dram=None, tri_dram=None, capacity=None, more_loads=()):
    nc = core.nc
    E, KT = n_experts, 2 if hid_dram is not None else 1
    W = P if kind == "top_capacity" else 32
    with Stage(core, name) as st:
        rw = st.sb("rw", [P, KT, E])
        bias = st.sb("bias", [P, E])
        scores = st.sb("scores", [P, NT, E])
        ranked = st.sb("ranked", [P, NT, E + 8])
        marked = st.sb("marked", [P, NT, E + 8])
        top8 = st.sb("top8", [P, NT, 8])
        mask = st.sb("mask", [P, NT, E])
        g_tm = st.sb("g_tm", [P, NT, W])
        small = st.sb("small", [P, NT, 8])
        rest = st.sb("rest", [32, N])
        part = st.sb("part", [32, N], BF16)
        if kind == "sigmoid_groups":
            tri = st.sb("tri", [P, 2, 16])
            gsum = st.sb("gsum", [P, NT, 4])
            work = st.sb("work", [P, NT, 16])
            work2 = st.sb("work2", [P, NT, 16])
        if hid_dram is not None:
            hw = st.sb("hw", [P, KT * P])
            hb = st.sb("hb", [P, KT])
            hid = st.sb("hid", [P, KT, N])
        if kind == "top_capacity":
            masks_t = st.sb("masks_t", [8, 2, N])
            probs_t = st.sb("probs_t", [8, 2, N])
            count = st.sb("count", [8, 2, N])
            ones = st.sb("ones", [8, N])
        (loaded, hid_psum, hid_ready, logits_ready, scores_ready, shifted, exp_ready, gates_ready, gates_t_psum,
         dve_step) = (st.sem(n) for n in ("loaded", "hid_psum", "hid_ready", "logits_ready", "scores_ready", "shifted",
                                          "exp_ready", "gates_ready", "gates_t_psum", "dve_step"))
        logits = core.psum[:, 0, 0:NT * E].rearrange("p (t e) -> p t e", e=E)
        loads = [(rw[:], w_dram), *more_loads]
        if bias_dram is not None:
            loads.append((bias[:], bias_dram.partition_broadcast(P)))
        if tri_dram is not None:
            loads.append((tri[:], tri_dram))
        if hid_dram is not None:
            loads += [(hw[:], hid_dram), (hb[:], hid_bias_dram)]

        with nc.Block() as block:
            @block.sync
            def _(sp):
                for to, of in loads:
                    sp.dma_start(to, of).then_inc(loaded, 16)

            @block.tensor
            def _(pe):
                pe.wait_ge(loaded, 16 * len(loads))
                if hid_dram is not None:
                    for b in range(B):
                        for k in range(KT):
                            n = b * KT + k
                            if n >= 2:
                                pe.wait_ge(hid_ready, n - 1)
                            nc.tensor.matmul(core.psum[:, 4 + n % 2, :], hw[:, k * P:(k + 1) * P], x[:, cols(b)],
                                             start=True, stop=True).then_inc(hid_psum, 1)
                    pe.wait_ge(hid_ready, B * KT)
                for t in range(NT):
                    for k in range(KT):
                        src = x[:, t * P:(t + 1) * P] if hid_dram is None else hid[:, k, t * P:(t + 1) * P]
                        last = nc.tensor.matmul(logits[:, t, :], src, rw[:, k, :], start=k == 0, stop=k == KT - 1)
                last.then_inc(logits_ready, 1)
                pe.wait_ge(gates_ready, 1)
                for t in range(NT):
                    last = nc.tensor.transpose(core.psum[0:W, t // QT, (t % QT) * P:(t % QT + 1) * P], g_tm[:, t, :], core.ident[:])
                    if t % QT == QT - 1:
                        last.then_inc(gates_t_psum, 1)

            @block.scalar
            def _(act):
                act.wait_ge(loaded, 16 * len(loads))
                if hid_dram is not None:
                    for b in range(B):
                        for k in range(KT):
                            act.wait_ge(hid_psum, b * KT + k + 1)
                            nc.scalar.activation(hid[:, k, cols(b)], core.psum[:, 4 + (b * KT + k) % 2, :], ACT.Gelu,
                                                 bias=hb[:, k:k + 1]).then_inc(hid_ready, 1)
                if kind == "sigmoid_groups":
                    act.wait_ge(logits_ready, 1)
                    nc.scalar.activation(scores[:], logits, ACT.Sigmoid).then_inc(scores_ready, 1)
                else:
                    act.wait_ge(shifted, 1)
                    to, of = (small[:, :, 1:2], small[:, :, 0:1]) if kind == "top_capacity" else (scores[:], scores[:])
                    nc.scalar.activation(to, of, ACT.Exp).then_inc(exp_ready, 1)

            @block.vector
            def _(dve):
                step = Steps(dve, dve_step)

                def wide(ap, n):
                    return ap.to_broadcast([P, NT, n])

                def find_top(k, out):
                    if k < 8:
                        step(nc.vector.memset(top8[:, :, k:8], SENT))
                    for t in range(NT):
                        last = nc.vector.match_replace(marked[:, t, :], top8[:, t, :], ranked[:, t, :], HIT)
                    step(last)
                    step(nc.vector.tensor_scalar(out, marked[:, :, 0:E], HIT, None, ALU.is_equal))

                def rank():
                    for t in range(NT):
                        last = nc.vector.max(top8[:, t, :], ranked[:, t, 0:E])
                    step(last)

                dve.wait_ge(loaded, 16 * len(loads))
                step(nc.vector.memset(ranked[:], SENT))
                step(nc.vector.memset(g_tm[:], 0.0))
                if kind == "sigmoid_groups":
                    dve.wait_ge(scores_ready, 1)
                    step(nc.vector.tensor_tensor(ranked[:, :, 0:E], scores[:], bias[:].unsqueeze(1).to_broadcast([P, NT, E]), ALU.add))
                    four = ranked[:, :, 0:E].rearrange("p t (g k) -> p t g k", k=4)
                    hi1, lo1, hi2, lo2 = (work[:, :, 4 * k:4 * k + 4] for k in range(4))
                    nc.vector.tensor_tensor(hi1, four[:, :, :, 0], four[:, :, :, 1], ALU.max)
                    nc.vector.tensor_tensor(lo1, four[:, :, :, 0], four[:, :, :, 1], ALU.min)
                    nc.vector.tensor_tensor(hi2, four[:, :, :, 2], four[:, :, :, 3], ALU.max)
                    step(nc.vector.tensor_tensor(lo2, four[:, :, :, 2], four[:, :, :, 3], ALU.min))
                    m1, m2, m3 = (work2[:, :, 4 * k:4 * k + 4] for k in range(3))
                    nc.vector.tensor_tensor(m1, hi1, hi2, ALU.max)
                    nc.vector.tensor_tensor(m2, hi1, hi2, ALU.min)
                    step(nc.vector.tensor_tensor(m3, lo1, lo2, ALU.max))
                    step(nc.vector.tensor_tensor(m2, m2, m3, ALU.max))
                    step(nc.vector.tensor_tensor(gsum[:], m1, m2, ALU.add))
                    of_j = gsum[:].unsqueeze(2).to_broadcast([P, NT, 4, 4])
                    of_i = gsum[:].unsqueeze(3).to_broadcast([P, NT, 4, 4])
                    nc.vector.tensor_tensor(work[:].rearrange("p t (i j) -> p t i j", j=4), of_j, of_i, ALU.is_ge)
                    step(nc.vector.tensor_tensor(work2[:].rearrange("p t (i j) -> p t i j", j=4), of_j, of_i, ALU.is_gt))
                    nc.vector.tensor_tensor(work[:], work[:], tri[:, 0:1, :].to_broadcast([P, NT, 16]), ALU.mult)
                    step(nc.vector.tensor_tensor(work2[:], work2[:], tri[:, 1:2, :].to_broadcast([P, NT, 16]), ALU.mult))
                    step(nc.vector.tensor_tensor(work[:], work[:], work2[:], ALU.add))
                    step(nc.vector.tensor_reduce(gsum[:], work[:].rearrange("p t (i j) -> p t i j", j=4), AX.X, ALU.add))
                    step(nc.vector.tensor_scalar(gsum[:], gsum[:], 2.0, None, ALU.is_lt))
                    step(nc.vector.tensor_tensor(four, four, gsum[:].unsqueeze(3).to_broadcast([P, NT, 4, 4]), ALU.mult))
                    step(nc.vector.tensor_scalar(ranked[:, :, 0:E], ranked[:, :, 0:E], 0.0, None, ALU.add))
                    rank()
                    find_top(top, mask[:])
                    step(nc.vector.tensor_tensor(mask[:], mask[:], scores[:], ALU.mult))
                    step(nc.vector.tensor_reduce(small[:, :, 0:1], mask[:], AX.X, ALU.add))
                    step(nc.vector.tensor_scalar(small[:, :, 0:1], small[:, :, 0:1], 1e-20, None, ALU.add))
                    step(nc.vector.reciprocal(small[:, :, 0:1], small[:, :, 0:1]))
                    step(nc.vector.tensor_tensor(mask[:], mask[:], wide(small[:, :, 0:1], E), ALU.mult))
                    nc.vector.tensor_scalar(g_tm[:, :, 0:E], mask[:], 2.5, None, ALU.mult)
                    nc.vector.memset(g_tm[:, :, E:E + 2], 1.0).then_inc(gates_ready, 1)
                elif kind == "softmax_top":
                    dve.wait_ge(logits_ready, 1)
                    step(nc.vector.tensor_tensor(scores[:], logits, bias[:].unsqueeze(1).to_broadcast([P, NT, E]), ALU.add))
                    step(nc.vector.tensor_reduce(small[:, :, 0:1], scores[:], AX.X, ALU.max))
                    nc.vector.tensor_tensor(scores[:], scores[:], wide(small[:, :, 0:1], E), ALU.subtract).then_inc(shifted, 1)
                    dve.wait_ge(exp_ready, 1)
                    step(nc.vector.tensor_reduce(small[:, :, 1:2], scores[:], AX.X, ALU.add))
                    step(nc.vector.reciprocal(small[:, :, 1:2], small[:, :, 1:2]))
                    step(nc.vector.tensor_tensor(ranked[:, :, 0:E], scores[:], wide(small[:, :, 1:2], E), ALU.mult))
                    rank()
                    find_top(top, mask[:])
                    nc.vector.tensor_tensor(g_tm[:, :, 0:E], mask[:], ranked[:, :, 0:E], ALU.mult)
                    nc.vector.memset(g_tm[:, :, E:E + 1], 1.0).then_inc(gates_ready, 1)
                else:
                    dve.wait_ge(logits_ready, 1)
                    step(nc.vector.tensor_copy(ranked[:, :, 0:E], logits))
                    rank()
                    nc.vector.tensor_tensor(small[:, :, 0:1], top8[:, :, 1:2], top8[:, :, 0:1], ALU.subtract).then_inc(shifted, 1)
                    dve.wait_ge(exp_ready, 1)
                    find_top(2, g_tm[:, :, 32:32 + E])
                    find_top(1, g_tm[:, :, 0:E])
                    step(nc.vector.tensor_tensor(g_tm[:, :, 32:32 + E], g_tm[:, :, 32:32 + E], g_tm[:, :, 0:E], ALU.subtract))
                    step(nc.vector.tensor_scalar(small[:, :, 2:3], small[:, :, 1:2], 1.0, None, ALU.add))
                    step(nc.vector.reciprocal(small[:, :, 2:3], small[:, :, 2:3]))
                    step(nc.vector.tensor_tensor(small[:, :, 3:4], small[:, :, 1:2], small[:, :, 2:3], ALU.mult))
                    nc.vector.tensor_tensor(g_tm[:, :, 64:64 + E], g_tm[:, :, 0:E], wide(small[:, :, 2:3], E), ALU.mult)
                    nc.vector.tensor_tensor(g_tm[:, :, 96:96 + E], g_tm[:, :, 32:32 + E], wide(small[:, :, 3:4], E), ALU.mult).then_inc(gates_ready, 1)

                dve.wait_ge(gates_t_psum, B)
                flat = core.psum[:, 0:4, :].rearrange("p b n -> p (b n)")
                if kind == "top_capacity":
                    step(nc.vector.memset(gates_t[:], 0.0))
                    for k in range(2):
                        nc.vector.tensor_copy(masks_t[:, k, :], flat[32 * k:32 * k + E, :])
                        nc.vector.tensor_copy(probs_t[:, k, :], flat[64 + 32 * k:64 + 32 * k + E, :])
                    step(nc.vector.memset(ones[:], 1.0))
                    step(nc.vector.tensor_tensor_scan(count[:, 0, :], ones[:], masks_t[:, 0, :], 0.0, ALU.mult, ALU.add))
                    step(nc.vector.tensor_tensor_scan(count[:, 1, :], ones[:], masks_t[:, 1, :], count[:, 0, N - 1:N], ALU.mult, ALU.add))
                    for k in range(2):
                        step(nc.vector.scalar_tensor_tensor(probs_t[:, k, :], count[:, k, :], float(capacity), probs_t[:, k, :], ALU.is_le, ALU.mult))
                    step(nc.vector.tensor_tensor(gates_t[0:E, :], probs_t[:, 0, :], probs_t[:, 1, :], ALU.add))
                else:
                    step(nc.vector.tensor_copy(gates_t[:], flat[0:32, :]))
                nc.vector.tensor_copy(gates3[0:32, :], gates_t[:])
                step(nc.vector.tensor_copy(part[:], gates_t[:]))
                step(nc.vector.tensor_tensor(rest[:], gates_t[:], part[:], ALU.subtract))
                nc.vector.tensor_copy(gates3[32:64, :], rest[:])
                step(nc.vector.tensor_copy(part[:], rest[:]))
                nc.vector.tensor_tensor(gates3[64:96, :], rest[:], part[:], ALU.subtract)


def ffn0(core):
    d = core.dram
    with Stage(core, "f0") as st:
        gt, g3 = st.sb("gates_t", [32, N]), st.sb("gates3", [GR, N], BF16)
        router(core, "r0", "sigmoid_groups", x=core.x, w_dram=d["l0_router"], n_experts=16, top=4, gates_t=gt, gates3=g3,
               bias_dram=d["l0_ebias"], tri_dram=d["c_tri"])
        experts(core, "e0", act_func=ACT.Silu, x=core.x, resid=core.x, gates_t=gt, gates3=g3, n_slots=9, unroll=3, tiles=1,
                w_dram=d["l0_experts"], glu=True)


def ffn1(core):
    d = core.dram
    with Stage(core, "f1") as st:
        gt, g3 = st.sb("gates_t", [32, N]), st.sb("gates3", [GR, N], BF16)
        capacity = int(2 * 1.25 * N / 8)
        capacity += capacity % 2
        router(core, "r1", "top_capacity", x=core.x, w_dram=d["l1_router"], n_experts=8, top=2, gates_t=gt, gates3=g3,
               capacity=capacity)
        experts(core, "e1", act_func=ACT.Gelu, x=core.x, resid=core.x, gates_t=gt, gates3=g3, n_slots=8, unroll=2, tiles=4,
                w_dram=d["l1_experts"])


def ffn3(core):
    d = core.dram
    with Stage(core, "f3") as st:
        gt, g3 = st.sb("gates_t", [32, N]), st.sb("gates3", [GR, N], BF16)
        b2 = st.sb("b2", [9, P])
        router(core, "r3", "softmax_top", x=core.x, w_dram=d["l3_router"], n_experts=8, top=2, gates_t=gt, gates3=g3,
               bias_dram=d["l3_rbias"], hid_dram=d["l3_gw1"], hid_bias_dram=d["l3_gb1"], more_loads=[(b2[:], d["l3_b2"])])
        experts(core, "e3", act_func=ACT.Gelu_apprx_tanh, x=core.x, resid=core.x, gates_t=gt, gates3=g3, n_slots=9, unroll=3, tiles=2,
                w_dram=d["l3_experts"], with_b1=True, b2=b2, b2_rows=9)


def init_sum(core, name, src, bias_dram=None, loads=()):
    nc = core.nc
    with Stage(core, name) as st:
        bias = st.sb("bias", [P, 1])
        loaded, for_later = st.sem("loaded"), st.sem("for_later")
        with nc.Block() as block:
            @block.sync
            def _(sp):
                if bias_dram is not None:
                    sp.dma_start(bias[:], bias_dram).then_inc(loaded, 16)
                for to, of in loads:
                    sp.dma_start(to, of).then_inc(for_later, 16)
                if loads:
                    sp.wait_ge(for_later, 16 * len(loads))

            @block.vector
            def _(dve):
                if bias_dram is None:
                    nc.vector.tensor_copy(core.sum[:], src[:])
                else:
                    dve.wait_ge(loaded, 16)
                    nc.vector.tensor_scalar(core.sum[:], src[:], bias[:], None, ALU.add)


def rope_attention(core, name, *, x, groups, heads, q_rows, w_dram, tables, qk_bias=False, v_bias=None):
    nc = core.nc
    dv = P // heads
    half = q_rows // 2
    halves = [(lo, lo + half if lo // half % 2 == 0 else lo - half) for lo in range(0, P, half)]
    AHEAD = 2
    wq_cols = P + 1 if qk_bias else P
    order = (0, 3, 1, 2)
    items = [(u, n, h) for u in range(B) for n in range(QT) for h in range(heads)]
    n_items, n_tiles = len(items), B * QT
    per_unit = QT * heads
    y_lag, out_lag = 2, 3
    parts = [(0, wq_cols), (wq_cols, wq_cols), (2 * wq_cols, P), (2 * wq_cols + P, P)]
    with Stage(core, name) as st:
        w = [st.sb(f"w{n}", [P, size]) for n, (_, size) in zip("qkvo", parts)]
        raw = st.sb("raw", [P, 2, T])
        swapped = st.sb("swapped", [P, 2, T])
        rot = st.sb("rot", [P, 2, T])
        qs = st.sb("q", [P, B, T])
        ks = st.sb("k", [P, B, T])
        vs = st.sb("v", [P, B, QT, P])
        probs = st.sb("probs", [P, 2, T])
        probs_t = st.sb("probs_t", [P, 2, QT, P])
        nmax = st.sb("nmax", [P, 4])
        rsum = st.sb("rsum", [P, QT, heads])
        rinv = st.sb("rinv", [P, QT, heads])
        y = st.sb("y", [P, 2, QT, P])
        y_t = st.sb("y_t", [P, T])
        w_loaded = [st.sem(f"w{n}_loaded") for n in "qkvo"]
        swap_loaded = [st.sem(f"{n}_swapped") for n in "qk"]
        (raw_ready, cos_ready, sin_ready, proj_ready, v_ready, qk_ready, s_ready, max_ready, probs_ready, pt_psum, pt_ready,
         y_psum, rinv_ready, y_ready, yt_psum, yt_ready, unit_done, sum_done) = (st.sem(n) for n in (
             "raw_ready", "cos_ready", "sin_ready", "proj_ready", "v_ready", "qk_ready", "s_ready", "max_ready", "probs_ready",
             "pt_psum", "pt_ready", "y_psum", "rinv_ready", "y_ready", "yt_psum", "yt_ready", "unit_done", "sum_done"))
        ps_s = [core.psum[:, k, :] for k in range(2)]
        ps_t = [core.psum[:, 2 + k, :] for k in range(2)]
        ps_y = core.psum[:, 4, 0:P]
        ps_o = core.psum[:, 5, :]
        ps_p = [core.psum[:, 6 + k, :] for k in range(2)]

        def whole(i, j):
            return i + j // n_items, j % n_items

        def per_group(engine, body):
            body(0, True, False)
            with engine.Fori(1, groups - 1) as i:
                body(i, False, False)
            body(groups - 1, False, True)

        with nc.Block() as block:
            @block.sync
            def _(sp):
                def load(i, k):
                    at, size = parts[k]
                    sp.dma_start(w[k][:], w_dram[bass.ds(i, 1), :, at:at + size].rearrange("o p n -> p (o n)")).then_inc(w_loaded[k], 16)

                def group(i, first, last):
                    for u in range(B):
                        U = i * B + u
                        for j in range(2):
                            sp.wait_ge(raw_ready, 2 * U + j + 1)
                            sp.wait_ge(qk_ready, 2 * U + j + 1)
                            for lo, hi in halves:
                                sp.dma_start(swapped[hi:hi + half, j, :], raw[lo:lo + half, j, :]).then_inc(swap_loaded[j], 16)
                            if u == B - 1 and not last:
                                load(i + 1, j)
                        if u == B - 1 and not last:
                            sp.wait_ge(proj_ready, 3 * U + 3)
                            load(i + 1, 2)
                        if u == 2:
                            sp.wait_ge(unit_done, i * B + B)
                            load(i, 3)

                for k in range(3):
                    load(0, k)
                per_group(sp, group)

            @block.gpsimd
            def _(pool):
                pool.sem_inc(qk_ready, 2)
                with pool.Fori(0, groups) as i:
                    for u in range(B):
                        U = i * B + u
                        pool.wait_ge(unit_done, U + 1)
                        for j, to in enumerate((qs, ks)):
                            pool.wait_ge(swap_loaded[j], (U + 1) * (16 * len(halves)))
                            nc.gpsimd.tensor_tensor(swapped[:, j, :], swapped[:, j, :], tables[:, 2 * j + 1, :], ALU.mult).then_inc(sin_ready, 1)
                            pool.wait_ge(sin_ready, 2 * U + j + 1)
                            pool.wait_ge(cos_ready, 2 * U + j + 1)
                            nc.gpsimd.tensor_tensor(to[:, u, :], rot[:, j, :], swapped[:, j, :], ALU.add).then_inc(qk_ready, 1)

            @block.tensor
            def _(pe):
                pe.sem_inc(unit_done, B)
                pe.sem_inc(pt_psum, 2)
                pe.sem_inc(y_psum, 2)
                pe.sem_inc(yt_psum, 2)

                def project(i, u, part):
                    U = i * B + u
                    if u == 0:
                        pe.wait_ge(w_loaded[part], 16 * i + 16)
                    if part == 2:
                        pe.wait_ge(raw_ready, 2 * U + 1)
                        for t in range(QT):
                            last = nc.tensor.matmul(ps_p[0][:, t * P:(t + 1) * P], x[:, u * T + t * P:u * T + (t + 1) * P], w[2][:], start=True, stop=True)
                        last.then_inc(proj_ready, 1)
                    else:
                        pe.wait_ge(v_ready if part == 0 else raw_ready, U + 1 if part == 0 else 2 * U + 1)
                        nc.tensor.matmul(ps_p[part], w[part][:, 0:P], x[:, cols(u)], start=True, stop=True).then_inc(proj_ready, 1)

                def scores(i, j):
                    u, n, h = items[j]
                    q = order[n]
                    if n == 0 and h == 0:
                        pe.wait_ge(qk_ready, 2 * (i * B + u) + 2 + 2)
                    pe.wait_ge(probs_ready, i * n_items + j + 1)
                    rows = slice(h * q_rows, (h + 1) * q_rows)
                    nc.tensor.matmul(ps_s[j % 2][:, 0:(q + 1) * P], qs[rows, u, q * P:(q + 1) * P], ks[rows, u, 0:(q + 1) * P],
                                     start=True, stop=False)
                    nc.tensor.matmul(ps_s[j % 2][:, q * P:(q + 1) * P], core.identb[:], core.maskb[:],
                                     start=False, stop=True).then_inc(s_ready, 1)

                def transpose(i, j):
                    q = order[items[j][1]]
                    g = i * n_items + j
                    pe.wait_ge(probs_ready, g + 1 + 2)
                    pe.wait_ge(pt_ready, g + 1)
                    for k in range(q + 1):
                        last = nc.tensor.transpose(ps_t[j % 2][:, k * P:(k + 1) * P], probs[:, j % 2, k * P:(k + 1) * P], core.ident[:])
                    last.then_inc(pt_psum, 1)

                def values(i, j):
                    u, n, h = items[j]
                    q = order[n]
                    if n == 0 and h == 0:
                        pe.wait_ge(v_ready, i * B + u + 1 + 1)
                    if h == 0:
                        pe.wait_ge(y_ready, i * n_tiles + u * QT + n + 1)
                    pe.wait_ge(pt_ready, i * n_items + j + 1 + 2)
                    for k in range(q + 1):
                        last = nc.tensor.matmul(ps_y[:, h * dv:(h + 1) * dv], probs_t[:, j % 2, k, :], vs[:, u, k, h * dv:(h + 1) * dv],
                                                start=k == 0, stop=k == q)
                    last.then_inc(y_psum, 1)

                def y_transposes(i, j):
                    u = items[j][0]
                    if j % per_unit == per_unit - 1:
                        pe.wait_ge(sum_done, i * B + u + 1)
                        pe.wait_ge(y_ready, i * n_tiles + u * QT + QT + 1)
                        for q in range(QT):
                            last = nc.tensor.transpose(ps_o[:, q * P:(q + 1) * P], y[:, u % 2, q, :], core.ident[:])
                        last.then_inc(yt_psum, 1)

                def out(i, j):
                    u = items[j][0]
                    if j % per_unit == per_unit - 1:
                        if u == 0:
                            pe.wait_ge(w_loaded[3], 16 * i + 16)
                        pe.wait_ge(yt_ready, i * B + u + 1)
                        nc.tensor.matmul(ps_o, w[3][:], y_t[:], start=True, stop=True).then_inc(unit_done, 1)

                def group(i, first, last):
                    for j in range(n_items + (out_lag if last else 0)):
                        if j + 1 < n_items or not last:
                            scores(*whole(i, j + 1))
                        if j < n_items:
                            transpose(i, j)
                        for step, back in ((values, 1), (out, out_lag), (y_transposes, y_lag)):
                            if (j >= back or not first) and j - back < n_items:
                                step(*whole(i, j - back))
                        u = j // per_unit + AHEAD
                        if j % per_unit < 3 and (u < B or not last):
                            project(i + u // B, u % B, j % per_unit)

                for u in range(AHEAD):
                    for part in range(3):
                        project(0, u, part)
                scores(0, 0)
                per_group(pe, group)

            @block.scalar
            def _(act):
                nc.scalar.preload_act_table_set("natural_log_exp_and_others")
                act.sem_inc(probs_ready, 2)

                def unrotated(i, u, part):
                    U = i * B + u
                    act.wait_ge(qk_ready, 2 * U + part + 1)
                    act.wait_ge(proj_ready, 3 * U + part + 1)
                    bias = {"bias": w[part][:, P:P + 1]} if qk_bias else {}
                    nc.scalar.activation(raw[:, part, :], ps_p[part], ACT.Identity, **bias).then_inc(raw_ready, 1)

                def group(i, first, last):
                    for j, (u, n, h) in enumerate(items):
                        g, q = i * n_items + j, order[n]
                        act.wait_ge(max_ready, g + 1)
                        act.wait_ge(pt_psum, g + 1)
                        nc.scalar.activation(probs[:, j % 2, 0:(q + 1) * P], ps_s[j % 2][:, 0:(q + 1) * P], ACT.Exp,
                                             bias=nmax[:, j % 4:j % 4 + 1], accum_out=rsum[:, q, h:h + 1]).then_inc(probs_ready, 1)
                        if 1 <= j % per_unit < 3 and (u + AHEAD < B or not last):
                            unrotated(i + (u + AHEAD) // B, (u + AHEAD) % B, j % per_unit - 1)

                for u in range(AHEAD):
                    unrotated(0, u, 0)
                    unrotated(0, u, 1)
                per_group(act, group)

            @block.vector
            def _(dve):
                dve.sem_inc(v_ready, 1)
                dve.sem_inc(pt_ready, 2)
                dve.sem_inc(y_ready, 1)
                dve.sem_inc(sum_done, 1)

                def project(i, u, part):
                    U = i * B + u
                    if part == 2:
                        dve.wait_ge(unit_done, U + 1)
                        dve.wait_ge(proj_ready, 3 * U + 3)
                        of = ps_p[0].rearrange("p (t d) -> p t d", d=P)
                        if v_bias is None:
                            nc.vector.tensor_copy(vs[:, u, :, :], of).then_inc(v_ready, 1)
                        else:
                            bias = v_bias[:, bass.ds(i * P, P)].unsqueeze(1).to_broadcast([P, QT, P])
                            nc.vector.tensor_tensor(vs[:, u, :, :], of, bias, ALU.add).then_inc(v_ready, 1)
                    else:
                        dve.wait_ge(raw_ready, 2 * U + part + 1)
                        dve.wait_ge(qk_ready, 2 * U + part + 1)
                        nc.vector.tensor_tensor(rot[:, part, :], raw[:, part, :], tables[:, 2 * part, :], ALU.mult).then_inc(cos_ready, 1)

                def maximum(i, j):
                    q = order[items[j][1]]
                    dve.wait_ge(s_ready, i * n_items + j + 1)
                    nc.vector.tensor_reduce(nmax[:, j % 4:j % 4 + 1], ps_s[j % 2][:, 0:(q + 1) * P], AX.X, ALU.max, negate=True).then_inc(max_ready, 1)

                def copy_t(i, j):
                    q = order[items[j][1]]
                    g = i * n_items + j
                    dve.wait_ge(pt_psum, g + 1 + 2)
                    dve.wait_ge(y_psum, g + 1)
                    nc.vector.tensor_copy(probs_t[:, j % 2, 0:q + 1, :].rearrange("p k n -> p (k n)"), ps_t[j % 2][:, 0:(q + 1) * P]).then_inc(pt_ready, 1)

                def normalise(i, j):
                    u, n, h = items[j]
                    q = order[n]
                    if h == heads - 1:
                        tile = i * n_tiles + u * QT + n
                        dve.wait_ge(y_psum, i * n_items + j + 1 + 2)
                        nc.vector.reciprocal(rinv[:, q, :], rsum[:, q, :]).then_inc(rinv_ready, 1)
                        dve.wait_ge(rinv_ready, tile + 1)
                        dve.wait_ge(yt_psum, i * B + u + 1)
                        nc.vector.tensor_tensor(y[:, u % 2, q, :].rearrange("p (h d) -> p h d", h=heads), ps_y.rearrange("p (h d) -> p h d", h=heads),
                                                rinv[:, q, :].unsqueeze(2).to_broadcast([P, heads, dv]), ALU.mult).then_inc(y_ready, 1)

                def copy_y(i, j):
                    if j % per_unit == per_unit - 1:
                        U = i * B + items[j][0]
                        dve.wait_ge(yt_psum, U + 1 + 2)
                        dve.wait_ge(unit_done, U + B)
                        nc.vector.tensor_copy(y_t[:], ps_o).then_inc(yt_ready, 1)

                def add_out(i, j):
                    if j % per_unit == per_unit - 1:
                        u = items[j][0]
                        U = i * B + u
                        dve.wait_ge(unit_done, U + 1 + B)
                        dve.wait_ge(sum_done, U + 1)
                        nc.vector.tensor_tensor(core.sum[:, cols(u)], ps_o, core.sum[:, cols(u)], ALU.add).then_inc(sum_done, 1)

                def group(i, first, last):
                    for j in range(n_items + (out_lag if last else 0)):
                        if j + 1 < n_items or not last:
                            maximum(*whole(i, j + 1))
                        if j < n_items:
                            copy_t(i, j)
                        for step, back in ((add_out, out_lag), (normalise, 1), (copy_y, y_lag)):
                            if (j >= back or not first) and j - back < n_items:
                                step(*whole(i, j - back))
                        u, part = j // per_unit + AHEAD, j % per_unit - 1
                        if 0 <= part < 3 and (u < B or not last) and j < n_items:
                            project(i + u // B, u % B, part)

                for u in range(AHEAD):
                    for part in range(3):
                        project(0, u, part)
                maximum(0, 0)
                per_group(dve, group)


def attn2(core):
    with Stage(core, "a2t") as st:
        tables = st.sb("tables", [P, 4, T])
        init_sum(core, "i2", core.x, loads=[(tables[:], core.dram["c_rope2"])])
        rope_attention(core, "a2", x=core.x, groups=8, heads=1, q_rows=P, w_dram=core.dram["l2_heads"], tables=tables)


def direction_scores(core, w_wide, q_parts, k_parts, v_aug):
    nc, dram = core.nc, core.dram
    with Stage(core, "a1p") as st:
        wv = st.sb("wv", [P, P])
        part_cols = st.sb("part_cols", [P, 5])
        raw = st.sb("raw", [P, 4, T])
        high = st.sb("high", [P, 4, T], BF16)
        rest = st.sb("rest", [P, 4, T])
        middle = st.sb("middle", [P, 4, T], BF16)
        (loaded, proj_ready, raw_ready, high_ready, rest_ready, middle_pool, middle_act, parts_ready, v_psum, v_zero, v_ones) = (
            st.sem(n) for n in ("loaded", "proj_ready", "raw_ready", "high_ready", "rest_ready", "middle_pool", "middle_act", "parts_ready",
                                "v_psum", "v_zero", "v_ones"))
        items = [(b, kind, g) for b in range(B) for kind in range(2) for g in range(2)]
        ps = [core.psum[:, k, :] for k in range(4)]
        with nc.Block() as block:
            @block.sync
            def _(sp):
                sp.dma_start(wv[:], dram["l1_wv"]).then_inc(loaded, 16)
                sp.dma_start(part_cols[:], dram["c_parts"]).then_inc(loaded, 16)

            @block.tensor
            def _(pe):
                pe.wait_ge(loaded, 2 * 16)
                for n, (b, kind, g) in enumerate(items):
                    if n >= 4:
                        pe.wait_ge(high_ready, n - 3)
                    nc.tensor.matmul(ps[n % 4], w_wide[:, kind, g, :], core.x[:, cols(b)], start=True, stop=True).then_inc(proj_ready, 1)
                    if kind == 1 and g == 1:
                        for t in range(QT):
                            at = b * T + t * P
                            last = nc.tensor.matmul(core.psum[:, 4 + b, t * P:(t + 1) * P], core.x[:, at:at + P], wv[:], start=True, stop=True)
                        last.then_inc(v_psum, 1)

            @block.scalar
            def _(act):
                def middle_of(n):
                    act.wait_ge(rest_ready, n + 1)
                    nc.scalar.activation(middle[:, n % 4, :], rest[:, n % 4, :], ACT.Copy).then_inc(middle_act, 1)

                act.wait_ge(loaded, 2 * 16)
                for n, (b, kind, g) in enumerate(items):
                    act.wait_ge(proj_ready, n + 1)
                    if n >= 4:
                        act.wait_ge(parts_ready, n - 3)
                    bias = {"bias": part_cols[:, 4:5]} if kind == 1 else {}
                    nc.scalar.activation(raw[:, n % 4, :], ps[n % 4], ACT.Identity, **bias).then_inc(raw_ready, 1)
                    nc.scalar.activation(high[:, n % 4, :], ps[n % 4], ACT.Identity, **bias).then_inc(high_ready, 1)
                    if n % 2 == 0 and n >= 2:
                        middle_of(n - 1)
                middle_of(len(items) - 1)

            @block.gpsimd
            def _(pool):
                nc.gpsimd.memset(v_aug[:], 0.0).then_inc(v_zero, 1)
                for n in range(0, len(items), 2):
                    pool.wait_ge(rest_ready, n + 1)
                    if n >= 4:
                        pool.wait_ge(parts_ready, n - 3)
                    nc.gpsimd.tensor_copy(middle[:, n % 4, :], rest[:, n % 4, :]).then_inc(middle_pool, 1)

            @block.vector
            def _(dve):
                dve.wait_ge(loaded, 2 * 16)

                def remainder(n):
                    kind = items[n][1]
                    dve.wait_ge(high_ready, n + 1)
                    nc.vector.scalar_tensor_tensor(rest[:, n % 4, :], high[:, n % 4, :], part_cols[:, 2 * kind:2 * kind + 1],
                                                   raw[:, n % 4, :], ALU.mult, ALU.add).then_inc(rest_ready, 1)

                remainder(0)
                for n, (b, kind, g) in enumerate(items):
                    if n + 1 < len(items):
                        remainder(n + 1)
                    dve.wait_ge((middle_pool, middle_act)[n % 2], n // 2 + 1)
                    to = (q_parts, k_parts)[kind][:, g, cols(b)]
                    nc.vector.scalar_tensor_tensor(to, middle[:, n % 4, :], part_cols[:, 2 * kind + 1:2 * kind + 2],
                                                   rest[:, n % 4, :], ALU.mult, ALU.add).then_inc(parts_ready, 1)
                    if kind == 1 and g == 1:
                        if b == 0:
                            dve.wait_ge(v_zero, 1)
                            nc.vector.memset(v_aug[:, :, :, 16:17], 1.0).then_inc(v_ones, 1)
                        dve.wait_ge(v_psum, b + 1)
                        nc.vector.tensor_copy(v_aug[:, b * QT:(b + 1) * QT, :, 0:16].rearrange("p t h d -> p (t h) d"),
                                              core.psum[:, 4 + b, :].rearrange("p (n d) -> p n d", d=16))


def direction_attention(core, q_parts, k_parts, v_aug, w_out, sum_spread):
    nc = core.nc
    first_items = [(h, q) for h in range(4) for q in range(QT)]
    second_items = [(h, k) for h in range(4) for k in range(QT)]
    n = len(first_items)
    in_slot = [[k for k in range(n) if k * 3 // 4 == j] for j in range(n)]
    with Stage(core, "a1") as st:
        nmax = st.sb("nmax", [P, QT, 4])
        nrest = st.sb("nrest", [P, QT, 4])
        nparts = st.sb("nparts", [P, QT, 4, 32], BF16)
        q_first, k_first, k_second = (st.sb(name, [P, 2, T], BF16) for name in ("q_first", "k_first", "k_second"))
        q_less = st.sb("q_less", [P, 2, T], BF16)
        v = st.sb("v", [P, 2, QT, P])
        probs_t = st.sb("probs_t", [P, 2, T])
        y = st.sb("y", [P, 2, T])
        ln_sum = st.sb("ln_sum", [P, T])
        inv_sum = st.sb("inv_sum", [P, T])
        yn = st.sb("yn", [P, 2, T])
        (zeroed, a_ready, max_ready, nparts_ready, rows_ready, q_ready, s_ready, probs_ready, first_ready, second_ready, values_done, y_ready,
         sums_ready, ln_ready, inv_ready, yn_ready, out_done, sum_done, split_step, passed) = (st.sem(n) for n in (
             "zeroed", "a_ready", "max_ready", "nparts_ready", "rows_ready", "q_ready", "s_ready", "probs_ready", "first_ready", "second_ready",
             "values_done", "y_ready", "sums_ready", "ln_ready", "inv_ready", "yn_ready", "out_done", "sum_done", "split_step",
             "passed"))
        ps_a = [core.psum[:, k, :] for k in range(2)]
        ps_s = [core.psum[:, 2 + k, :] for k in range(2)]
        ps_y = [core.psum[:, 4 + k, :] for k in range(2)]
        ps_m = core.psum[:, 6, :]
        ps_o = core.psum[:, 7, :]

        def per_sequence(engine, body):
            body(0, True, False)
            with engine.Fori(1, B - 1) as b:
                body(b, False, False)
            body(B - 1, False, True)

        def ahead(b, g):
            return (b, 1) if g == 0 else (b + 1, 0)

        def behind(b, g):
            return (b, 0) if g == 1 else (b - 1, 1)

        with nc.Block() as block:
            @block.gpsimd
            def _(pool):
                nc.gpsimd.memset(nparts[:], 0.0).then_inc(zeroed, 1)
                with pool.Fori(0, B) as b:
                    for g in range(2):
                        pool.wait_ge(a_ready, (2 * b + g) * n + n)
                        pool.sem_inc(passed, 1)
                        nc.gpsimd.tensor_copy(q_first[:, g, :], q_parts[:, g, cols(b)])
                        nc.gpsimd.tensor_copy(k_first[:, g, :], k_parts[:, g, cols(b)]).then_inc(first_ready, 1)
                        pool.wait_ge(values_done, (2 * b + g) * n + n)
                        pool.sem_inc(passed, 1)
                        nc.gpsimd.tensor_copy(k_second[:, g, :], k_parts[:, g, cols(b)])
                        nc.gpsimd.tensor_copy(v[:, g, :, :], v_aug[:].rearrange("p t h d -> p t (h d)")[:, bass.ds(b * QT, QT), g * P:(g + 1) * P]).then_inc(second_ready, 1)

            @block.tensor
            def _(pe):
                pe.sem_inc(a_ready, 2 * n)
                pe.sem_inc(values_done, 2 * n)
                pe.sem_inc(out_done, 2)

                def first_scores(b, g, k):
                    h, q = first_items[k]
                    rows = slice(32 * h, 32 * h + 32)
                    if k == 0:
                        pe.wait_ge(first_ready, 2 * b + g + 1)
                    pe.wait_ge(max_ready, (2 * b + g) * n + k + 1)
                    nc.tensor.matmul(ps_a[k % 2][:, 0:(q + 1) * P], q_first[rows, g, q * P:(q + 1) * P],
                                     k_first[rows, g, 0:(q + 1) * P], start=True, stop=False)
                    nc.tensor.matmul(ps_a[k % 2][:, q * P:(q + 1) * P], core.identb[:], core.maskb[:],
                                     start=False, stop=True).then_inc(a_ready, 1)

                def max_rows(b, g):
                    U = 2 * b + g
                    pe.wait_ge(nparts_ready, U + 1)
                    pe.wait_ge(ln_ready, U + 1)
                    for t in range(QT):
                        last = nc.tensor.matmul(ps_m[:, t * P:(t + 1) * P], nparts[:, t, :, :].rearrange("p h r -> p (h r)"), core.identb[:],
                                                start=True, stop=True)
                    last.then_inc(rows_ready, 1)

                def second_scores(b, g, j):
                    h, k = second_items[j]
                    rows, size = slice(32 * h, 32 * h + 32), (QT - k) * P
                    U = 2 * b + g
                    if j == 0:
                        pe.wait_ge(second_ready, U + 1)
                        pe.wait_ge(q_ready, U + 1)
                    pe.wait_ge(probs_ready, U * n + j + 1)
                    nc.tensor.matmul(ps_s[j % 2][:, 0:size], k_second[rows, g, k * P:(k + 1) * P], q_less[rows, g, k * P:T],
                                     start=True, stop=False)
                    nc.tensor.matmul(ps_s[j % 2][:, 0:P], core.maskb[:], core.identb[:], start=False, stop=True).then_inc(s_ready, 1)

                def values(b, g, j):
                    h, k = second_items[j]
                    U = 2 * b + g
                    if j == 0:
                        pe.wait_ge(y_ready, U + 1)
                    pe.wait_ge(probs_ready, U * n + j + 1 + 2)
                    nc.tensor.matmul(ps_y[g][32 * h:32 * h + 32, k * P:T], v[:, g, k, 32 * h:32 * h + 32], probs_t[:, j % 2, 0:(QT - k) * P],
                                     start=k == 0, stop=k == QT - 1, skip_group_check=True).then_inc(values_done, 1)

                def spread_sums(b, g):
                    pe.wait_ge(y_ready, 2 * b + g + 1 + 2)
                    nc.tensor.matmul(ps_m, sum_spread[:], y[:, g, :], start=True, stop=True).then_inc(sums_ready, 1)

                def out(b, g):
                    pe.wait_ge(yn_ready, 2 * b + g + 1 + 2)
                    if g == 0:
                        pe.wait_ge(sum_done, b + 1)
                    nc.tensor.matmul(ps_o, w_out[:, g, :], yn[:, g, :], start=g == 0, stop=g == 1, skip_group_check=True).then_inc(out_done, 1)

                def sequence(b, first, last):
                    for g in range(2):
                        nxt = None if last and g == 1 else ahead(b, g)
                        for j in range(n):
                            if j + 1 < n:
                                second_scores(b, g, j + 1)
                            elif nxt:
                                second_scores(*nxt, 0)
                            for k in in_slot[j] if nxt else []:
                                first_scores(*nxt, k)
                            values(b, g, j)
                            if j == 1 and not (first and g == 0):
                                spread_sums(*behind(b, g))
                            if j == 6 and not (first and g == 0):
                                out(*behind(b, g))
                            if j == 13 and nxt:
                                max_rows(*nxt)

                for k in range(n):
                    first_scores(0, 0, k)
                max_rows(0, 0)
                second_scores(0, 0, 0)
                per_sequence(pe, sequence)
                spread_sums(B - 1, 1)
                out(B - 1, 1)

            @block.scalar
            def _(act):
                nc.scalar.preload_act_table_set("natural_log_exp_and_others")
                act.sem_inc(probs_ready, 2)
                act.sem_inc(y_ready, 2)
                act.sem_inc(ln_ready, 2)

                def probabilities(b, g, j):
                    size = (QT - second_items[j][1]) * P
                    U = 2 * b + g
                    act.wait_ge(s_ready, U * n + j + 1)
                    act.wait_ge(values_done, U * n + j - 1 + 2 * n)
                    nc.scalar.activation(probs_t[:, j % 2, 0:size], ps_s[j % 2][:, 0:size], ACT.Exp).then_inc(probs_ready, 1)

                def copy_y(b, g):
                    U = 2 * b + g
                    act.wait_ge(values_done, U * n + n + 2 * n)
                    act.wait_ge(yn_ready, U + 1)
                    nc.scalar.activation(y[:, g, :], ps_y[g], ACT.Identity).then_inc(y_ready, 1)

                def inverse(b, g):
                    U = 2 * b + g
                    act.wait_ge(sums_ready, U + 1)
                    nc.scalar.activation(ln_sum[:], ps_m, ACT.Ln).then_inc(ln_ready, 1)
                    act.wait_ge(ln_ready, U + 1 + 2)
                    act.wait_ge(yn_ready, U + 2)
                    nc.scalar.activation(inv_sum[:], ln_sum[:], ACT.Exp, scale=-1.0).then_inc(inv_ready, 1)

                def sequence(b, first, last):
                    for g in range(2):
                        for j in range(n):
                            probabilities(b, g, j)
                            if j == 0 and not (first and g == 0):
                                copy_y(*behind(b, g))
                            if j == 2 and not (first and g == 0):
                                inverse(*behind(b, g))

                per_sequence(act, sequence)
                copy_y(B - 1, 1)
                inverse(B - 1, 1)

            @block.vector
            def _(dve):
                dve.sem_inc(max_ready, 2)
                dve.sem_inc(yn_ready, 2)
                dve.sem_inc(sum_done, 1)
                dve.wait_ge(zeroed, 1)

                def maximum(b, g, k):
                    h, q = first_items[k]
                    dve.wait_ge(a_ready, (2 * b + g) * n + k + 1 + 2 * n)
                    nc.vector.tensor_reduce(nmax[:, q, h:h + 1], ps_a[k % 2][:, 0:(q + 1) * P], AX.X, ALU.max, negate=True).then_inc(max_ready, 1)

                def split_maxima(b, g):
                    U = 2 * b + g
                    step = Steps(dve, split_step, U * 3)
                    dve.wait_ge(max_ready, U * n + n + 2)
                    step(nc.vector.tensor_copy(nparts[:, :, :, 24], nmax[:]))
                    step(nc.vector.tensor_tensor(nrest[:], nmax[:], nparts[:, :, :, 24], ALU.subtract))
                    step(nc.vector.tensor_copy(nparts[:, :, :, 25], nrest[:]))
                    nc.vector.tensor_tensor(nparts[:, :, :, 26], nrest[:], nparts[:, :, :, 25], ALU.subtract).then_inc(nparts_ready, 1)

                def less_maxima(b, g):
                    dve.wait_ge(rows_ready, 2 * b + g + 1)
                    nc.vector.tensor_tensor(q_less[:, g, :], ps_m, q_parts[:, g, cols(b)], ALU.add).then_inc(q_ready, 1)

                def normalise(b, g):
                    U = 2 * b + g
                    dve.wait_ge(inv_ready, U + 1)
                    dve.wait_ge(out_done, U + 1)
                    nc.vector.tensor_tensor(yn[:, g, :], y[:, g, :], inv_sum[:], ALU.mult).then_inc(yn_ready, 1)

                def add_out(b):
                    dve.wait_ge(out_done, 2 * b + 2 + 2)
                    nc.vector.tensor_tensor(core.sum[:, cols(b)], ps_o, core.x[:, cols(b)], ALU.add).then_inc(sum_done, 1)

                def sequence(b, first, last):
                    for g in range(2):
                        nxt = None if last and g == 1 else ahead(b, g)
                        for j in range(n):
                            for k in in_slot[j] if nxt else []:
                                maximum(*nxt, k)
                            if j == 4 and not (first and g == 0):
                                normalise(*behind(b, g))
                            if j == 8 and g == 0 and not first:
                                add_out(b - 1)
                            if j == 12 and nxt:
                                split_maxima(*nxt)
                            if j == 14 and nxt:
                                less_maxima(*nxt)

                for k in range(n):
                    maximum(0, 0, k)
                split_maxima(0, 0)
                less_maxima(0, 0)
                per_sequence(dve, sequence)
                normalise(B - 1, 1)
                add_out(B - 1)



def attn1(core):
    nc, dram = core.nc, core.dram
    with Stage(core, "a1w") as st:
        w_wide = st.sb("w_wide", [P, 2, 2, P])
        w_out = st.sb("w_out", [P, 2, P])
        sum_spread = st.sb("sum_spread", [P, P])
        q_parts, k_parts = (st.sb(n, [P, 2, N], BF16) for n in ("q_parts", "k_parts"))
        v_aug = st.sb("v_aug", [P, NT, 8, 32])
        w3 = st.sb("w3", [24, 2, P])
        spread = st.sb("spread", [24, 2 * P])
        scale = st.sb("scale", [P, 1])
        loaded, wide_psum, wide_ready = (st.sem(n) for n in ("loaded", "wide_psum", "wide_ready"))
        with nc.Block() as block:
            @block.sync
            def _(sp):
                sp.dma_start(w3[:, 0, :], dram["l1_wq"]).then_inc(loaded, 16)
                sp.dma_start(w3[:, 1, :], dram["l1_wk"]).then_inc(loaded, 16)
                sp.dma_start(spread[:], dram["c_spread"]).then_inc(loaded, 16)
                sp.dma_start(scale[:], dram["l1_scale"].partition_broadcast(P)).then_inc(loaded, 16)
                sp.dma_start(w_out[:], dram["l1_wout"]).then_inc(loaded, 16)
                sp.dma_start(sum_spread[:], dram["c_sumspread"]).then_inc(loaded, 16)

            @block.tensor
            def _(pe):
                pe.wait_ge(loaded, 6 * 16)
                for k in range(2):
                    nc.tensor.matmul(core.psum[:, k, 0:2 * P], w3[:, k, :], spread[:], start=True, stop=True).then_inc(wide_psum, 1)

            @block.vector
            def _(dve):
                dve.wait_ge(loaded, 6 * 16)
                dve.wait_ge(wide_psum, 2)
                for k in range(2):
                    last = nc.vector.tensor_copy(w_wide[:, k, :, :].rearrange("p g r -> p (g r)"), core.psum[:, k, 0:2 * P])
                last.then_inc(wide_ready, 1)
                dve.wait_ge(wide_ready, 1)
                rows = w_wide[:, 0, :, :].rearrange("p g (h r) -> p (g h) r", r=32)[:, :, 0:24].rearrange("p h (m c) -> p h m c", c=4)
                nc.vector.tensor_scalar(rows[:, :, :, 0:3], rows[:, :, :, 0:3], scale[:], None, ALU.mult)
        direction_scores(core, w_wide, q_parts, k_parts, v_aug)
        direction_attention(core, q_parts, k_parts, v_aug, w_out, sum_spread)


def rope_tables(core, tables, theta_dram, scale):
    nc = core.nc
    two_pi = 2 * np.pi
    c1 = 6.28125
    c2 = float(np.float32(np.round((two_pi - c1) * 2 ** 22) / 2 ** 22))
    c3 = float(two_pi - c1 - c2)
    magic = 1.5 * 2 ** 23
    with Stage(core, "rt") as st:
        pos, ang, turns, sin_h = (st.sb(n, [P, T]) for n in ("pos", "ang", "turns", "sin_h"))
        col = st.sb("col", [P, 2])
        loaded, reduced, sin_ready, dve_step = (st.sem(n) for n in ("loaded", "reduced", "sin_ready", "dve_step"))
        sin = tables[:, 3, :]
        with nc.Block() as block:
            @block.sync
            def _(sp):
                sp.dma_start(pos[:], core.dram["c_pos"].partition_broadcast(P)).then_inc(loaded, 16)
                sp.dma_start(col[:, 0:1], theta_dram).then_inc(loaded, 16)
                sp.dma_start(col[:, 1:2], core.dram["c_ropesign"]).then_inc(loaded, 16)

            @block.scalar
            def _(act):
                act.wait_ge(reduced, 1)
                nc.scalar.activation(sin, ang[:], ACT.Sin).then_inc(sin_ready, 1)
                nc.scalar.activation(sin_h[:], ang[:], ACT.Sin, scale=0.5).then_inc(sin_ready, 1)

            @block.vector
            def _(dve):
                step = Steps(dve, dve_step)
                dve.wait_ge(loaded, 3 * 16)
                step(nc.vector.tensor_scalar(ang[:], pos[:], col[:, 0:1], None, ALU.mult))
                step(nc.vector.tensor_scalar(turns[:], ang[:], 1 / two_pi, None, ALU.mult))
                step(nc.vector.tensor_scalar(turns[:], turns[:], magic, None, ALU.add))
                step(nc.vector.tensor_scalar(turns[:], turns[:], magic, None, ALU.subtract))
                for c in (c1, c2, c3):
                    step(nc.vector.scalar_tensor_tensor(ang[:], turns[:], -c, ang[:], ALU.mult, ALU.add))
                nc.vector.tensor_scalar(ang[:], ang[:], 3.1415925, -3.1415925, ALU.min, ALU.max).then_inc(reduced, 1)
                dve.wait_ge(sin_ready, 2)
                step(nc.vector.tensor_scalar(sin, sin, col[:, 1:2], None, ALU.mult))
                step(nc.vector.tensor_tensor(sin_h[:], sin_h[:], sin_h[:], ALU.mult))
                step(nc.vector.tensor_scalar(tables[:, 2, :], sin_h[:], -2.0, 1.0, ALU.mult, ALU.add))
                nc.vector.tensor_scalar(tables[:, 0:2, :], tables[:, 2:4, :], scale, None, ALU.mult)


def ffn2(core):
    nc, d = core.nc, core.dram
    with Stage(core, "f2") as st:
        xn = st.sb("xn", [P, N])
        norm(core, "g1", core.x, xn, False, 0, core.gammas[:, 0, 0:1])
        with Stage(core, "a2f") as sa:
            tables = sa.sb("tables", [P, 4, T])
            v_bias = sa.sb("v_bias", [P, 8 * P])
            init_sum(core, "if2", xn, d["l2_ob"], loads=[(v_bias[:], d["l2_vb"].partition_broadcast(P))])
            rope_tables(core, tables, d["l2_theta"], 64 ** -0.5)
            rope_attention(core, "h2", x=xn, groups=8, heads=2, q_rows=64, w_dram=d["l2f_heads"], tables=tables,
                      qk_bias=True, v_bias=v_bias)
        an = st.sb("an", [P, N])
        norm(core, "g2", core.sum, an, False, 0, core.gammas[:, 0, 1:2])
        added = st.sem("added")
        with nc.Block() as block:
            @block.vector
            def _(dve):
                nc.vector.tensor_tensor(xn[:], an[:], core.sum[:], ALU.add).then_inc(added, 1)
                dve.wait_ge(added, 1)
                nc.vector.tensor_tensor(xn[:], xn[:], core.x[:], ALU.add)
        gt, g3 = st.sb("gates_t", [32, N]), st.sb("gates3", [GR, N], BF16)
        b2 = st.sb("b2", [32, P])
        router(core, "r2", "softmax_top", x=an, w_dram=d["l2_router"], n_experts=31, top=3, gates_t=gt, gates3=g3,
               bias_dram=d["l2_rbias"], more_loads=[(b2[:], d["l2_b2"])])
        experts(core, "e2", act_func=ACT.Gelu, x=an, resid=xn, gates_t=gt, gates3=g3, n_slots=32, unroll=4, tiles=1,
                w_dram=d["l2_experts"], with_b1=True, b2=b2, b2_rows=32)


def hawk(core):
    nc, d = core.nc, core.dram
    with Stage(core, "h3") as st:
        xn = st.sb("xn", [P, N])
        x2 = st.sb("x2", [P, N])
        norm(core, "g3", core.x, xn, False, 2, core.gammas[:, 1, 0:1])
        recurrence(core, xn, x2)
        norm(core, "g4", x2, xn, False, 2, core.gammas[:, 1, 1:2])
        gated_mlp(core, xn, x2)


def recurrence(core, xn, x2):
    nc, d = core.nc, core.dram
    K = 4
    C = 2
    with Stage(core, "rc") as st:
        w_in = st.sb("w_in", [P, 4 * P])
        w_g = st.sb("w_g", [P, C, 4 * P])
        w_out = st.sb("w_out", [P, C, P])
        taps = st.sb("taps", [P, C, K])
        cols_ = st.sb("cols", [P, 8])
        coef = st.sb("coef", [P, C])
        small = st.sb("small", [P, 6, C])
        gate = st.sb("gate", [P, C, T])
        padded = st.sb("padded", [P, C, K - 1 + T])
        xc, alpha, inp, beta, h = (st.sb(n, [P, C, T]) for n in ("xc", "alpha", "inp", "beta", "h"))
        partial = st.sb("partial", [P, C, T])
        (loaded, abs_ready, u_ready, coef_ready, z_ready, gate_ready, conv_ready, g_ready, sig_ready, alpha_ready,
         sq_ready, rest_ready, ln_ready, beta_ready, scan_ready, h_ready, out_ready, out_added, dve_step) = (st.sem(n) for n in (
             "loaded", "abs_ready", "u_ready", "coef_ready", "z_ready", "gate_ready", "conv_ready", "g_ready", "sig_ready",
             "alpha_ready", "sq_ready", "rest_ready", "ln_ready", "beta_ready", "scan_ready", "h_ready", "out_ready", "out_added", "dve_step"))
        bank = [core.psum[:, k, :] for k in range(8)]
        loads = [(w_in[:], d["l3_win"]), (w_g[:], d["l3_wgates"]), (w_out[:], d["l3_wout"]), (taps[:], d["l3_taps"]), (cols_[:], d["l3_cols"])]
        DVE_STEPS = K + 2

        with nc.Block() as block:
            @block.sync
            def _(sp):
                for to, of in loads:
                    sp.dma_start(to, of).then_inc(loaded, 16)

            @block.tensor
            def _(pe):
                def z(c):
                    for k in range(4):
                        if k < C:
                            pe.wait_ge(gate_ready, 2 * c + k + 1)
                        elif k == C:
                            pe.wait_ge(out_added, c + 1)
                        nc.tensor.matmul(bank[k], w_in[:, k * P:(k + 1) * P], xn[:, cols(c)], start=True, stop=True).then_inc(z_ready, 1)

                def gates(c):
                    pe.wait_ge(conv_ready, c + 1)
                    for m in range(4):
                        pe.wait_ge(sig_ready, 4 * c + m + 1)
                        for k in range(C):
                            last = nc.tensor.matmul(bank[4 + m], w_g[:, k, m * P:(m + 1) * P], xc[:, k, :], start=k == 0, stop=k == C - 1)
                        last.then_inc(g_ready, 1)

                def out(c):
                    pe.wait_ge(h_ready, c + 1 + 1)
                    for k in range(C):
                        mm = nc.tensor.matmul(bank[2], w_out[:, k, :], h[:, k, :], start=k == 0, stop=k == C - 1)
                    mm.then_inc(out_ready, 1)

                def chunk(c, last):
                    if not last:
                        z(c + 1)
                        gates(c + 1)
                    out(c)

                pe.wait_ge(loaded, 16 * len(loads))
                z(0)
                gates(0)
                with pe.Fori(0, B - 1) as c:
                    chunk(c, False)
                chunk(B - 1, True)

            @block.scalar
            def _(act):
                act.wait_ge(loaded, 16 * len(loads))
                nc.scalar.activation(small[:, 0, :], cols_[:, 6:8], ACT.Abs).then_inc(abs_ready, 1)
                act.wait_ge(abs_ready, 1)
                nc.scalar.activation(small[:, 1, :], small[:, 0, :], ACT.Exp, scale=-1.0).then_inc(u_ready, 1)
                act.wait_ge(coef_ready, 1)
                act.sem_inc(gate_ready, C)
                act.sem_inc(sig_ready, 4)

                def gate_gelu(c):
                    for k in range(C):
                        act.wait_ge(z_ready, 4 * c + k + 1)
                        act.wait_ge(h_ready, c + 1)
                        nc.scalar.activation(gate[:, k, :], bank[k], ACT.Gelu).then_inc(gate_ready, 1)

                def chunk(c, last):
                    act.wait_ge(scan_ready, c + 1)
                    for m in range(4):
                        act.wait_ge(g_ready, 4 * c + m + 1)
                        to = alpha[:, m, :] if m < C else inp[:, m - C, :]
                        nc.scalar.activation(to, bank[4 + m], ACT.Sigmoid, bias=cols_[:, 2 + m:3 + m]).then_inc(sig_ready, 1)
                    nc.scalar.preload_act_table_set("natural_log_exp_and_others")
                    act.wait_ge(sig_ready, 4 * c + 4 + 4)
                    for k in range(C):
                        nc.scalar.activation(alpha[:, k, :], alpha[:, k, :], ACT.Exp, scale=coef[:, k:k + 1]).then_inc(alpha_ready, 1)
                    for k in range(C):
                        act.wait_ge(alpha_ready, 2 * c + k + 1)
                        nc.scalar.activation(beta[:, k, :], alpha[:, k, :], ACT.Square).then_inc(sq_ready, 1)
                    act.wait_ge(rest_ready, c + 1)
                    nc.scalar.activation(beta[:], beta[:], ACT.Ln, bias=core.eps[:, 1:2]).then_inc(ln_ready, 1)
                    act.wait_ge(ln_ready, c + 1)
                    nc.scalar.activation(beta[:], beta[:], ACT.Exp, scale=0.5).then_inc(beta_ready, 1)
                    if not last:
                        gate_gelu(c + 1)

                gate_gelu(0)
                with act.Fori(0, B - 1) as c:
                    chunk(c, False)
                chunk(B - 1, True)

            @block.vector
            def _(dve):
                u, s, s2, p, pos = (small[:, k, :] for k in range(1, 6))
                dve.wait_ge(loaded, 16 * len(loads))
                dve.wait_ge(u_ready, 1)
                pre = Steps(dve, dve_step)
                pre(nc.vector.tensor_scalar(s2, u, 2.0, None, ALU.add))
                pre(nc.vector.reciprocal(s2, s2))
                pre(nc.vector.tensor_tensor(s, u, s2, ALU.mult))
                pre(nc.vector.tensor_tensor(s2, s, s, ALU.mult))
                pre(nc.vector.memset(p, 1 / 19))
                for n in range(17, 0, -2):
                    pre(nc.vector.tensor_tensor(p, p, s2, ALU.mult))
                    pre(nc.vector.tensor_scalar(p, p, 1 / n, None, ALU.add))
                pre(nc.vector.tensor_tensor(p, p, s, ALU.mult))
                pre(nc.vector.tensor_scalar(p, p, 2.0, None, ALU.mult))
                pre(nc.vector.tensor_scalar(pos, cols_[:, 6:8], 0.0, None, ALU.max))
                pre(nc.vector.tensor_tensor(p, p, pos, ALU.add))
                nc.vector.tensor_scalar(coef[:], p, -8.0, None, ALU.mult).then_inc(coef_ready, 1)
                pre(nc.vector.memset(padded[:, :, 0:K - 1], 0.0))
                before = pre.n

                def convolve(c, step):
                    for k in range(C):
                        dve.wait_ge(z_ready, 4 * c + 2 + k + 1)
                        last = nc.vector.tensor_copy(padded[:, k, K - 1:], bank[2 + k])
                    step(last)
                    for t in range(K - 1):
                        for k in range(C):
                            seen = padded[:, k, t:t + T]
                            if t == 0:
                                last = nc.vector.tensor_scalar(partial[:, k, :], seen, taps[:, k, 0:1], cols_[:, k:k + 1], ALU.mult, ALU.add)
                            else:
                                last = nc.vector.scalar_tensor_tensor(partial[:, k, :], seen, taps[:, k, t:t + 1], partial[:, k, :], ALU.mult, ALU.add)
                        step(last)

                def last_tap(c):
                    for k in range(C):
                        last = nc.vector.scalar_tensor_tensor(xc[:, k, :], padded[:, k, K - 1:], taps[:, k, K - 1:K], partial[:, k, :], ALU.mult, ALU.add)
                    last.then_inc(conv_ready, 1)

                def add_out(c):
                    dve.wait_ge(out_ready, c + 1)
                    nc.vector.tensor_tensor(x2[:, cols(c)], bank[2], core.x[:, cols(c)], ALU.add).then_inc(out_added, 1)

                def chunk(c, first, last):
                    step = Steps(dve, dve_step, before + K + c * DVE_STEPS)
                    if not first:
                        add_out(c - 1)
                    if not last:
                        convolve(c + 1, step)
                    dve.wait_ge(sig_ready, 4 * c + 4 + 4)
                    step(nc.vector.tensor_tensor(inp[:], inp[:], xc[:], ALU.mult))
                    if not last:
                        last_tap(c + 1)
                    dve.wait_ge(sq_ready, 2 * c + 2)
                    nc.vector.tensor_scalar(beta[:], beta[:], -1.0, 1.0, ALU.mult, ALU.add).then_inc(rest_ready, 1)
                    dve.wait_ge(beta_ready, c + 1)
                    step(nc.vector.tensor_tensor(inp[:], inp[:], beta[:], ALU.mult))
                    for k in range(C):
                        scan = nc.vector.tensor_tensor_scan(h[:, k, :], alpha[:, k, :], inp[:, k, :], 0.0, ALU.mult, ALU.add)
                    scan.then_inc(scan_ready, 1)
                    dve.wait_ge(scan_ready, c + 1 + 1)
                    dve.wait_ge(gate_ready, 2 * c + 2 + C)
                    nc.vector.tensor_tensor(h[:], h[:], gate[:], ALU.mult).then_inc(h_ready, 1)
                    assert last or step.n == DVE_STEPS, step.n

                dve.sem_inc(scan_ready, 1)
                dve.sem_inc(h_ready, 1)
                dve.sem_inc(out_added, 2)
                convolve(0, Steps(dve, dve_step, before))
                last_tap(0)
                chunk(0, True, False)
                with dve.Fori(1, B - 1) as c:
                    chunk(c, False, False)
                chunk(B - 1, False, True)
                add_out(B - 1)


def gated_mlp(core, xn, x2):
    nc, d = core.nc, core.dram
    C = 2
    with Stage(core, "gm") as st:
        w_grow = st.sb("w_grow", [P, 4 * P])
        w_shrink = st.sb("w_shrink", [P, C, P])
        gate = st.sb("gate", [P, C, T])
        both = st.sb("both", [P, T])
        loaded, z_ready, gate_ready, prod_ready, out_ready, both_ready, chunk_done = (st.sem(n) for n in (
            "loaded", "z_ready", "gate_ready", "prod_ready", "out_ready", "both_ready", "chunk_done"))
        bank = [core.psum[:, k, :] for k in range(8)]
        with nc.Block() as block:
            @block.sync
            def _(sp):
                sp.dma_start(w_grow[:], d["l3_wgrow"]).then_inc(loaded, 16)
                sp.dma_start(w_shrink[:], d["l3_wshrink"]).then_inc(loaded, 16)

            @block.gpsimd
            def _(pool):
                with pool.Fori(0, B) as c:
                    pool.wait_ge(chunk_done, c + 1)
                    nc.gpsimd.tensor_tensor(both[:], core.x[:, cols(c)], x2[:, cols(c)], ALU.add).then_inc(both_ready, 1)

            @block.tensor
            def _(pe):
                pe.wait_ge(loaded, 32)
                with pe.Fori(0, B) as c:
                    pe.wait_ge(chunk_done, c + 1)
                    for k in range(4):
                        nc.tensor.matmul(bank[k], w_grow[:, k * P:(k + 1) * P], xn[:, cols(c)], start=True, stop=True).then_inc(z_ready, 1)
                    for k in range(C):
                        pe.wait_ge(prod_ready, 2 * c + k + 1)
                        last = nc.tensor.matmul(bank[4], w_shrink[:, k, :], gate[:, k, :], start=k == 0, stop=k == C - 1)
                    last.then_inc(out_ready, 1)

            @block.scalar
            def _(act):
                with act.Fori(0, B) as c:
                    for k in range(C):
                        act.wait_ge(z_ready, 4 * c + k + 1)
                        nc.scalar.activation(gate[:, k, :], bank[k], ACT.Gelu).then_inc(gate_ready, 1)

            @block.vector
            def _(dve):
                dve.sem_inc(chunk_done, 1)
                with dve.Fori(0, B) as c:
                    for k in range(C):
                        dve.wait_ge(gate_ready, 2 * c + k + 1)
                        dve.wait_ge(z_ready, 4 * c + 2 + k + 1)
                        nc.vector.tensor_tensor(gate[:, k, :], gate[:, k, :], bank[2 + k], ALU.mult).then_inc(prod_ready, 1)
                    dve.wait_ge(both_ready, c + 1)
                    dve.wait_ge(out_ready, c + 1)
                    nc.vector.tensor_tensor(core.sum[:, cols(c)], bank[4], both[:], ALU.add).then_inc(chunk_done, 1)


def post_norm(core, name):
    norm(core, name, core.sum, core.x, True, 0)
    recycle(core)


def build_program(nc, dram):
    with ExitStack() as ctx:
        core = Core(nc, ctx, dram)
        load_start(core)
        window_attention(core)
        post_norm(core, "n0a")
        ffn0(core)
        post_norm(core, "n0f")
        attn1(core)
        post_norm(core, "n1a")
        ffn1(core)
        post_norm(core, "n1f")
        attn2(core)
        post_norm(core, "n2a")
        ffn2(core)
        post_norm(core, "n2f")
        hawk(core)
        post_norm(core, "n3a")
        ffn3(core)
        post_norm(core, "n3f")
        store_end(core)


def arrays(i):
    f = np.float32
    d = {}
    c = np.ascontiguousarray
    eye = np.eye(128, dtype=f)
    idx = np.arange(128)
    d["c_ident"] = eye
    d["c_mean_w"] = np.full((128, 128), 1 / 128, f)
    d["c_center_w"] = (eye - f(1 / 128)).astype(f)
    d["c_eps"] = np.tile(np.array([1e-5, 1e-6, 0, 0], f), (128, 1))
    d["c_mask"] = np.where(idx[None, :] > idx[:, None], f(-1e30), f(0)).astype(f)
    d["c_headmask"] = ((idx[:, None] % 32) // 8 == np.arange(4)[None, :]).astype(f)
    d["c_wmask"] = np.where(np.arange(32)[None, :] > (idx[:, None] % 32), f(-1e30), f(0)).astype(f)
    d["l0_wqkv"] = i["L0_attn_w_qkv"]
    d["l0_wproj"] = i["L0_attn_w_proj"]
    d["l0_lnw"] = i["L0_attn_ln_w"].reshape(128, 1)
    d["c_sel"] = (np.arange(96)[:, None] % 32 == np.arange(32)[None, :]).astype(f)
    pair = (np.arange(96)[:, None, None] % 32 == 2 * np.arange(9)[:, None] + idx[None, :] // 64)
    d["c_selpair"] = pair.astype(f).reshape(96, 9 * 128)
    ij = np.arange(16)
    tri = np.stack([ij % 4 < ij // 4, ij % 4 > ij // 4]).astype(f)
    d["c_tri"] = np.broadcast_to(tri, (128, 2, 16))

    def pairs(w, shared):
        return np.concatenate([w.reshape(8, 128, 128).transpose(0, 2, 1), shared.T[None]])
    down = np.concatenate([i["L0_ffn_down_w"].transpose(0, 2, 1).reshape(8, 128, 128), i["L0_ffn_sh_down_w"].T[None]])
    d["l0_experts"] = np.concatenate([pairs(i["L0_ffn_gate_w"], i["L0_ffn_sh_gate_w"]),
                                      pairs(i["L0_ffn_up_w"], i["L0_ffn_sh_up_w"]), down], axis=2)
    d["l0_router"] = i["L0_ffn_router_weight"].T.reshape(128, 1, 16)
    d["l0_ebias"] = i["L0_ffn_e_bias"]

    def two_layers(w1, w2):
        e, dim, hid = w1.shape
        w2 = w2.reshape(e, hid // 128, 128, dim).transpose(0, 2, 1, 3).reshape(e, 128, hid)
        return np.concatenate([w1, w2], axis=2)
    d["l1_experts"] = two_layers(i["L1_ffn_c_fc"], i["L1_ffn_c_proj"])
    d["l1_router"] = i["L1_ffn_w_g"].reshape(128, 1, 8)
    d["l2_experts"] = np.concatenate([np.concatenate([
        two_layers(i["L2_ffn_re_w1"], i["L2_ffn_re_w2"]), two_layers(i["L2_ffn_sh_w1"][None], i["L2_ffn_sh_w2"][None])]),
        np.concatenate([i["L2_ffn_re_b1"], i["L2_ffn_sh_b1"][None]])[:, :, None]], axis=2)
    d["l2_b2"] = np.concatenate([i["L2_ffn_re_b2"], i["L2_ffn_sh_b2"][None]])
    d["l2_router"] = i["L2_ffn_router_w"].reshape(128, 1, 31)
    d["l2_rbias"] = i["L2_ffn_router_b"]
    d["l3_experts"] = np.concatenate([np.concatenate([
        two_layers(i["L3_ffn_We1"], i["L3_ffn_We2"]), two_layers(i["L3_ffn_Ws1"][None], i["L3_ffn_Ws2"][None])]),
        np.concatenate([i["L3_ffn_be1"], i["L3_ffn_bs1"][None]]).reshape(9, 2, 128).transpose(0, 2, 1)], axis=2)
    d["l3_b2"] = np.concatenate([i["L3_ffn_be2"], i["L3_ffn_bs2"][None]])
    d["l3_gw1"] = i["L3_ffn_gw1"]
    d["l3_gb1"] = i["L3_ffn_gb1"].reshape(2, 128).T
    d["l3_router"] = i["L3_ffn_gw2"].reshape(2, 128, 8).transpose(1, 0, 2)
    d["l3_rbias"] = i["L3_ffn_gb2"]

    wq, wk, wv = (i["L2_attn_w_a" + n].transpose(1, 0, 2) for n in "qkv")
    d["l2_heads"] = np.concatenate([wq, wk, wv, i["L2_attn_w_ao"]], axis=2)
    freqs = np.power(f(10000.0), -np.arange(64, dtype=f) / f(64)).astype(f)
    angles = (np.arange(512, dtype=f)[None, :] * freqs[:, None]).astype(f)
    cos, sin = np.cos(angles).astype(f), np.sin(angles).astype(f)
    cos, sin = np.concatenate([cos, cos]), np.concatenate([-sin, sin])
    d["c_rope2"] = np.stack([cos / f(128), sin / f(128), cos, sin], axis=1)
    signs = np.array([[a, b, e] for a in (-1, 1) for b in (-1, 1) for e in (-1, 1)], f)
    dirs = signs / np.linalg.norm(signs, axis=1, keepdims=True)
    spread = np.zeros((24, 256), f)
    for h in range(8):
        for at in range(32 * h, 32 * h + 24, 4):
            spread[3 * h:3 * h + 3, at:at + 3] = np.eye(3)
            spread[3 * h:3 * h + 3, at + 3] = dirs[h]
    d["c_spread"] = spread
    q_part, k_part = (np.repeat(p + [0, 0], 4)[idx % 32] for p in ([0, 0, 1, 1, 0, 2], [0, 1, 0, 1, 2, 0]))
    d["c_parts"] = np.stack([-1.0 * (q_part >= 1), -1.0 * (q_part == 2), -1.0 * (k_part >= 1), -1.0 * (k_part == 2),
                             (idx % 32 >= 24) & (idx % 32 < 27)], axis=1).astype(f)
    d["c_sumspread"] = ((idx[:, None] % 32 == 16) & (idx[:, None] // 32 == idx[None, :] // 32)).astype(f)
    d["l1_wq"], d["l1_wk"] = i["L1_attn_Wq"], i["L1_attn_Wk"]
    d["l1_scale"] = i["L1_attn_scale"].reshape(1)
    d["l1_wv"] = i["L1_attn_Wv"].T
    w_out = np.zeros((2, 4, 32, 128), f)
    w_out[:, :, :16] = i["L1_attn_Wo"].T.reshape(2, 4, 16, 128)
    d["l1_wout"] = w_out.reshape(2, 128, 128).transpose(1, 0, 2)

    def even_odd(w):
        w = w.reshape(w.shape[:-1] + (16, 32, 2)).swapaxes(-1, -2)
        return w.reshape(w.shape[:-3] + (8, 128))
    q_b, k_b = (even_odd(i[f"L2_ffn_{n}_b"])[:, :, None] for n in "qk")
    q_w, k_w = (even_odd(i[f"L2_ffn_{n}_w"]).transpose(1, 0, 2) for n in "qk")
    v_w = i["L2_ffn_v_w"].reshape(128, 8, 128).transpose(1, 0, 2)
    d["l2f_heads"] = np.concatenate([q_w, q_b, k_w, k_b, v_w, i["L2_ffn_o_w"].reshape(8, 128, 128)], axis=2)
    d["l2_vb"] = i["L2_ffn_v_b"]
    d["l2_ob"] = i["L2_ffn_o_b"].reshape(128, 1)
    d["l2_gammas"] = np.stack([i["L2_ffn_gamma1"], i["L2_ffn_gamma2"]], axis=1)
    d["l2_theta"] = np.tile(i["L2_ffn_theta"], 4).reshape(128, 1)
    d["c_pos"] = np.arange(512, dtype=f)
    d["c_ropesign"] = np.where(idx % 64 < 32, f(-1), f(1)).astype(f).reshape(128, 1)

    d["l3_gammas"] = np.stack([i["L3_attn_gamma1"], i["L3_attn_gamma2"]], axis=1)
    d["l3_win"] = i["L3_attn_W_in"].T
    d["l3_wgates"] = i["L3_attn_W_gates"].T.reshape(2, 128, 512).transpose(1, 0, 2)
    d["l3_wout"] = i["L3_attn_W_out"].T.reshape(2, 128, 128).transpose(1, 0, 2)
    d["l3_taps"] = i["L3_attn_conv_w"].reshape(2, 128, 4).transpose(1, 0, 2)
    d["l3_cols"] = np.concatenate([i["L3_attn_conv_b"].reshape(2, 128), i["L3_attn_b_gates"].reshape(4, 128),
                                   i["L3_attn_forget_base"].reshape(2, 128)]).T
    d["l3_wgrow"] = i["L3_attn_W_grow"].T
    d["l3_wshrink"] = i["L3_attn_W_shrink"].T.reshape(2, 128, 128).transpose(1, 0, 2)
    return {k: c(v) for k, v in d.items()}


def kernel(**inputs):
    import concourse.bacc as bacc
    from concourse.bass_utils import run_bass_kernel_spmd

    inputs = {name: np.asarray(a) for name, a in inputs.items()}
    laid = arrays(inputs)
    laid["x"] = np.ascontiguousarray(inputs["L0_attn_x"].reshape(N, P))
    nc = bacc.Bacc("TRN2", target_bir_lowering=False, num_devices=1)
    dram = {name: nc.dram_tensor(f"in_{name}", a.shape, mybir.dt.from_np(a.dtype), kind="ExternalInput").ap() for name, a in laid.items()}
    dram["out"] = nc.dram_tensor("out_tokens", (N, P), F32, kind="ExternalOutput").ap()
    build_program(nc, dram)
    result = run_bass_kernel_spmd(nc, [{f"in_{name}": a for name, a in laid.items()}], core_ids=[0])
    return result.results[0]["out_tokens"].reshape(B, T, P)
```
